# Optimizing a Trainium2 kernel written in Bass

```python
import numpy as np
import jax
import jax.numpy as jnp

def _softmax(x, axis=-1):
    return jax.nn.softmax(x, axis=axis)

def _gelu(x):
    return jax.nn.gelu(x, approximate=True)

def _silu(x):
    return jax.nn.silu(x)

def _sigmoid(x):
    return jax.nn.sigmoid(x)

def _layernorm(x, axis=-1, eps=1e-05):
    m = jnp.mean(x, axis=axis, keepdims=True)
    v = jnp.var(x, axis=axis, keepdims=True)
    return (x - m) / jnp.sqrt(v + eps)

def _scatter_add(tgt, idx, src, axis=0):
    return tgt.at[idx].add(src)

def _segment_sum(src, seg, n):
    return jax.ops.segment_sum(src, seg, n)
kernel_name = 'mk_gnn_resnorm_d4_gnn_r8_929046'

def setup_inputs(seed: int=0):
    np.random.seed(seed)
    _w = jnp.asarray

    def _rec_inputs():
        import jax
        import jax.numpy as jnp
        _gk = jax.random.key(seed)
        x = -0.0004942 + 1 * jax.random.normal(jax.random.fold_in(_gk, 1), (6250, 128), jnp.float32)
        src = jax.random.randint(jax.random.fold_in(_gk, 2), (100000,), 0, 6250, jnp.int32)
        dst = jnp.minimum((6250 * jax.random.uniform(jax.random.fold_in(_gk, 3), (100000,)) ** 2.0).astype(jnp.int32), 49999)
        _o = jnp.argsort(dst, stable=True)
        src = src[_o]
        dst = dst[_o]
        edge_attr_16 = 0.000196303 + 1.00016 * jax.random.normal(jax.random.fold_in(_gk, 12), (100000, 16), jnp.float32)
        edge_attr_64 = 0.000149146 + 1.0001 * jax.random.normal(jax.random.fold_in(_gk, 13), (100000, 64), jnp.float32)
        edge_type_16 = jax.random.randint(jax.random.fold_in(_gk, 15), (100000,), 0, 16, jnp.int32)
        edge_weight = jax.random.uniform(jax.random.fold_in(_gk, 16), (100000,), jnp.float32, 0.0, 0.999998)
        node_vec = jax.random.uniform(jax.random.fold_in(_gk, 17), (6250,), jnp.float32, 0.0, 999.994)
        return (x, src, dst, edge_attr_16, edge_attr_64, edge_type_16, edge_weight, node_vec)
    x, src, dst, edge_attr_16, edge_attr_64, edge_type_16, edge_weight, node_vec = _rec_inputs()

    def _L0_gnn_setup():
        import jax, jax.numpy as jnp
        import numpy as np
        N, E, D, R, H, L = (3750, 60000, 128, 16, 4, 3)
        DH = D // H
        key = jax.random.key(seed)
        ks = jax.random.split(key, 16)
        s = 1.0 / np.sqrt(D)
        return {'feat': jax.random.normal(ks[0], (N, D), jnp.float32), 'src': jax.random.randint(ks[1], (E,), 0, N, jnp.int32), 'dst': jax.random.randint(ks[2], (E,), 0, N, jnp.int32), 'etype': jax.random.randint(ks[3], (E,), 0, R, jnp.int32), 'temporal_weight': jax.random.uniform(ks[4], (E,), jnp.float32), 'W_rel': jax.random.normal(ks[5], (L, R, D, D), jnp.float32) * s, 'b_rel': jnp.zeros((L, D), jnp.float32), 'W_loop': jax.random.normal(ks[6], (L, D, D), jnp.float32) * s, 'W_gat': jax.random.normal(ks[7], (L, D, D), jnp.float32) * s, 'attn_l': jax.random.normal(ks[8], (L, H, DH), jnp.float32) * s, 'attn_r': jax.random.normal(ks[9], (L, H, DH), jnp.float32) * s, 'b_gat': jnp.zeros((L, D), jnp.float32), 'W_fuse': jax.random.normal(ks[10], (2 * D, D), jnp.float32) * (1.0 / np.sqrt(2 * D)), 'b_fuse': jnp.zeros((D,), jnp.float32), 'W_gate': jax.random.normal(ks[11], (D + 1, D), jnp.float32) * s, 'b_gate': jnp.zeros((D,), jnp.float32)}
    _L0_gnn_all = _L0_gnn_setup()
    _L0_gnn_in = {k: v for k, v in _L0_gnn_all.items() if k in ('W_rel', 'b_rel', 'W_loop', 'W_gat', 'attn_l', 'attn_r', 'b_gat', 'W_fuse', 'b_fuse', 'W_gate', 'b_gate')}
    del _L0_gnn_all

    def _L1_gnn_setup():
        import jax, jax.numpy as jnp
        import numpy as np
        LN_EPS = 1e-05
        N_NODES = 6250
        IN_DIM = 128
        OUT_DIM = 128
        N_EDGES = 100000

        def _ln(x, g, b):
            m = jnp.mean(x, axis=-1, keepdims=True)
            v = jnp.mean((x - m) ** 2, axis=-1, keepdims=True)
            return (x - m) * jax.lax.rsqrt(v + LN_EPS) * g + b
        key = jax.random.key(seed)
        ks = jax.random.split(key, 16)

        def lin(k, fan_in, fan_out):
            return jax.random.normal(k, (fan_in, fan_out), dtype=jnp.float32) / np.sqrt(fan_in)
        x = jax.random.normal(ks[0], (N_NODES, IN_DIM), dtype=jnp.float32)
        edge_index = jax.random.randint(ks[1], (2, N_EDGES), 0, N_NODES, dtype=jnp.int64)
        return {'x': x, 'edge_index': edge_index, 'W1': lin(ks[2], IN_DIM, OUT_DIM), 'b1': jnp.zeros((OUT_DIM,), jnp.float32), 'g1': jnp.ones((OUT_DIM,), jnp.float32), 'bt1': jnp.zeros((OUT_DIM,), jnp.float32), 'We1': lin(ks[3], 2 * OUT_DIM, OUT_DIM), 'be1': jnp.zeros((OUT_DIM,), jnp.float32), 'We2': lin(ks[4], OUT_DIM, 1), 'be2': jnp.zeros((1,), jnp.float32), 'Wn1': lin(ks[5], OUT_DIM, OUT_DIM), 'bn1': jnp.zeros((OUT_DIM,), jnp.float32), 'Wn2': lin(ks[6], OUT_DIM, 1), 'bn2': jnp.zeros((1,), jnp.float32), 'Wg': lin(ks[7], 2 * OUT_DIM, OUT_DIM), 'bg': jnp.zeros((OUT_DIM,), jnp.float32), 'g2': jnp.ones((OUT_DIM,), jnp.float32), 'bt2': jnp.zeros((OUT_DIM,), jnp.float32)}
    _L1_gnn_all = _L1_gnn_setup()
    _L1_gnn_in = {k: v for k, v in _L1_gnn_all.items() if k in ('W1', 'b1', 'g1', 'bt1', 'We1', 'be1', 'We2', 'be2', 'Wn1', 'bn1', 'Wn2', 'bn2', 'Wg', 'bg', 'g2', 'bt2')}
    del _L1_gnn_all

    def _L2_gnn_setup():
        import jax, jax.numpy as jnp
        import numpy as np
        H, C = (4, 32)
        NEG_SLOPE = 0.2
        LN_EPS = 1e-05
        N_NODES = 6250
        N_EDGES = 200000
        IN_CH = 128
        EDGE_DIM = 16
        key = jax.random.key(seed)
        ks = jax.random.split(key, 10)
        sc = 0.1
        return {'x': jax.random.normal(ks[0], (N_NODES, IN_CH), jnp.float32), 'edge_index': jax.random.randint(ks[1], (2, N_EDGES), 0, N_NODES, jnp.int32), 'edge_attr': jax.random.normal(ks[2], (N_EDGES, EDGE_DIM), jnp.float32), 'W_lin': jax.random.normal(ks[3], (H * C, IN_CH), jnp.float32) * sc, 'W_edge': jax.random.normal(ks[4], (H * C, EDGE_DIM), jnp.float32) * sc, 'att_src': jax.random.normal(ks[5], (1, H, C), jnp.float32) * sc, 'att_dst': jax.random.normal(ks[6], (1, H, C), jnp.float32) * sc, 'att_edge': jax.random.normal(ks[7], (1, H, C), jnp.float32) * sc, 'bias': jnp.zeros((H * C,), jnp.float32), 'ln_gamma': jnp.ones((H * C,), jnp.float32), 'ln_beta': jnp.zeros((H * C,), jnp.float32)}
    _L2_gnn_all = _L2_gnn_setup()
    _L2_gnn_in = {k: v for k, v in _L2_gnn_all.items() if k in ('W_lin', 'W_edge', 'att_src', 'att_dst', 'att_edge', 'bias', 'ln_gamma', 'ln_beta')}
    del _L2_gnn_all

    def _L3_gnn_setup():
        import jax, jax.numpy as jnp
        import numpy as np
        N = 12500
        E = 80000
        IN_CH = 128
        OUT_CH = 128
        MSG_DIM = 64
        TIME_DIM = 64
        EDGE_DIM = MSG_DIM + TIME_DIM
        HEADS = 4

        def _linear_params(key, fan_in, fan_out, bias=True, scale=0.02):
            k1, k2 = jax.random.split(key)
            W = jax.random.normal(k1, (fan_in, fan_out), jnp.float32) * scale
            if bias:
                b = jax.random.normal(k2, (fan_out,), jnp.float32) * scale
                return (W, b)
            return W

        def transformer_conv(x, src, dst, edge_attr, Wq, bq, Wk, bk, Wv, bv, We, Wskip, bskip):
            n = x.shape[0]
            HC = Wq.shape[1]
            C = HC // HEADS
            q = (x @ Wq + bq).reshape(n, HEADS, C)
            k = (x @ Wk + bk).reshape(n, HEADS, C)
            v = (x @ Wv + bv).reshape(n, HEADS, C)
            e = (edge_attr @ We).reshape(-1, HEADS, C)
            k_j = k[src] + e
            v_j = v[src] + e
            alpha = jnp.einsum('ehc,ehc->eh', q[dst], k_j) / jnp.sqrt(jnp.float32(C))
            amax = jax.ops.segment_max(alpha, dst, num_segments=n)
            expa = jnp.exp(alpha - amax[dst])
            denom = jax.ops.segment_sum(expa, dst, num_segments=n)
            attn = expa / (denom[dst] + 1e-16)
            out = jax.ops.segment_sum(attn[:, :, None] * v_j, dst, num_segments=n)
            out = out.reshape(n, HC)
            return out + x @ Wskip + bskip
        key = jax.random.key(seed)
        ks = jax.random.split(key, 16)
        inp = {'x': jax.random.normal(ks[0], (N, IN_CH), jnp.float32), 'last_update': jax.random.uniform(ks[1], (N,), jnp.float32) * 1000.0, 't': jax.random.uniform(ks[2], (E,), jnp.float32) * 1000.0, 'msg': jax.random.normal(ks[3], (E, MSG_DIM), jnp.float32), 'edge_index': jax.random.randint(ks[4], (2, E), 0, N, jnp.int64)}
        inp['Wt'], inp['bt'] = _linear_params(ks[5], 1, TIME_DIM)
        HC1 = HEADS * (IN_CH // 4)
        inp['Wq1'], inp['bq1'] = _linear_params(ks[6], IN_CH, HC1)
        inp['Wk1'], inp['bk1'] = _linear_params(ks[7], IN_CH, HC1)
        inp['Wv1'], inp['bv1'] = _linear_params(ks[8], IN_CH, HC1)
        inp['We1'] = _linear_params(ks[9], EDGE_DIM, HC1, bias=False)
        inp['Wskip1'], inp['bskip1'] = _linear_params(ks[10], IN_CH, HC1)
        HC2 = HEADS * (OUT_CH // 4)
        inp['Wq2'], inp['bq2'] = _linear_params(ks[11], IN_CH, HC2)
        inp['Wk2'], inp['bk2'] = _linear_params(ks[12], IN_CH, HC2)
        inp['Wv2'], inp['bv2'] = _linear_params(ks[13], IN_CH, HC2)
        inp['We2'] = _linear_params(ks[14], EDGE_DIM, HC2, bias=False)
        inp['Wskip2'], inp['bskip2'] = _linear_params(ks[15], IN_CH, HC2)
        return inp
    _L3_gnn_all = _L3_gnn_setup()
    _L3_gnn_in = {k: v for k, v in _L3_gnn_all.items() if k in ('Wt', 'bt', 'Wq1', 'bq1', 'Wk1', 'bk1', 'Wv1', 'bv1', 'We1', 'Wskip1', 'bskip1', 'Wq2', 'bq2', 'Wk2', 'bk2', 'Wv2', 'bv2', 'We2', 'Wskip2', 'bskip2')}
    del _L3_gnn_all
    return {'x': x, 'src': src, 'dst': dst, 'edge_attr_16': edge_attr_16, 'edge_attr_64': edge_attr_64, 'edge_type_16': edge_type_16, 'edge_weight': edge_weight, 'node_vec': node_vec, 'L0_gnn_W_rel': _L0_gnn_in['W_rel'], 'L0_gnn_b_rel': _L0_gnn_in['b_rel'], 'L0_gnn_W_loop': _L0_gnn_in['W_loop'], 'L0_gnn_W_gat': _L0_gnn_in['W_gat'], 'L0_gnn_attn_l': _L0_gnn_in['attn_l'], 'L0_gnn_attn_r': _L0_gnn_in['attn_r'], 'L0_gnn_b_gat': _L0_gnn_in['b_gat'], 'L0_gnn_W_fuse': _L0_gnn_in['W_fuse'], 'L0_gnn_b_fuse': _L0_gnn_in['b_fuse'], 'L0_gnn_W_gate': _L0_gnn_in['W_gate'], 'L0_gnn_b_gate': _L0_gnn_in['b_gate'], 'L1_gnn_W1': _L1_gnn_in['W1'], 'L1_gnn_b1': _L1_gnn_in['b1'], 'L1_gnn_g1': _L1_gnn_in['g1'], 'L1_gnn_bt1': _L1_gnn_in['bt1'], 'L1_gnn_We1': _L1_gnn_in['We1'], 'L1_gnn_be1': _L1_gnn_in['be1'], 'L1_gnn_We2': _L1_gnn_in['We2'], 'L1_gnn_be2': _L1_gnn_in['be2'], 'L1_gnn_Wn1': _L1_gnn_in['Wn1'], 'L1_gnn_bn1': _L1_gnn_in['bn1'], 'L1_gnn_Wn2': _L1_gnn_in['Wn2'], 'L1_gnn_bn2': _L1_gnn_in['bn2'], 'L1_gnn_Wg': _L1_gnn_in['Wg'], 'L1_gnn_bg': _L1_gnn_in['bg'], 'L1_gnn_g2': _L1_gnn_in['g2'], 'L1_gnn_bt2': _L1_gnn_in['bt2'], 'L2_gnn_W_lin': _L2_gnn_in['W_lin'], 'L2_gnn_W_edge': _L2_gnn_in['W_edge'], 'L2_gnn_att_src': _L2_gnn_in['att_src'], 'L2_gnn_att_dst': _L2_gnn_in['att_dst'], 'L2_gnn_att_edge': _L2_gnn_in['att_edge'], 'L2_gnn_bias': _L2_gnn_in['bias'], 'L2_gnn_ln_gamma': _L2_gnn_in['ln_gamma'], 'L2_gnn_ln_beta': _L2_gnn_in['ln_beta'], 'L3_gnn_Wt': _L3_gnn_in['Wt'], 'L3_gnn_bt': _L3_gnn_in['bt'], 'L3_gnn_Wq1': _L3_gnn_in['Wq1'], 'L3_gnn_bq1': _L3_gnn_in['bq1'], 'L3_gnn_Wk1': _L3_gnn_in['Wk1'], 'L3_gnn_bk1': _L3_gnn_in['bk1'], 'L3_gnn_Wv1': _L3_gnn_in['Wv1'], 'L3_gnn_bv1': _L3_gnn_in['bv1'], 'L3_gnn_We1': _L3_gnn_in['We1'], 'L3_gnn_Wskip1': _L3_gnn_in['Wskip1'], 'L3_gnn_bskip1': _L3_gnn_in['bskip1'], 'L3_gnn_Wq2': _L3_gnn_in['Wq2'], 'L3_gnn_bq2': _L3_gnn_in['bq2'], 'L3_gnn_Wk2': _L3_gnn_in['Wk2'], 'L3_gnn_bk2': _L3_gnn_in['bk2'], 'L3_gnn_Wv2': _L3_gnn_in['Wv2'], 'L3_gnn_bv2': _L3_gnn_in['bv2'], 'L3_gnn_We2': _L3_gnn_in['We2'], 'L3_gnn_Wskip2': _L3_gnn_in['Wskip2'], 'L3_gnn_bskip2': _L3_gnn_in['bskip2']}

def reference(x, src, dst, edge_attr_16, edge_attr_64, edge_type_16, edge_weight, node_vec, L0_gnn_W_rel, L0_gnn_b_rel, L0_gnn_W_loop, L0_gnn_W_gat, L0_gnn_attn_l, L0_gnn_attn_r, L0_gnn_b_gat, L0_gnn_W_fuse, L0_gnn_b_fuse, L0_gnn_W_gate, L0_gnn_b_gate, L1_gnn_W1, L1_gnn_b1, L1_gnn_g1, L1_gnn_bt1, L1_gnn_We1, L1_gnn_be1, L1_gnn_We2, L1_gnn_be2, L1_gnn_Wn1, L1_gnn_bn1, L1_gnn_Wn2, L1_gnn_bn2, L1_gnn_Wg, L1_gnn_bg, L1_gnn_g2, L1_gnn_bt2, L2_gnn_W_lin, L2_gnn_W_edge, L2_gnn_att_src, L2_gnn_att_dst, L2_gnn_att_edge, L2_gnn_bias, L2_gnn_ln_gamma, L2_gnn_ln_beta, L3_gnn_Wt, L3_gnn_bt, L3_gnn_Wq1, L3_gnn_bq1, L3_gnn_Wk1, L3_gnn_bk1, L3_gnn_Wv1, L3_gnn_bv1, L3_gnn_We1, L3_gnn_Wskip1, L3_gnn_bskip1, L3_gnn_Wq2, L3_gnn_bq2, L3_gnn_Wk2, L3_gnn_bk2, L3_gnn_Wv2, L3_gnn_bv2, L3_gnn_We2, L3_gnn_Wskip2, L3_gnn_bskip2):
    import jax
    import jax.numpy as jnp

    def _L0_gnn_ref(feat, src, dst, etype, temporal_weight, W_rel, b_rel, W_loop, W_gat, attn_l, attn_r, b_gat, W_fuse, b_fuse, W_gate, b_gate):
        import jax, jax.numpy as jnp
        import numpy as np
        N, E, D, R, H, L = (3750, 60000, 128, 16, 4, 3)
        DH = D // H
        n = feat.shape[0]
        h = feat
        tw_mean = jnp.mean(temporal_weight)
        for l in range(L):
            ht = jnp.einsum('nd,rdo->nro', h, W_rel[l])
            msg = ht[src, etype]
            h_rel = jax.ops.segment_sum(msg, dst, num_segments=n)
            h_rel = h_rel + h @ W_loop[l] + b_rel[l]
            z = (h @ W_gat[l]).reshape(n, H, DH)
            el = jnp.sum(z * attn_l[l], axis=-1)
            er = jnp.sum(z * attn_r[l], axis=-1)
            e = jax.nn.leaky_relu(el[src] + er[dst], 0.2)
            m = jax.ops.segment_max(e, dst, num_segments=n)
            ex = jnp.exp(e - m[dst])
            denom = jax.ops.segment_sum(ex, dst, num_segments=n)
            alpha = ex / denom[dst]
            h_gat = jax.ops.segment_sum(alpha[:, :, None] * z[src], dst, num_segments=n)
            h_gat = h_gat.reshape(n, D) + b_gat[l]
            hc = jnp.concatenate([h_rel, h_gat], axis=1) @ W_fuse + b_fuse
            if l == 0:
                avg = jnp.full((n, 1), tw_mean, dtype=hc.dtype)
                gate = jax.nn.sigmoid(jnp.concatenate([hc, avg], axis=1) @ W_gate + b_gate)
                hc = hc * gate
            h = jax.nn.relu(hc)
        return h

    def _L1_gnn_ref(x, edge_index, W1, b1, g1, bt1, We1, be1, We2, be2, Wn1, bn1, Wn2, bn2, Wg, bg, g2, bt2):
        import jax, jax.numpy as jnp
        import numpy as np
        LN_EPS = 1e-05
        N_NODES = 6250
        IN_DIM = 128
        OUT_DIM = 128
        N_EDGES = 100000

        def _ln(x, g, b):
            m = jnp.mean(x, axis=-1, keepdims=True)
            v = jnp.mean((x - m) ** 2, axis=-1, keepdims=True)
            return (x - m) * jax.lax.rsqrt(v + LN_EPS) * g + b
        n = x.shape[0]
        h = jax.nn.relu(_ln(x @ W1 + b1, g1, bt1))
        row, col = (edge_index[0], edge_index[1])
        h_src = h[row]
        ef = jnp.concatenate([h_src, h[col]], axis=1)
        edge_weights = jax.nn.sigmoid(jax.nn.relu(ef @ We1 + be1) @ We2 + be2)[:, 0]
        node_weights = jax.nn.sigmoid(jax.nn.relu(h @ Wn1 + bn1) @ Wn2 + bn2)[:, 0]
        _ = node_weights
        aggr = jax.ops.segment_sum(edge_weights[:, None] * h_src, col, num_segments=n)
        gate = jax.nn.sigmoid(jnp.concatenate([h, aggr], axis=-1) @ Wg + bg)
        h_new = gate * aggr + (1.0 - gate) * h
        return _ln(h_new, g2, bt2)

    def _L2_gnn_ref(x, edge_index, edge_attr, W_lin, W_edge, att_src, att_dst, att_edge, bias, ln_gamma, ln_beta):
        import jax, jax.numpy as jnp
        import numpy as np
        H, C = (4, 32)
        NEG_SLOPE = 0.2
        LN_EPS = 1e-05
        N_NODES = 6250
        N_EDGES = 200000
        IN_CH = 128
        EDGE_DIM = 16
        N = x.shape[0]
        src, dst = (edge_index[0], edge_index[1])
        xl = (x @ W_lin.T).reshape(N, H, C)
        ef = (edge_attr @ W_edge.T).reshape(-1, H, C)
        x_j = xl[src]
        x_i = xl[dst]
        alpha = (x_i * att_src).sum(-1) + (x_j * att_dst).sum(-1) + (ef * att_edge).sum(-1)
        alpha = jax.nn.leaky_relu(alpha, NEG_SLOPE)
        amax = jax.ops.segment_max(alpha, dst, num_segments=N)
        e = jnp.exp(alpha - amax[dst])
        denom = jax.ops.segment_sum(e, dst, num_segments=N)
        alpha = e / (denom[dst] + 1e-16)
        msg = x_j * alpha[..., None]
        out = jax.ops.segment_sum(msg, dst, num_segments=N)
        out = out.reshape(N, H * C) + bias
        out = out + x
        mu = out.mean(-1, keepdims=True)
        var = ((out - mu) ** 2).mean(-1, keepdims=True)
        out = (out - mu) / jnp.sqrt(var + LN_EPS) * ln_gamma + ln_beta
        return jax.nn.elu(out)

    def _L3_gnn_ref(x, last_update, t, msg, edge_index, Wt, bt, Wq1, bq1, Wk1, bk1, Wv1, bv1, We1, Wskip1, bskip1, Wq2, bq2, Wk2, bk2, Wv2, bv2, We2, Wskip2, bskip2):
        import jax, jax.numpy as jnp
        import numpy as np
        N = 12500
        E = 80000
        IN_CH = 128
        OUT_CH = 128
        MSG_DIM = 64
        TIME_DIM = 64
        EDGE_DIM = MSG_DIM + TIME_DIM
        HEADS = 4

        def _linear_params(key, fan_in, fan_out, bias=True, scale=0.02):
            k1, k2 = jax.random.split(key)
            W = jax.random.normal(k1, (fan_in, fan_out), jnp.float32) * scale
            if bias:
                b = jax.random.normal(k2, (fan_out,), jnp.float32) * scale
                return (W, b)
            return W

        def transformer_conv(x, src, dst, edge_attr, Wq, bq, Wk, bk, Wv, bv, We, Wskip, bskip):
            n = x.shape[0]
            HC = Wq.shape[1]
            C = HC // HEADS
            q = (x @ Wq + bq).reshape(n, HEADS, C)
            k = (x @ Wk + bk).reshape(n, HEADS, C)
            v = (x @ Wv + bv).reshape(n, HEADS, C)
            e = (edge_attr @ We).reshape(-1, HEADS, C)
            k_j = k[src] + e
            v_j = v[src] + e
            alpha = jnp.einsum('ehc,ehc->eh', q[dst], k_j) / jnp.sqrt(jnp.float32(C))
            amax = jax.ops.segment_max(alpha, dst, num_segments=n)
            expa = jnp.exp(alpha - amax[dst])
            denom = jax.ops.segment_sum(expa, dst, num_segments=n)
            attn = expa / (denom[dst] + 1e-16)
            out = jax.ops.segment_sum(attn[:, :, None] * v_j, dst, num_segments=n)
            out = out.reshape(n, HC)
            return out + x @ Wskip + bskip
        src, dst = (edge_index[0], edge_index[1])
        rel_t = last_update[src] - t
        rel_t_enc = jnp.cos(rel_t[:, None] * Wt[0][None, :] + bt)
        edge_attr = jnp.concatenate([rel_t_enc, msg], axis=-1)
        h = transformer_conv(x, src, dst, edge_attr, Wq1, bq1, Wk1, bk1, Wv1, bv1, We1, Wskip1, bskip1)
        return transformer_conv(h, src, dst, edge_attr, Wq2, bq2, Wk2, bk2, Wv2, bv2, We2, Wskip2, bskip2)
    edge_index = jnp.stack([src, dst])
    x = _layernorm(x + _L0_gnn_ref(x, src, dst, edge_type_16, edge_weight, L0_gnn_W_rel, L0_gnn_b_rel, L0_gnn_W_loop, L0_gnn_W_gat, L0_gnn_attn_l, L0_gnn_attn_r, L0_gnn_b_gat, L0_gnn_W_fuse, L0_gnn_b_fuse, L0_gnn_W_gate, L0_gnn_b_gate), axis=-1)
    x = _layernorm(x + _L1_gnn_ref(x, edge_index, L1_gnn_W1, L1_gnn_b1, L1_gnn_g1, L1_gnn_bt1, L1_gnn_We1, L1_gnn_be1, L1_gnn_We2, L1_gnn_be2, L1_gnn_Wn1, L1_gnn_bn1, L1_gnn_Wn2, L1_gnn_bn2, L1_gnn_Wg, L1_gnn_bg, L1_gnn_g2, L1_gnn_bt2), axis=-1)
    x = _layernorm(x + _L2_gnn_ref(x, edge_index, edge_attr_16, L2_gnn_W_lin, L2_gnn_W_edge, L2_gnn_att_src, L2_gnn_att_dst, L2_gnn_att_edge, L2_gnn_bias, L2_gnn_ln_gamma, L2_gnn_ln_beta), axis=-1)
    x = _layernorm(x + _L3_gnn_ref(x, node_vec, edge_weight, edge_attr_64, edge_index, L3_gnn_Wt, L3_gnn_bt, L3_gnn_Wq1, L3_gnn_bq1, L3_gnn_Wk1, L3_gnn_bk1, L3_gnn_Wv1, L3_gnn_bv1, L3_gnn_We1, L3_gnn_Wskip1, L3_gnn_bskip1, L3_gnn_Wq2, L3_gnn_bq2, L3_gnn_Wk2, L3_gnn_bk2, L3_gnn_Wv2, L3_gnn_bv2, L3_gnn_We2, L3_gnn_Wskip2, L3_gnn_bskip2), axis=-1)
    return x

_drawn_inputs = setup_inputs


def setup_inputs(seed=0):
    import zlib

    import numpy as np

    out = dict(_drawn_inputs(seed))
    spreads = {'L0_gnn_b_rel': (0.0, 0.1),
     'L0_gnn_b_gat': (0.0, 0.1),
     'L0_gnn_b_fuse': (0.0, 0.1),
     'L0_gnn_b_gate': (0.0, 0.393),
     'L1_gnn_b1': (0.0, 0.1),
     'L1_gnn_g1': (1.0, 0.2),
     'L1_gnn_bt1': (0.0, 0.1),
     'L1_gnn_be1': (0.0, 0.397),
     'L1_gnn_bn1': (0.0, 0.1),
     'L1_gnn_bg': (0.0, 0.336),
     'L1_gnn_g2': (1.0, 0.2),
     'L1_gnn_bt2': (0.0, 0.1),
     'L2_gnn_bias': (0.0, 0.1),
     'L2_gnn_ln_gamma': (1.0, 0.2),
     'L2_gnn_ln_beta': (0.0, 0.1)}
    factors = {'edge_attr_16': 2.789,
     'edge_weight': 64.0,
     'L2_gnn_W_edge': 3.065,
     'L2_gnn_att_src': 3.053,
     'L3_gnn_bt': 27.17,
     'L3_gnn_Wq1': 8.0,
     'L3_gnn_bq1': 41.463,
     'L3_gnn_Wk1': 8.0,
     'L3_gnn_bk1': 64.0,
     'L3_gnn_bv1': 8.0,
     'L3_gnn_We1': 2.772,
     'L3_gnn_bskip1': 8.0,
     'L3_gnn_Wq2': 8.0,
     'L3_gnn_bq2': 47.175,
     'L3_gnn_Wk2': 8.0,
     'L3_gnn_bk2': 64.0,
     'L3_gnn_bv2': 2.743,
     'L3_gnn_bskip2': 3.064}
    for name, (base, spread) in spreads.items():
        noise = np.random.default_rng([zlib.crc32(name.encode()), seed]).standard_normal(out[name].shape)
        drawn = base * np.exp(spread * noise) if base else spread * noise
        out[name] = jnp.asarray(drawn.astype(out[name].dtype))
    for name, factor in factors.items():
        out[name] = (out[name] * factor).astype(out[name].dtype)
    return out
```

```python
from contextlib import ExitStack

import concourse.bass as bass
from concourse import mybir

F32 = mybir.dt.float32
BF16 = mybir.dt.bfloat16
I32 = mybir.dt.int32
U32 = mybir.dt.uint32
ALU = mybir.AluOpType
ACT = mybir.ActivationFunctionType
AX = mybir.AxisListType.X

P = 128
NODES, EDGES, D = 6250, 100000, 128
RELS, HEADS, DH = 16, 4, 32
NBINS = -(-NODES // P)
LAST = NODES - (NBINS - 1) * P
NB = 7
NSTEPS = NBINS // NB
EP = 125
EC = EDGES // EP
GT = 2
GE = GT * P
GPS = 4
ST = GPS * GT
NGROUPS = (EDGES + NBINS * (GE - 1)) // GE
NSUPER = -(-NGROUPS // GPS)
NGROUPS = NSUPER * GPS
NTILES = NGROUPS * GT
SLOTS = NTILES * P
RING = 4
REC = 64 + 16 + 4
PLACE = 82 - 1
HZ = DH + 1
ZW = HEADS * HZ
BIG = 1e30
LN_EPS = 1e-5
TWO_PI = 6.283185307179586


class Chain:

    def __init__(self, engine, sem, start=0):
        self.engine, self.sem, self.start, self.n = engine, sem, start, 0

    def link(self, ins):
        ins.then_inc(self.sem, 1)
        self.n += 1
        self.engine.wait_ge(self.sem, self.start + self.n)

    def end(self, per):
        assert self.n == per, self.n


def hold(engine, sem, value):
    if not isinstance(value, int) or value > 0:
        engine.wait_ge(sem, value)


def park(engine):
    engine.nop(nofuse=True)



def steps(engine, count, step):
    step(0)
    with engine.Fori(1, count) as t:
        step(t)


def bins_of(t):
    return bass.ds(t * NB, NB)


def flat(tile):
    return tile[:, :, :].rearrange("p b c -> p (b c)")


def heads_of(tile):
    return tile.rearrange("p b (h c) -> p b h c", h=HEADS)


def over_bins(vec):
    return vec[:, :].unsqueeze(1).to_broadcast([P, NB, D])


def load_row(sp, tile, vec, loaded):
    sp.dma_start(tile[:, :], vec.partition_broadcast(P)).then_inc(loaded, 16)


class Pass:

    def __init__(self, g, name):
        self.g, self.stack, self.name = g, ExitStack(), name
        self.used = []

    def __enter__(self):
        return self

    def __exit__(self, failed, *_):
        if failed:
            return
        with self.g.nc.Block() as block:
            @block.gpsimd
            def _(pool):
                for used in self.used:
                    pool.sem_clear(used)
        self.stack.close()

    def buffer(self, name, shape=(P, NB, D), dt=F32):
        return self.stack.enter_context(self.g.nc.sbuf_tensor(f"{self.name}_{name}", list(shape), dt))

    def gathers_before(self, slots=RING):
        before = list(self.g.seen)
        for u in range(NSUPER):
            self.g.seen[u % slots] += 16 * ST
        return before

    def semaphore(self, name):
        self.used.append(self.stack.enter_context(self.g.nc.semaphore(f"{self.name}_{name}")))
        return self.used[-1]


def flip(pe, g, src, tile_ready, ready, flipped):
    pe.wait_ge(tile_ready, ready)
    for j in range(NB):
        ins = pe.transpose(g.bank[0][:, j * D:(j + 1) * D], src[:, j, :], g.ident[:, :])
    ins.then_inc(flipped, 1)


def keep_flipped(act, g, dst, flipped, value, kept):
    act.wait_ge(flipped, value)
    act.activation(flat(dst), g.bank[0][:, 0:NB * D], ACT.Copy).then_inc(kept, 1)


def product(pe, g, bank, pairs, made):
    for j in range(NB):
        for n, (tT, w) in enumerate(pairs):
            ins = pe.matmul(g.bank[bank][:, j * D:(j + 1) * D], tT[:, j, :], w,
                            start=n == 0, stop=n == len(pairs) - 1)
    ins.then_inc(made, 1)


def bank_tiles(g, n):
    return g.bank[n][:, 0:NB * D].rearrange("p (b c) -> p b c", c=D)


def normalise(v, c, tile, square, stat, variance_ready, deviation_ready, value):
    def wide(col):
        return stat[:, col, :].unsqueeze(2).to_broadcast([P, NB, D])
    c.link(v.tensor_reduce(stat[:, 0, :], tile[:, :, :], AX, ALU.add))
    c.link(v.tensor_scalar(stat[:, 0, :], stat[:, 0, :], 1.0 / D, None, ALU.mult))
    c.link(v.tensor_tensor(tile[:, :, :], tile[:, :, :], wide(0), ALU.subtract))
    c.link(v.tensor_tensor(square[:, :, :], tile[:, :, :], tile[:, :, :], ALU.mult))
    c.link(v.tensor_reduce(stat[:, 1, :], square[:, :, :], AX, ALU.add))
    v.tensor_scalar(stat[:, 1, :], stat[:, 1, :], 1.0 / D, LN_EPS, ALU.mult, ALU.add).then_inc(variance_ready, 1)
    v.wait_ge(deviation_ready, value)
    c.link(v.reciprocal(stat[:, 3, :], stat[:, 2, :]))
    c.link(v.tensor_tensor(tile[:, :, :], tile[:, :, :], wide(3), ALU.mult))


NORM_LINKS = 7


def deviation(act, stat, variance_ready, value, deviation_ready):
    act.wait_ge(variance_ready, value)
    act.activation(stat[:, 2, :], stat[:, 1, :], ACT.Sqrt).then_inc(deviation_ready, 1)


def attended(v, c, g, t, tile, denom):
    z = g.acc[:, bins_of(t), D:D + ZW].rearrange("p b (h z) -> p b h z", h=HEADS)
    c.link(v.tensor_scalar(denom[:, :, :], z[:, :, :, DH], 1e-16, None, ALU.add))
    c.link(v.reciprocal(denom[:, :, :], denom[:, :, :]))
    c.link(v.tensor_tensor(heads_of(tile[:, :, :]), z[:, :, :, 0:DH],
                           denom[:, :, :].unsqueeze(3).to_broadcast([P, NB, HEADS, DH]), ALU.mult))


ATTENDED_LINKS = 3


def node_scores(v, c, zrow, prod, weights, out):
    z = zrow[:, :, :].rearrange("p b (h z) -> p b h z", h=HEADS)[:, :, :, 0:DH]
    w = weights[:, :].rearrange("p (h c) -> p h c", h=HEADS).unsqueeze(1).to_broadcast([P, NB, HEADS, DH])
    c.link(v.tensor_tensor(heads_of(prod[:, :, :]), z, w, ALU.mult))
    return v.tensor_reduce(out, heads_of(prod[:, :, :]), AX, ALU.add)


def clear_sums(v, c, g):
    v.memset(g.acc[:, :, :].rearrange("p b c -> p (b c)"), 0.0)
    c.link(v.memset(g.top[:, :, :].rearrange("p b h -> p (b h)"), -BIG))


def attention_sources(g, name, inp, w_z, flip_w, w_src, w_dst, layer=None):
    a, nc = g.a, g.nc
    rel = layer is not None
    with Pass(g, name) as p:
        wz_in, wz = p.buffer("wz_in", (P, D)), p.buffer("wz", (P, D))
        asrc, adst = p.buffer("asrc", (P, D)), p.buffer("adst", (P, D))
        cur, curT, prod = p.buffer("cur"), p.buffer("curT"), p.buffer("prod")
        zrow, er = p.buffer("zrow", (P, NB, ZW)), p.buffer("er", (P, NB, HEADS))
        if rel:
            w_rel, w_loop = p.buffer("w_rel", (P, RELS, D)), p.buffer("w_loop", (P, D))
            b_rel, relbuf = p.buffer("b_rel", (P, D)), p.buffer("relbuf", (P, 2, RELS * D))
        loaded, wflip, wkept = p.semaphore("weights_in"), p.semaphore("weight_flipped"), p.semaphore("weight_kept")
        tile_ready, flipped, kept = p.semaphore("tile_ready"), p.semaphore("flipped"), p.semaphore("kept")
        z_made, z_kept, rows_ready = p.semaphore("z_made"), p.semaphore("z_kept"), p.semaphore("rows_ready")
        dst_kept, rows_out, chain = p.semaphore("dst_kept"), p.semaphore("rows_out"), p.semaphore("chain")
        loop_made, loop_kept = p.semaphore("loop_made"), p.semaphore("loop_kept")
        rel_made, even_kept, odd_kept = p.semaphore("rel_made"), p.semaphore("even_kept"), p.semaphore("odd_kept")
        rel_out = [p.semaphore(f"rel_out{s}") for s in range(2)]
        uses = [NB - NB // 2, NB // 2]
        n_loads = 16 * (6 if rel else 3)
        zv = zrow[:, :, :].rearrange("p b (h z) -> p b h z", h=HEADS)

        def slot_free(engine, t, j):
            hold(engine, rel_out[j % 2], (t * uses[j % 2] + j // 2) * 16)

        with nc.Block() as block:
            @block.sync
            def _(sp):
                sp.dma_start(wz_in[:, :], w_z).then_inc(loaded, 16)
                load_row(sp, asrc, w_src, loaded)
                load_row(sp, adst, w_dst, loaded)
                if rel:
                    sp.dma_start(w_rel[:, :, :], a["L0_gnn_W_rel"][layer].rearrange("r d o -> d r o")
                                 ).then_inc(loaded, 16)
                    sp.dma_start(w_loop[:, :], a["L0_gnn_W_loop"][layer]).then_inc(loaded, 16)
                    load_row(sp, b_rel, a["L0_gnn_b_rel"][layer], loaded)
                if rel:
                    tab = g.table0.rearrange("(b p r) c -> p b r c", p=P, r=RELS)
                else:
                    tab = g.table2.rearrange("(b p) c -> p b c", p=P)

                def step(t):
                    sp.wait_ge(rows_ready, t + 1)
                    park(sp)
                    if not rel:
                        sp.dma_start(tab[:, bins_of(t), :], zrow[:, :, :]).then_inc(rows_out, 16)
                        return
                    for j in range(NB):
                        sp.dma_start(tab[:, bass.ds(t * NB + j, 1), :, D:D + ZW].rearrange("p b r c -> p (b r) c"),
                                     zrow[:, j, :].unsqueeze(1).to_broadcast([P, RELS, ZW])).then_inc(rows_out, 16)
                    for j in range(NB):
                        sp.wait_ge(even_kept, t * NB + j + 1)
                        park(sp)
                        sp.wait_ge(odd_kept, t * NB + j + 1)
                        park(sp)
                        sp.dma_start(tab[:, bass.ds(t * NB + j, 1), :, 0:D].rearrange("p b r c -> p (b r) c"),
                                     relbuf[:, j % 2, :].rearrange("p (r c) -> p r c", r=RELS)
                                     ).then_inc(rel_out[j % 2], 16)
                steps(sp, NSTEPS, step)
                sp.wait_ge(rows_out, 16 * (NBINS if rel else NSTEPS))
                if rel:
                    for s in range(2):
                        sp.wait_ge(rel_out[s], 16 * NSTEPS * uses[s])

            @block.tensor
            def _(pe):
                pe.wait_ge(loaded, n_loads)
                weight = wz_in
                if flip_w:
                    pe.transpose(g.bank[1][:, 0:D], wz_in[:, :], g.ident[:, :]).then_inc(wflip, 1)
                    pe.wait_ge(wkept, 1)
                    weight = wz

                def step(t):
                    if rel:
                        hold(pe, loop_kept, t)
                    else:
                        hold(pe, kept, t)
                    flip(pe, g, cur, tile_ready, t + 1, flipped)
                    pe.wait_ge(kept, t + 1)
                    hold(pe, z_kept, t)
                    product(pe, g, 1, [(curT, weight[:, :])], z_made)
                    if not rel:
                        return
                    product(pe, g, 0, [(curT, w_loop[:, :])], loop_made)
                    for j in range(NB):
                        for half in range(2):
                            hold(pe, odd_kept if half else even_kept, t * NB + j)
                            for q in range(2):
                                r = half * 8 + q * 4
                                ins = pe.matmul(g.bank[2 + half][:, q * 512:(q + 1) * 512], curT[:, j, :],
                                                w_rel[:, r:r + 4, :].rearrange("p r c -> p (r c)"),
                                                start=True, stop=True)
                            ins.then_inc(rel_made, 1)
                steps(pe, NSTEPS, step)

            @block.scalar
            def _(act):
                if flip_w:
                    act.wait_ge(wflip, 1)
                    act.activation(wz[:, :], g.bank[1][:, 0:D], ACT.Copy).then_inc(wkept, 1)

                def step(t):
                    hold(act, rel_made if rel else z_made, t * (2 * NB if rel else 1))
                    keep_flipped(act, g, curT, flipped, t + 1, kept)
                    act.wait_ge(z_made, t + 1)
                    hold(act, dst_kept, t)
                    hold(act, rows_out, 16 * t * (NB if rel else 1))
                    act.activation(zv[:, :, :, 0:DH].rearrange("p b h z -> p (b h) z"),
                                   g.bank[1][:, 0:NB * D].rearrange("p (k z) -> p k z", z=DH), ACT.Copy
                                   ).then_inc(z_kept, 1)
                    if rel:
                        for j in range(NB):
                            act.wait_ge(rel_made, t * 2 * NB + 2 * j + 1)
                            slot_free(act, t, j)
                            act.activation(relbuf[:, j % 2, 0:1024], g.bank[2][:, :], ACT.Copy
                                           ).then_inc(even_kept, 1)
                steps(act, NSTEPS, step)

            @block.vector
            def _(v):
                c = Chain(v, chain)
                clear_sums(v, c, g)
                v.wait_ge(loaded, n_loads)
                PER = 3

                def step(t):
                    d = Chain(v, chain, t * PER + 1)
                    hold(v, flipped, t)
                    v.tensor_scalar(cur[:, :, :], inp[:, bins_of(t), :], 1.0, None, ALU.mult).then_inc(tile_ready, 1)
                    v.wait_ge(z_kept, t + 1)
                    hold(v, dst_kept, t)
                    ins = node_scores(v, d, zrow, prod, asrc, zv[:, :, :, DH])
                    ins.then_inc(rows_ready, 1)
                    v.wait_ge(rows_ready, t + 1)
                    d.link(node_scores(v, d, zrow, prod, adst, er[:, :, :]))
                    v.tensor_tensor(g.dst[:, bins_of(t), 0:HEADS], er[:, :, :], er[:, :, :], ALU.max
                                    ).then_inc(dst_kept, 1)
                    d.end(PER)
                    if rel:
                        v.wait_ge(loop_made, t + 1)
                        v.tensor_tensor(g.acc[:, bins_of(t), 0:D], bank_tiles(g, 0), over_bins(b_rel), ALU.add
                                        ).then_inc(loop_kept, 1)
                        for j in range(NB):
                            v.wait_ge(rel_made, t * 2 * NB + 2 * j + 2)
                            slot_free(v, t, j)
                            v.tensor_copy(relbuf[:, j % 2, 1024:2048], g.bank[3][:, :]).then_inc(odd_kept, 1)
                steps(v, NSTEPS, step)


def relational_close(g, layer):
    a, nc = g.a, g.nc
    gated, last = layer == 0, layer == 2
    with Pass(g, f"close0{layer}") as p:
        w_fuse, b_gat, b_fuse = p.buffer("w_fuse", (P, 2, D)), p.buffer("b_gat", (P, D)), p.buffer("b_fuse", (P, D))
        w_gate, b_gate, w_tw = p.buffer("w_gate", (P, D)), p.buffer("b_gate", (P, D)), p.buffer("w_tw", (P, D))
        rel, gat, hc = p.buffer("rel"), p.buffer("gat"), p.buffer("hc")
        relT, gatT, denom = p.buffer("relT"), p.buffer("gatT"), p.buffer("denom", (P, NB, HEADS))
        stat, square = p.buffer("stat", (P, 4, NB)), p.buffer("square")
        loaded, tile_ready, flipped, kept = (p.semaphore("weights_in"), p.semaphore("tile_ready"), p.semaphore("flipped"),
                                             p.semaphore("kept"))
        made, gate_in, gate_made, chain = (p.semaphore("product_made"), p.semaphore("gate_in"), p.semaphore("gate_made"),
                                           p.semaphore("chain"))
        hc_kept = p.semaphore("hc_kept")
        variance_ready, deviation_ready = p.semaphore("variance_ready"), p.semaphore("deviation_ready")
        F = 3 if gated else 2
        M = 2 if gated else 1
        with nc.Block() as block:
            @block.sync
            def _(sp):
                sp.dma_start(w_fuse[:, :, :], a["L0_gnn_W_fuse"].rearrange("(k p) c -> p k c", k=2)
                             ).then_inc(loaded, 16)
                load_row(sp, b_gat, a["L0_gnn_b_gat"][layer], loaded)
                load_row(sp, b_fuse, a["L0_gnn_b_fuse"], loaded)
                sp.dma_start(w_gate[:, :], a["L0_gnn_W_gate"][0:D, :]).then_inc(loaded, 16)
                load_row(sp, w_tw, a["L0_gnn_W_gate"][D, :], loaded)
                load_row(sp, b_gate, a["L0_gnn_b_gate"], loaded)
                sp.wait_ge(loaded, 96)

            @block.tensor
            def _(pe):
                pe.wait_ge(loaded, 96)

                def step(t):
                    hold(pe, kept, F * t)
                    flip(pe, g, rel, tile_ready, 2 * t + 1, flipped)
                    pe.wait_ge(kept, F * t + 1)
                    flip(pe, g, gat, tile_ready, 2 * t + 2, flipped)
                    pe.wait_ge(kept, F * t + 2)
                    hold(pe, hc_kept, t)
                    product(pe, g, 1, [(relT, w_fuse[:, 0, :]), (gatT, w_fuse[:, 1, :])], made)
                    if gated:
                        flip(pe, g, hc, hc_kept, t + 1, flipped)
                        pe.wait_ge(kept, F * t + 3)
                        hold(pe, gate_in, t)
                        product(pe, g, 2, [(relT, w_gate[:, :])], made)
                steps(pe, NSTEPS, step)

            @block.scalar
            def _(act):
                def step(t):
                    hold(act, made, M * t)
                    keep_flipped(act, g, relT, flipped, F * t + 1, kept)
                    keep_flipped(act, g, gatT, flipped, F * t + 2, kept)
                    if gated:
                        act.wait_ge(made, M * t + 1)
                        keep_flipped(act, g, relT, flipped, F * t + 3, kept)
                        act.wait_ge(gate_in, t + 1)
                        act.activation(flat(gat), flat(rel), ACT.Sigmoid).then_inc(gate_made, 1)
                    if last:
                        deviation(act, stat, variance_ready, t + 1, deviation_ready)
                steps(act, NSTEPS, step)

            @block.vector
            def _(v):
                v.wait_ge(loaded, 96)
                c = Chain(v, chain)
                c.link(v.scalar_tensor_tensor(b_gate[:, :], w_tw[:, :], g.tw_mean[:, 0:1], b_gate[:, :],
                                              ALU.mult, ALU.add))
                PER = ATTENDED_LINKS + (2 + NORM_LINKS if last else 1) + (1 if gated else 0)

                def step(t):
                    d = Chain(v, chain, t * PER + 1)
                    hold(v, flipped, F * t)
                    v.tensor_scalar(rel[:, :, :], g.acc[:, bins_of(t), 0:D], 1.0, None, ALU.mult
                                    ).then_inc(tile_ready, 1)
                    attended(v, d, g, t, gat, denom)
                    v.tensor_tensor(gat[:, :, :], gat[:, :, :], over_bins(b_gat), ALU.add).then_inc(tile_ready, 1)
                    v.wait_ge(made, M * t + 1)
                    v.tensor_tensor(hc[:, :, :], bank_tiles(g, 1), over_bins(b_fuse), ALU.add
                                    ).then_inc(hc_kept, 1)
                    v.wait_ge(hc_kept, t + 1)
                    if gated:
                        v.wait_ge(made, M * t + 2)
                        v.tensor_tensor(rel[:, :, :], bank_tiles(g, 2), over_bins(b_gate), ALU.add
                                        ).then_inc(gate_in, 1)
                        v.wait_ge(gate_made, t + 1)
                        d.link(v.tensor_tensor(hc[:, :, :], hc[:, :, :], gat[:, :, :], ALU.mult))
                    if last:
                        d.link(v.scalar_tensor_tensor(hc[:, :, :], hc[:, :, :], 0.0, g.x[:, bins_of(t), :],
                                                      ALU.max, ALU.add))
                        normalise(v, d, hc, square, stat, variance_ready, deviation_ready, t + 1)
                        d.link(v.tensor_scalar(g.x[:, bins_of(t), :], hc[:, :, :], 1.0, None, ALU.mult))
                    else:
                        d.link(v.tensor_scalar(g.h[:, bins_of(t), :], hc[:, :, :], 0.0, None, ALU.max))
                    d.end(PER)
                steps(v, NSTEPS, step)


def gated_sources(g):
    a, nc = g.a, g.nc
    with Pass(g, "source1") as p:
        w1, we1 = p.buffer("w1", (P, D)), p.buffer("we1", (P, 2, D))
        b1, g1, bt1, be1 = (p.buffer(n, (P, D)) for n in ("b1", "g1", "bt1", "be1"))
        nv = p.buffer("nv", (P, NBINS))
        cur, curT, square, stat = p.buffer("cur"), p.buffer("curT"), p.buffer("square"), p.buffer("stat", (P, 4, NB))
        hc, row = p.buffer("hc"), p.buffer("row", (P, NB, 2 * D + 1))
        loaded, nv_zero, tile_ready, flipped, kept = (p.semaphore("weights_in"), p.semaphore("node_vec_cleared"),
                                                      p.semaphore("tile_ready"), p.semaphore("flipped"), p.semaphore("kept"))
        made, bank_read, rows_ready, rows_out, chain = (p.semaphore("product_made"), p.semaphore("product_read"),
                                                        p.semaphore("rows_ready"), p.semaphore("rows_out"),
                                                        p.semaphore("chain"))
        a_kept, h_ready = p.semaphore("a_kept"), p.semaphore("h_ready")
        variance_ready, deviation_ready = p.semaphore("variance_ready"), p.semaphore("deviation_ready")
        with nc.Block() as block:
            @block.sync
            def _(sp):
                sp.dma_start(w1[:, :], a["L1_gnn_W1"]).then_inc(loaded, 16)
                sp.dma_start(we1[:, :, :], a["L1_gnn_We1"].rearrange("(k p) c -> p k c", k=2)).then_inc(loaded, 16)
                for tile, n in ((b1, "b1"), (g1, "g1"), (bt1, "bt1"), (be1, "be1")):
                    load_row(sp, tile, a["L1_gnn_" + n], loaded)
                full = (NBINS - 1) * P
                sp.wait_ge(nv_zero, 1)
                sp.dma_start(nv[:, 0:NBINS - 1], a["node_vec"][0:full].rearrange("(b p) -> p b", p=P),
                             allow_slow_non_contiguous=True).then_inc(loaded, 16)
                sp.dma_start(nv[0:LAST, NBINS - 1:NBINS], a["node_vec"][full:NODES].unsqueeze(1)
                             ).then_inc(loaded, 16)
                tab = g.table1.rearrange("(b p) c -> p b c", p=P)

                def step(t):
                    sp.wait_ge(rows_ready, t + 1)
                    park(sp)
                    sp.wait_ge(a_kept, t + 1)
                    park(sp)
                    sp.dma_start(tab[:, bins_of(t), :], row[:, :, :]).then_inc(rows_out, 16)
                steps(sp, NSTEPS, step)
                sp.wait_ge(rows_out, 16 * NSTEPS)

            @block.tensor
            def _(pe):
                pe.wait_ge(loaded, 128)

                def step(t):
                    hold(pe, kept, 2 * t)
                    flip(pe, g, cur, tile_ready, t + 1, flipped)
                    pe.wait_ge(kept, 2 * t + 1)
                    hold(pe, bank_read, 2 * t)
                    product(pe, g, 1, [(curT, w1[:, :])], made)
                    flip(pe, g, hc, h_ready, t + 1, flipped)
                    pe.wait_ge(kept, 2 * t + 2)
                    hold(pe, a_kept, t)
                    product(pe, g, 2, [(curT, we1[:, 0, :])], made)
                    product(pe, g, 3, [(curT, we1[:, 1, :])], made)
                steps(pe, NSTEPS, step)

            @block.scalar
            def _(act):
                def step(t):
                    hold(act, made, 3 * t)
                    keep_flipped(act, g, curT, flipped, 2 * t + 1, kept)
                    deviation(act, stat, variance_ready, t + 1, deviation_ready)
                    act.wait_ge(made, 3 * t + 1)
                    keep_flipped(act, g, curT, flipped, 2 * t + 2, kept)
                    act.wait_ge(made, 3 * t + 2)
                    hold(act, rows_out, 16 * t)
                    act.activation(row[:, :, D:2 * D], bank_tiles(g, 2), ACT.Copy).then_inc(a_kept, 1)
                steps(act, NSTEPS, step)

            @block.vector
            def _(v):
                v.memset(nv[:, :], 0.0).then_inc(nv_zero, 1)
                c = Chain(v, chain)
                clear_sums(v, c, g)
                v.wait_ge(loaded, 128)
                PER = NORM_LINKS + 4

                def step(t):
                    d = Chain(v, chain, t * PER + 1)
                    hold(v, flipped, 2 * t)
                    v.tensor_scalar(cur[:, :, :], g.x[:, bins_of(t), :], 1.0, None, ALU.mult).then_inc(tile_ready, 1)
                    v.wait_ge(made, 3 * t + 1)
                    v.tensor_tensor(hc[:, :, :], bank_tiles(g, 1), over_bins(b1), ALU.add).then_inc(bank_read, 1)
                    v.wait_ge(bank_read, 2 * t + 1)
                    normalise(v, d, hc, square, stat, variance_ready, deviation_ready, t + 1)
                    d.link(v.tensor_tensor(hc[:, :, :], hc[:, :, :], over_bins(g1), ALU.mult))
                    d.link(v.tensor_tensor(hc[:, :, :], hc[:, :, :], over_bins(bt1), ALU.add))
                    v.tensor_scalar(hc[:, :, :], hc[:, :, :], 0.0, None, ALU.max).then_inc(h_ready, 1)
                    v.wait_ge(h_ready, t + 1)
                    d.link(v.tensor_scalar(g.h[:, bins_of(t), :], hc[:, :, :], 1.0, None, ALU.mult))
                    hold(v, rows_out, 16 * t)
                    v.tensor_copy(row[:, :, 0:D], hc[:, :, :])
                    v.tensor_tensor(row[:, :, 2 * D], nv[:, bins_of(t)], nv[:, bins_of(t)], ALU.max
                                    ).then_inc(rows_ready, 1)
                    v.wait_ge(made, 3 * t + 3)
                    d.link(v.tensor_tensor(square[:, :, :], bank_tiles(g, 3), over_bins(be1), ALU.add))
                    v.tensor_scalar(g.dst[:, bins_of(t), :], square[:, :, :], 1.0, None, ALU.mult
                                    ).then_inc(bank_read, 1)
                    v.wait_ge(bank_read, 2 * t + 2)
                    d.end(PER)
                steps(v, NSTEPS, step)


def gated_close(g):
    a, nc = g.a, g.nc
    with Pass(g, "close1") as p:
        wg = p.buffer("wg", (P, 2, D))
        bg, g2, bt2 = (p.buffer(n, (P, D)) for n in ("bg", "g2", "bt2"))
        hc, ag, hT, aT = p.buffer("hc"), p.buffer("ag"), p.buffer("hT"), p.buffer("aT")
        gin, gate, square, stat = p.buffer("gin"), p.buffer("gate"), p.buffer("square"), p.buffer("stat", (P, 4, NB))
        loaded, tile_ready, flipped, kept = (p.semaphore("weights_in"), p.semaphore("tile_ready"), p.semaphore("flipped"),
                                             p.semaphore("kept"))
        made, gate_in, gate_made, chain = (p.semaphore("product_made"), p.semaphore("gate_in"), p.semaphore("gate_made"),
                                           p.semaphore("chain"))
        variance_ready, deviation_ready = p.semaphore("variance_ready"), p.semaphore("deviation_ready")
        with nc.Block() as block:
            @block.sync
            def _(sp):
                sp.dma_start(wg[:, :, :], a["L1_gnn_Wg"].rearrange("(k p) c -> p k c", k=2)).then_inc(loaded, 16)
                for tile, n in ((bg, "bg"), (g2, "g2"), (bt2, "bt2")):
                    load_row(sp, tile, a["L1_gnn_" + n], loaded)
                sp.wait_ge(loaded, 64)

            @block.tensor
            def _(pe):
                pe.wait_ge(loaded, 64)

                def step(t):
                    hold(pe, kept, 2 * t)
                    flip(pe, g, hc, tile_ready, 2 * t + 1, flipped)
                    pe.wait_ge(kept, 2 * t + 1)
                    flip(pe, g, ag, tile_ready, 2 * t + 2, flipped)
                    pe.wait_ge(kept, 2 * t + 2)
                    hold(pe, gate_in, t)
                    product(pe, g, 1, [(hT, wg[:, 0, :]), (aT, wg[:, 1, :])], made)
                steps(pe, NSTEPS, step)

            @block.scalar
            def _(act):
                def step(t):
                    hold(act, made, t)
                    keep_flipped(act, g, hT, flipped, 2 * t + 1, kept)
                    keep_flipped(act, g, aT, flipped, 2 * t + 2, kept)
                    act.wait_ge(gate_in, t + 1)
                    act.activation(flat(gate), flat(gin), ACT.Sigmoid).then_inc(gate_made, 1)
                    deviation(act, stat, variance_ready, 2 * t + 1, deviation_ready)
                    deviation(act, stat, variance_ready, 2 * t + 2, deviation_ready)
                steps(act, NSTEPS, step)

            @block.vector
            def _(v):
                v.wait_ge(loaded, 64)
                PER = 2 * NORM_LINKS + 7

                def step(t):
                    d = Chain(v, chain, t * PER)
                    hold(v, flipped, 2 * t)
                    v.tensor_scalar(hc[:, :, :], g.h[:, bins_of(t), :], 1.0, None, ALU.mult).then_inc(tile_ready, 1)
                    v.tensor_scalar(ag[:, :, :], g.acc[:, bins_of(t), 0:D], 1.0, None, ALU.mult
                                    ).then_inc(tile_ready, 1)
                    v.wait_ge(made, t + 1)
                    v.tensor_tensor(gin[:, :, :], bank_tiles(g, 1), over_bins(bg), ALU.add).then_inc(gate_in, 1)
                    v.wait_ge(gate_made, t + 1)
                    d.link(v.tensor_tensor(ag[:, :, :], ag[:, :, :], hc[:, :, :], ALU.subtract))
                    d.link(v.tensor_tensor(ag[:, :, :], ag[:, :, :], gate[:, :, :], ALU.mult))
                    d.link(v.tensor_tensor(ag[:, :, :], ag[:, :, :], hc[:, :, :], ALU.add))
                    normalise(v, d, ag, square, stat, variance_ready, deviation_ready, 2 * t + 1)
                    d.link(v.tensor_tensor(ag[:, :, :], ag[:, :, :], over_bins(g2), ALU.mult))
                    d.link(v.tensor_tensor(ag[:, :, :], ag[:, :, :], over_bins(bt2), ALU.add))
                    d.link(v.tensor_tensor(ag[:, :, :], ag[:, :, :], g.x[:, bins_of(t), :], ALU.add))
                    normalise(v, d, ag, square, stat, variance_ready, deviation_ready, 2 * t + 2)
                    d.link(v.tensor_scalar(g.x[:, bins_of(t), :], ag[:, :, :], 1.0, None, ALU.mult))
                    d.end(PER)
                steps(v, NSTEPS, step)


def edge_attention_close(g):
    a, nc = g.a, g.nc
    with Pass(g, "close2") as p:
        bias, gamma, beta = (p.buffer(n, (P, D)) for n in ("bias", "gamma", "beta"))
        y, low, square, stat = p.buffer("y"), p.buffer("low"), p.buffer("square"), p.buffer("stat", (P, 4, NB))
        denom = p.buffer("denom", (P, NB, HEADS))
        loaded, low_ready, low_made, chain = (p.semaphore("weights_in"), p.semaphore("low_ready"), p.semaphore("low_made"),
                                              p.semaphore("chain"))
        variance_ready, deviation_ready = p.semaphore("variance_ready"), p.semaphore("deviation_ready")
        with nc.Block() as block:
            @block.sync
            def _(sp):
                for tile, n in ((bias, "bias"), (gamma, "ln_gamma"), (beta, "ln_beta")):
                    load_row(sp, tile, a["L2_gnn_" + n], loaded)
                sp.wait_ge(loaded, 48)

            @block.scalar
            def _(act):
                def step(t):
                    deviation(act, stat, variance_ready, 2 * t + 1, deviation_ready)
                    act.wait_ge(low_ready, t + 1)
                    act.activation(flat(low), flat(low), ACT.Exp).then_inc(low_made, 1)
                    deviation(act, stat, variance_ready, 2 * t + 2, deviation_ready)
                steps(act, NSTEPS, step)

            @block.vector
            def _(v):
                v.wait_ge(loaded, 48)
                PER = ATTENDED_LINKS + 2 * NORM_LINKS + 8

                def step(t):
                    d = Chain(v, chain, t * PER)
                    attended(v, d, g, t, y, denom)
                    d.link(v.tensor_tensor(y[:, :, :], y[:, :, :], over_bins(bias), ALU.add))
                    d.link(v.tensor_tensor(y[:, :, :], y[:, :, :], g.x[:, bins_of(t), :], ALU.add))
                    normalise(v, d, y, square, stat, variance_ready, deviation_ready, 2 * t + 1)
                    d.link(v.tensor_tensor(y[:, :, :], y[:, :, :], over_bins(gamma), ALU.mult))
                    d.link(v.tensor_tensor(y[:, :, :], y[:, :, :], over_bins(beta), ALU.add))
                    v.tensor_scalar(low[:, :, :], y[:, :, :], 0.0, None, ALU.min).then_inc(low_ready, 1)
                    d.link(v.tensor_scalar(y[:, :, :], y[:, :, :], 0.0, -1.0, ALU.max, ALU.add))
                    v.wait_ge(low_made, t + 1)
                    d.link(v.tensor_tensor(y[:, :, :], y[:, :, :], low[:, :, :], ALU.add))
                    d.link(v.tensor_tensor(y[:, :, :], y[:, :, :], g.x[:, bins_of(t), :], ALU.add))
                    normalise(v, d, y, square, stat, variance_ready, deviation_ready, 2 * t + 2)
                    d.link(v.tensor_scalar(g.x[:, bins_of(t), :], y[:, :, :], 1.0, None, ALU.mult))
                    d.end(PER)
                steps(v, NSTEPS, step)


def conv_sources(g, k, inp):
    a, nc = g.a, g.nc
    with Pass(g, f"source3{k}") as p:
        names = ("q", "k", "v", "skip")
        w = {n: p.buffer("w" + n, (P, D)) for n in names}
        b = {n: p.buffer("b" + n, (P, D)) for n in names}
        cur, curT, qs, row = p.buffer("cur"), p.buffer("curT"), p.buffer("qs"), p.buffer("row", (P, NB, D + ZW))
        loaded, tile_ready, flipped, kept = (p.semaphore("weights_in"), p.semaphore("tile_ready"), p.semaphore("flipped"),
                                             p.semaphore("kept"))
        made, taken, rows_ready, rows_out, chain = (p.semaphore("product_made"), p.semaphore("products_taken"),
                                                    p.semaphore("rows_ready"), p.semaphore("rows_out"), p.semaphore("chain"))
        with nc.Block() as block:
            @block.sync
            def _(sp):
                for n in names:
                    sp.dma_start(w[n][:, :], a[f"L3_gnn_W{n}{k}"]).then_inc(loaded, 16)
                    load_row(sp, b[n], a[f"L3_gnn_b{n}{k}"], loaded)
                tab = g.table3.rearrange("(b p) c -> p b c", p=P)

                def step(t):
                    sp.wait_ge(rows_ready, t + 1)
                    park(sp)
                    sp.dma_start(tab[:, bins_of(t), :], row[:, :, :]).then_inc(rows_out, 16)
                steps(sp, NSTEPS, step)
                sp.wait_ge(rows_out, 16 * NSTEPS)

            @block.tensor
            def _(pe):
                pe.wait_ge(loaded, 128)

                def step(t):
                    hold(pe, taken, t)
                    flip(pe, g, cur, tile_ready, t + 1, flipped)
                    pe.wait_ge(kept, t + 1)
                    for bank, n in ((1, "k"), (2, "v"), (3, "q"), (0, "skip")):
                        product(pe, g, bank, [(curT, w[n][:, :])], made)
                steps(pe, NSTEPS, step)

            @block.scalar
            def _(act):
                def step(t):
                    hold(act, made, 4 * t)
                    keep_flipped(act, g, curT, flipped, t + 1, kept)
                steps(act, NSTEPS, step)

            @block.vector
            def _(v):
                c = Chain(v, chain)
                clear_sums(v, c, g)
                c.link(v.memset(row[:, :, :].rearrange("p b c -> p (b c)"), 0.0))
                v.wait_ge(loaded, 128)
                PER = 1
                rz = row[:, :, D:D + ZW].rearrange("p b (h z) -> p b h z", h=HEADS)[:, :, :, 0:DH]
                bv = b["v"][:, :].rearrange("p (h c) -> p h c", h=HEADS).unsqueeze(1).to_broadcast([P, NB, HEADS, DH])

                def step(t):
                    d = Chain(v, chain, t * PER + 2)
                    hold(v, flipped, t)
                    v.tensor_scalar(cur[:, :, :], inp[:, bins_of(t), :], 1.0, None, ALU.mult).then_inc(tile_ready, 1)
                    v.wait_ge(made, 4 * t + 2)
                    hold(v, rows_out, 16 * t)
                    v.tensor_tensor(row[:, :, 0:D], bank_tiles(g, 1), over_bins(b["k"]), ALU.add)
                    v.tensor_tensor(rz, heads_of(bank_tiles(g, 2)), bv, ALU.add).then_inc(rows_ready, 1)
                    v.wait_ge(made, 4 * t + 3)
                    hold(v, taken, t)
                    d.link(v.tensor_tensor(qs[:, :, :], bank_tiles(g, 3), over_bins(b["q"]), ALU.add))
                    v.tensor_scalar(g.dst[:, bins_of(t), :], qs[:, :, :], float(DH) ** -0.5, None, ALU.mult)
                    v.wait_ge(made, 4 * t + 4)
                    v.tensor_tensor(g.acc[:, bins_of(t), 0:D], bank_tiles(g, 0), over_bins(b["skip"]), ALU.add
                                    ).then_inc(taken, 1)
                    d.end(PER)
                steps(v, NSTEPS, step)


def conv_close(g, last):
    nc = g.nc
    with Pass(g, f"close3{int(last)}") as p:
        y, square, stat = p.buffer("y"), p.buffer("square"), p.buffer("stat", (P, 4, NB))
        denom = p.buffer("denom", (P, NB, HEADS))
        chain, variance_ready, deviation_ready = (p.semaphore("chain"), p.semaphore("variance_ready"),
                                                  p.semaphore("deviation_ready"))
        written = p.semaphore("result_written")
        PER = ATTENDED_LINKS + (3 + NORM_LINKS if last else 1)
        with nc.Block() as block:
            if last:
                @block.scalar
                def _(act):
                    steps(act, NSTEPS, lambda t: deviation(act, stat, variance_ready, t + 1, deviation_ready))

                @block.sync
                def _(sp):
                    sp.wait_ge(chain, NSTEPS * PER)
                    full = (NBINS - 1) * P
                    sp.dma_start(g.out[0:full, :].rearrange("(b p) c -> p b c", p=P), g.x[:, 0:NBINS - 1, :]
                                 ).then_inc(written, 16)
                    sp.dma_start(g.out[full:NODES, :], g.x[0:LAST, NBINS - 1, :]).then_inc(written, 16)
                    sp.wait_ge(written, 32)

            @block.vector
            def _(v):
                def step(t):
                    d = Chain(v, chain, t * PER)
                    attended(v, d, g, t, y, denom)
                    skip = g.acc[:, bins_of(t), 0:D]
                    if last:
                        d.link(v.tensor_tensor(y[:, :, :], y[:, :, :], skip, ALU.add))
                        d.link(v.tensor_tensor(y[:, :, :], y[:, :, :], g.x[:, bins_of(t), :], ALU.add))
                        normalise(v, d, y, square, stat, variance_ready, deviation_ready, t + 1)
                        d.link(v.tensor_scalar(g.x[:, bins_of(t), :], y[:, :, :], 1.0, None, ALU.mult))
                    else:
                        d.link(v.tensor_tensor(g.h[:, bins_of(t), :], y[:, :, :], skip, ALU.add))
                    d.end(PER)
                steps(v, NSTEPS, step)



def superblocks(engine, step):
    def full(q, s):
        n, m = s + 2, s + 1
        step((q + n // RING, n % RING), (q + m // RING, m % RING), (q, s))
    step((0, 0), None, None)
    step((0, 1), (0, 0), None)
    for s in range(RING):
        full(0, s)
    with engine.Fori(1, (NSUPER - 2) // RING) as q:
        for s in range(RING):
            full(q, s)
    end = (NSUPER - 2) // RING
    step(None, (end, 1), (end, 0))
    step(None, None, (end, 1))


def number(qs):
    return qs[0] * RING + qs[1]


def tiles_of(u):
    return bass.ds(u * ST, ST)


def load_bins(engine, g, u):
    return [engine.value_load(g.bin_row[0:1, bass.ds(u * GPS + k, 1)], min_val=0, max_val=NBINS - 1)
            for k in range(GPS)]


def make_onehot(v, g, u, onehot, onehot_made):
    v.tensor_tensor(onehot[:, :, :], g.place1[:, :].unsqueeze(1).to_broadcast([P, ST, P]),
                    g.places[:, tiles_of(u)].unsqueeze(2).to_broadcast([P, ST, P]), ALU.is_equal
                    ).then_inc(onehot_made, 1)


def gather_rows(pool, g, table, index, ring, rows, ring_kept, sums_made, gathered):
    def one(q, s):
        u = q * len(rows) + s
        hold(pool, sums_made, GPS * (u - len(rows) + 1))
        hold(pool, ring_kept, u)
        park(pool)
        pool.tensor_copy(ring[:, s * ST:(s + 1) * ST], index[:, tiles_of(u)]).then_inc(ring_kept, 1)
        pool.wait_ge(ring_kept, u + 1)
        park(pool)
        for j in range(ST):
            pool.indirect_dma_start(out=rows[s][:, j, :], out_offset=None, in_=table,
                                    in_offset=bass.IndirectOffsetOnAxis(ap=ring[:, s * ST + j:s * ST + j + 1], axis=0)
                                    ).then_inc(gathered[s], 16)
    for s in range(len(rows)):
        one(0, s)
    with pool.Fori(1, NSUPER // len(rows)) as q:
        for s in range(len(rows)):
            one(q, s)
    for s in range(NSUPER % len(rows)):
        one(NSUPER // len(rows), s)


def attention_edges(g, name, table, index, scored_edges=False, conv=None):
    a, nc = g.a, g.nc
    Z = 0 if scored_edges else D
    W = Z + ZW
    A0 = 0 if conv is None and not scored_edges else Z
    ACC0 = D - Z + A0
    with Pass(g, name) as p:
        spare = g.h[:, :, :].rearrange("p b c -> p (b c)")
        rows = [spare[:, s * ST * W:(s + 1) * ST * W].rearrange("p (t c) -> p t c", c=W) for s in range(RING - 1)]
        rows.append(p.buffer("rows3", (P, ST, W))[:, :, :])
        ring = p.buffer("ring", (P, RING * ST), U32)
        onehot = [p.buffer(f"onehot{s}", (P, ST, P)) for s in range(RING)]
        flippedT = [p.buffer(f"onehotT{s}", (P, ST, P)) for s in range(2)]
        maskT = [p.buffer(f"maskT{s}", (P, ST, P), BF16) for s in range(2)]
        parts = p.buffer("parts", (P, ST, P), BF16)
        partsT = [p.buffer(f"partsT{s}", (P, ST, P), BF16) for s in range(2)]
        score = [p.buffer(f"score{s}", (P, ST, HEADS)) for s in range(2)]
        rest = p.buffer("rest", (P, ST, HEADS))
        arg, weight = p.buffer("arg", (P, ST, HEADS)), p.buffer("weight", (P, ST, HEADS))
        gmax, newmax, fall = (p.buffer(n, (P, GPS, HEADS)) for n in ("gmax", "newmax", "fall"))
        rate = [p.buffer(f"rate{s}", (P, GPS, HEADS)) for s in range(2)]
        gathered, seen = g.gathered, p.gathers_before()
        (ring_kept, onehot_made, onehot_flipped, flipped_kept, dst_spread, parts_made, parts_flipped, parts_kept,
         scores_spread, group_scanned, max_made, max_spread, arg_made, weight_made, rate_made, rows_weighted,
         sums_made, sums_taken, chain, cleared) = (p.semaphore(n) for n in (
             "ring_kept", "onehot_made", "onehot_flipped", "flipped_kept", "dst_spread", "parts_made",
             "parts_flipped", "parts_kept", "scores_spread", "group_scanned", "max_made", "max_spread", "arg_made",
             "weight_made", "rate_made", "rows_weighted", "sums_made", "sums_taken", "chain", "cleared"))
        if conv is not None:
            w_e = p.buffer("w_e", (P, D))
            feat = g.edge_score[:, :, :].rearrange("p t h -> p (t h)")[:, 0:2 * ST * P].rearrange(
                "p (s c) -> p s c", s=2)
            feat_in = [p.semaphore(f"feat_in{s}") for s in range(2)]
            w_in, half_ready, half_taken = p.semaphore("w_in"), p.semaphore("half_ready"), p.semaphore("half_taken")
        flip_b = g.bank[0]
        partsT_b = flip_b[:, 0:512].bitcast(BF16)
        spread_b = [g.bank[1], g.bank[2]]
        small_b = g.bank[3][:, 0:2 * ST * HEADS]
        sum_b = g.bank[3][:, 512:512 + W - A0]
        dst_b, max_b = small_b[:, 0:ST * HEADS], small_b[:, ST * HEADS:2 * ST * HEADS]

        def hview(t):
            return t.rearrange("p (b h) -> p b h", h=HEADS)

        def zrows(s):
            return rows[s][:, :, Z:Z + ZW].rearrange("p b (h z) -> p b h z", h=HEADS)

        with nc.Block() as block:
            @block.gpsimd
            def _(pool):
                gather_rows(pool, g, table, index, ring, rows, ring_kept, sums_made, gathered)

            if conv is not None:
                @block.sync
                def _(sp):
                    sp.dma_start(w_e[:, :], a[f"L3_gnn_We{conv}"]).then_inc(w_in, 16)

                    def load(q, s):
                        u = q * 2 + s
                        hold(sp, half_ready, 2 * (u - 1))
                        park(sp)
                        sp.dma_start(feat[:, s, :], g.edge_feat[:, bass.ds(u * (ST * P), ST * P)]
                                     ).then_inc(feat_in[s], 16)
                    load(0, 0)
                    load(0, 1)
                    with sp.Fori(1, NSUPER // 2) as q:
                        load(q, 0)
                        load(q, 1)

            @block.tensor
            def _(pe):
                if conv is not None:
                    pe.wait_ge(w_in, 16)

                def flip_onehot(n):
                    u, s = number(n), n[1]
                    pe.wait_ge(onehot_made, u + 1)
                    hold(pe, parts_kept, u)
                    for j in range(ST):
                        ins = pe.transpose(flip_b[:, j * P:(j + 1) * P], onehot[s][:, j, :], g.ident[:, :])
                    ins.then_inc(onehot_flipped, 1)

                def spread_dst(n):
                    u, s = number(n), n[1] % 2
                    bins = load_bins(pe, g, u)
                    pe.wait_ge(flipped_kept, 2 * u + 2)
                    hold(pe, parts_made, u)
                    hold(pe, arg_made, u - 1)
                    for j in range(ST):
                        ins = pe.matmul(dst_b[:, j * HEADS:(j + 1) * HEADS], flippedT[s][:, j, :],
                                        g.dst[:, bass.ds(bins[j // GT], 1), 0:HEADS].rearrange("p b c -> p (b c)"),
                                        start=True, stop=True)
                    ins.then_inc(dst_spread, 1)

                def spread_half(n, half, bins):
                    u, s = number(n), n[1] % 2
                    if half == 0:
                        pe.wait_ge(flipped_kept, 2 * u + 2)
                        pe.wait_ge(feat_in[s], 16 * (n[0] * (RING // 2) + (n[1] // 2 + 1)))
                    hold(pe, half_taken, 2 * u + half)
                    for j in range(ST // 2):
                        tile = half * (ST // 2) + j
                        pe.matmul(flip_b[:, j * P:(j + 1) * P], flippedT[s][:, tile, :],
                                  g.dst[:, bass.ds(bins[tile // GT], 1), :].rearrange("p b c -> p (b c)"),
                                  start=True, stop=True)
                        ins = pe.matmul(flip_b[:, 512 + j * P:512 + (j + 1) * P],
                                        feat[:, s, tile * P:(tile + 1) * P], w_e[:, :], start=True, stop=True)
                    ins.then_inc(half_ready, 1)

                def flip_parts(n):
                    u, s = number(n), n[1] % 2
                    pe.wait_ge(parts_made, u + 1)
                    for j in range(ST):
                        ins = pe.transpose(partsT_b[:, j * P:(j + 1) * P], parts[:, j, :], g.identb[:, :])
                    ins.then_inc(parts_flipped, 1)

                def spread_scores(m, k):
                    u, s = number(m), m[1] % 2
                    if k == 0:
                        pe.wait_ge(parts_kept, u + 1)
                    hold(pe, group_scanned, GPS * u + k - 1)
                    b = spread_b[k % 2]
                    mask = maskT[s][:, k * GT:(k + 1) * GT, :].rearrange("p t c -> p (t c)")
                    partT = partsT[s][:, k * GT:(k + 1) * GT, :].rearrange("p t c -> p (t c)")
                    for half in range(2):
                        pe.matmul(b[:, half * 512:(half + 1) * 512], g.identb[:, :],
                                  mask.unsqueeze(1).to_broadcast([P, 2, GE]), start=True, stop=False,
                                  skip_group_check=True)
                        for hh in range(2):
                            at = half * 512 + hh * GE
                            ins = pe.matmul(b[:, at:at + GE], g.sel[:, half * 2 + hh, :], partT, start=False,
                                            stop=True, skip_group_check=True)
                    ins.then_inc(scores_spread, 1)

                def spread_max(m):
                    u, s = number(m), m[1] % 2
                    pe.wait_ge(max_made, u + 1)
                    hold(pe, arg_made, u)
                    for j in range(ST):
                        ins = pe.matmul(max_b[:, j * HEADS:(j + 1) * HEADS], flippedT[s][:, j, :],
                                        newmax[:, j // GT, :], start=True, stop=True)
                    ins.then_inc(max_spread, 1)

                def sum_group(o, k):
                    u, s = number(o), o[1]
                    if k == 0:
                        pe.wait_ge(rows_weighted, u + 1)
                    hold(pe, sums_taken, GPS * u + k)
                    for j in range(k * GT, (k + 1) * GT):
                        ins = pe.matmul(sum_b, onehot[s][:, j, :], rows[s][:, j, A0:W],
                                        start=j == k * GT, stop=j == (k + 1) * GT - 1)
                    ins.then_inc(sums_made, 1)

                def step(n, m, o):
                    if n:
                        flip_onehot(n)
                    if m:
                        spread_scores(m, 0)
                        spread_scores(m, 1)
                    if o:
                        sum_group(o, 0)
                    if n:
                        if conv is None:
                            spread_dst(n)
                        else:
                            bins = load_bins(pe, g, number(n))
                            spread_half(n, 0, bins)
                    if o:
                        sum_group(o, 1)
                    if m:
                        spread_scores(m, 2)
                        spread_scores(m, 3)
                    if n and conv is not None:
                        spread_half(n, 1, bins)
                    if o:
                        sum_group(o, 2)
                    if n:
                        flip_parts(n)
                    if o:
                        sum_group(o, 3)
                    if m:
                        spread_max(m)
                superblocks(pe, step)

            @block.scalar
            def _(act):
                def step(n, m, o):
                    if n:
                        u, s = number(n), n[1] % 2
                        act.wait_ge(onehot_flipped, u + 1)
                        hold(act, max_spread, u - 1)
                        act.activation(flippedT[s][:, :, :].rearrange("p t c -> p (t c)"), flip_b[:, :], ACT.Copy
                                       ).then_inc(flipped_kept, 1)
                        hold(act, scores_spread, GPS * (u - 1))
                        act.activation(maskT[s][:, :, :].rearrange("p t c -> p (t c)"), flip_b[:, :], ACT.Copy,
                                       bias=-BIG, scale=BIG).then_inc(flipped_kept, 1)
                        act.wait_ge(parts_flipped, u + 1)
                        act.activation(partsT[s][:, :, :].rearrange("p t c -> p (t c)"), partsT_b[:, :], ACT.Copy
                                       ).then_inc(parts_kept, 1)
                    if m:
                        u, s = number(m), m[1] % 2
                        act.wait_ge(max_made, u + 1)
                        hold(act, sums_taken, GPS * (u - 1))
                        act.activation(rate[s][:, :, :].rearrange("p k h -> p (k h)"),
                                       fall[:, :, :].rearrange("p k h -> p (k h)"), ACT.Exp).then_inc(rate_made, 1)
                        act.wait_ge(arg_made, u + 1)
                        act.activation(weight[:, :, :].rearrange("p k h -> p (k h)"),
                                       arg[:, :, :].rearrange("p k h -> p (k h)"), ACT.Exp).then_inc(weight_made, 1)
                superblocks(act, step)

            @block.vector
            def _(v):
                v.memset(parts[:, :, :].rearrange("p t c -> p (t c)"), 0.0).then_inc(cleared, 1)
                v.wait_ge(cleared, 1)
                LA = (3 if conv is not None or scored_edges else 2) + 3
                LB = 3 * GPS
                LC = GPS

                def convolve_half(n, half, c):
                    u, s = number(n), n[1]
                    if half == 0:
                        v.wait_ge(gathered[s], seen[s] + 16 * ST * (n[0] + 1))
                    tiles = slice(half * (ST // 2), (half + 1) * (ST // 2))
                    v.wait_ge(half_ready, 2 * u + half + 1)
                    e = flip_b[:, 512:1024].rearrange("p (t c) -> p t c", c=D)
                    qd = flip_b[:, 0:512].rearrange("p (t c) -> p t c", c=D)
                    kr = rows[s][:, tiles, 0:D]
                    zr = zrows(s)[:, tiles, :, 0:DH]
                    v.tensor_tensor(zr, zr, e.rearrange("p t (h c) -> p t h c", h=HEADS), ALU.add)
                    c.link(v.tensor_tensor(kr, kr, e, ALU.add))
                    v.tensor_tensor(kr, kr, qd, ALU.mult).then_inc(half_taken, 1)

                def score_parts(n, c):
                    u, s = number(n), n[1]
                    sc = score[s % 2][:, :, :]
                    if conv is None:
                        v.wait_ge(gathered[s], seen[s] + 16 * ST * (n[0] + 1))
                        v.wait_ge(dst_spread, u + 1)
                        c.link(v.tensor_tensor(sc, zrows(s)[:, :, :, DH], hview(dst_b), ALU.add))
                        if scored_edges:
                            c.link(v.tensor_tensor(sc, sc, g.edge_score[:, tiles_of(u), :], ALU.add))
                        c.link(v.scalar_tensor_tensor(sc, sc, 0.2, sc, ALU.mult, ALU.max))
                    else:
                        v.wait_ge(half_taken, 2 * u + 2)
                        c.link(v.tensor_reduce(sc, rows[s][:, :, 0:D].rearrange("p t (h c) -> p t h c", h=HEADS),
                                               AX, ALU.add))
                    hold(v, parts_flipped, u)
                    c.link(v.tensor_copy(parts[:, :, 0:4], sc))
                    c.link(v.tensor_tensor(rest[:, :, :], sc, parts[:, :, 0:4], ALU.subtract))
                    c.link(v.tensor_copy(parts[:, :, 4:8], rest[:, :, :]))
                    v.tensor_tensor(parts[:, :, 8:12], rest[:, :, :], parts[:, :, 4:8], ALU.subtract
                                    ).then_inc(parts_made, 1)
                    v.wait_ge(parts_made, u + 1)

                def scan_group(m, k):
                    u = number(m)
                    v.wait_ge(scores_spread, GPS * u + k + 1)
                    v.tensor_reduce(gmax[:, k, :], spread_b[k % 2][:, :].rearrange("p (h e) -> p h e", h=HEADS),
                                    AX, ALU.max).then_inc(group_scanned, 1)

                def update_max(m, c):
                    u = number(m)
                    bins = load_bins(v, g, u)
                    v.wait_ge(group_scanned, GPS * (u + 1))
                    hold(v, rate_made, u)
                    hold(v, max_spread, u)
                    for k in range(GPS):
                        now = g.top[:, bass.ds(bins[k], 1), :].rearrange("p b h -> p (b h)")
                        c.link(v.tensor_tensor(newmax[:, k, :], now, gmax[:, k, :], ALU.max))
                        c.link(v.tensor_tensor(fall[:, k, :], now, newmax[:, k, :], ALU.subtract))
                        ins = v.tensor_tensor(now, newmax[:, k, :], newmax[:, k, :], ALU.max)
                        if k < GPS - 1:
                            c.link(ins)
                    ins.then_inc(max_made, 1)
                    v.wait_ge(max_made, u + 1)

                def subtract_max(m):
                    u, s = number(m), m[1]
                    v.wait_ge(max_spread, u + 1)
                    hold(v, weight_made, u)
                    v.tensor_tensor(arg[:, :, :], score[s % 2][:, :, :], hview(max_b), ALU.subtract
                                    ).then_inc(arg_made, 1)

                def weigh_rows(m, c):
                    u, s = number(m), m[1]
                    v.wait_ge(weight_made, u + 1)
                    c.link(v.tensor_scalar(zrows(s)[:, :, :, DH], weight[:, :, :], 1.0, None, ALU.min))
                    zr = zrows(s)[:, :, :, 0:DH]
                    v.tensor_tensor(zr, zr, zrows(s)[:, :, :, DH:HZ].to_broadcast([P, ST, HEADS, DH]), ALU.mult
                                    ).then_inc(rows_weighted, 1)

                def take_sums(o, k, c, bins):
                    u, s = number(o), o[1] % 2
                    acc = g.acc[:, bass.ds(bins[k], 1), :]
                    az = acc[:, :, D:D + ZW].rearrange("p b (h z) -> p (b h) z", h=HEADS)
                    if k == 0:
                        v.wait_ge(rate_made, u + 1)
                    hold(v, sums_taken, GPS * u + k)
                    c.link(v.tensor_tensor(az, az, rate[s][:, k, :].unsqueeze(2).to_broadcast([P, HEADS, HZ]),
                                           ALU.mult))
                    v.wait_ge(sums_made, GPS * u + k + 1)
                    part = acc[:, :, ACC0:D + ZW].rearrange("p b c -> p (b c)")
                    v.tensor_tensor(part, part, sum_b, ALU.add).then_inc(sums_taken, 1)

                def step(n, m, o):
                    if o is None:
                        start = LA if m else 0
                    else:
                        start = 2 * LA + LB + number(o) * (LA + LB + LC)
                        if m is None:
                            start -= LA
                    c = Chain(v, chain, start)
                    if n:
                        hold(v, sums_made, GPS * (number(n) - RING + 1))
                        make_onehot(v, g, number(n), onehot[n[1]], onehot_made)
                    if m:
                        scan_group(m, 0)
                        scan_group(m, 1)
                    if o:
                        bins = load_bins(v, g, number(o))
                        take_sums(o, 0, c, bins)
                    if n:
                        if conv is None:
                            score_parts(n, c)
                        else:
                            convolve_half(n, 0, c)
                    if o:
                        take_sums(o, 1, c, bins)
                    if m:
                        scan_group(m, 2)
                        scan_group(m, 3)
                    if n and conv is not None:
                        convolve_half(n, 1, c)
                        score_parts(n, c)
                    if o:
                        take_sums(o, 2, c, bins)
                    if m:
                        update_max(m, c)
                    if o:
                        take_sums(o, 3, c, bins)
                    if m:
                        subtract_max(m)
                        weigh_rows(m, c)
                    assert c.n == (LA if n else 0) + (LB if m else 0) + (LC if o else 0)
                superblocks(v, step)


def gated_edges(g):
    a, nc = g.a, g.nc
    W = 2 * D + 1
    with Pass(g, "edges1") as p:
        rows, ring = p.buffer("rows", (P, 2, ST, W)), p.buffer("ring", (P, 2 * ST), U32)
        onehot = [p.buffer(f"onehot{s}", (P, ST, P)) for s in range(2)]
        flippedT = p.buffer("onehotT", (P, ST, P))
        we2, be2 = p.buffer("we2", (P, D)), p.buffer("be2", (P, 1))
        dot, gate = p.buffer("dot", (P, ST)), p.buffer("gate", (P, ST))
        wt, bt = p.buffer("wt", (P, 64)), p.buffer("bt", (P, 64))
        attrs, feat = p.buffer("attrs", (P, 2, ST * REC)), p.buffer("feat", (P, ST, P))
        featT = p.buffer("featT", (P, 2, ST * P))
        rel, turns, half_pi = p.buffer("rel", (P, ST)), p.buffer("turns", (P, ST, 64)), p.buffer("half_pi", (P, 1))
        angle = p.buffer("angle", (P, ST, 64))
        gathered, seen = g.gathered, p.gathers_before(2)
        attrs_in = [p.semaphore(f"attrs_in{s}") for s in range(2)]
        feat_out = [p.semaphore(f"feat_out{s}") for s in range(2)]
        (ring_kept, onehot_made, onehot_flipped, flipped_kept, dst_spread, dot_made, gate_made, rows_weighted,
         sums_made, sums_taken, chain, loaded, angle_made, cos_made, msg_copied, feat_flipped, featT_kept) = (
             p.semaphore(n) for n in (
                 "ring_kept", "onehot_made", "onehot_flipped", "flipped_kept", "dst_spread", "dot_made", "gate_made",
                 "rows_weighted", "sums_made", "sums_taken", "chain", "weights_in", "angle_made", "cos_made",
                 "msg_copied", "feat_flipped", "featT_kept"))
        flip_b, dst_b, feat_b, sum_b = g.bank[0], g.bank[1], g.bank[2], g.bank[3][:, 0:D]
        rec = g.rec.rearrange("(g p s) r -> p g (s r)", p=P, s=GT)
        with nc.Block() as block:
            @block.gpsimd
            def _(pool):
                gather_rows(pool, g, g.table1, g.src_idx, ring, [rows[:, s, :, :] for s in range(2)], ring_kept,
                            sums_made, gathered)

            @block.sync
            def _(sp):
                load_row(sp, we2, a["L1_gnn_We2"].rearrange("k o -> (o k)"), loaded)
                load_row(sp, be2, a["L1_gnn_be2"], loaded)
                load_row(sp, wt, a["L3_gnn_Wt"].rearrange("o k -> (o k)"), loaded)
                load_row(sp, bt, a["L3_gnn_bt"], loaded)

                def load(q, s):
                    u = q * 2 + s
                    hold(sp, msg_copied, u - 1)
                    park(sp)
                    sp.dma_start(attrs[:, s, :].rearrange("p (g r) -> p g r", g=GPS),
                                 rec[:, bass.ds(u * GPS, GPS), :]).then_inc(attrs_in[s], 16)

                def store(q, s):
                    u = q * 2 + s
                    sp.wait_ge(featT_kept, u + 1)
                    park(sp)
                    sp.dma_start(g.edge_feat[:, bass.ds(u * (ST * P), ST * P)], featT[:, s, :]
                                 ).then_inc(feat_out[s], 16)
                load(0, 0)
                load(0, 1)
                store(0, 0)
                with sp.Fori(0, NSUPER // 2 - 1) as q:
                    load(q + 1, 0)
                    store(q, 1)
                    load(q + 1, 1)
                    store(q + 1, 0)
                store(NSUPER // 2 - 1, 1)
                for s in range(2):
                    sp.wait_ge(feat_out[s], 16 * NSUPER // 2)

            @block.tensor
            def _(pe):
                def one(q, s):
                    u = q * 2 + s
                    pe.wait_ge(onehot_made, u + 1)
                    hold(pe, flipped_kept, u)
                    for j in range(ST):
                        ins = pe.transpose(flip_b[:, j * P:(j + 1) * P], onehot[s][:, j, :], g.ident[:, :])
                    ins.then_inc(onehot_flipped, 1)
                    bins = load_bins(pe, g, u)
                    pe.wait_ge(flipped_kept, u + 1)
                    hold(pe, dot_made, u)
                    for j in range(ST):
                        ins = pe.matmul(dst_b[:, j * P:(j + 1) * P], flippedT[:, j, :],
                                        g.dst[:, bass.ds(bins[j // GT], 1), :].rearrange("p b c -> p (b c)"),
                                        start=True, stop=True)
                    ins.then_inc(dst_spread, 1)
                    pe.wait_ge(cos_made, u + 1)
                    pe.wait_ge(msg_copied, u + 1)
                    hold(pe, featT_kept, u)
                    for j in range(ST):
                        ins = pe.transpose(feat_b[:, j * P:(j + 1) * P], feat[:, j, :], g.ident[:, :])
                    ins.then_inc(feat_flipped, 1)
                    pe.wait_ge(rows_weighted, u + 1)
                    for k in range(GPS):
                        hold(pe, sums_taken, GPS * u + k)
                        for j in range(k * GT, (k + 1) * GT):
                            ins = pe.matmul(sum_b, onehot[s][:, j, :], rows[:, s, j, 0:D],
                                            start=j == k * GT, stop=j == (k + 1) * GT - 1)
                        ins.then_inc(sums_made, 1)
                one(0, 0)
                one(0, 1)
                with pe.Fori(1, NSUPER // 2) as q:
                    one(q, 0)
                    one(q, 1)

            @block.scalar
            def _(act):
                act.wait_ge(loaded, 64)
                act.wait_ge(chain, 1)

                def one(q, s):
                    u = q * 2 + s
                    act.wait_ge(onehot_flipped, u + 1)
                    hold(act, dst_spread, u)
                    act.activation(flippedT[:, :, :].rearrange("p t c -> p (t c)"), flip_b[:, :], ACT.Copy
                                   ).then_inc(flipped_kept, 1)
                    act.wait_ge(angle_made, u + 1)
                    hold(act, feat_flipped, u)
                    act.activation(feat[:, :, 0:64], angle[:, :, :], ACT.Sin, bias=half_pi[:, 0:1], scale=-1.0
                                   ).then_inc(cos_made, 1)
                    act.wait_ge(feat_flipped, u + 1)
                    hold(act, feat_out[s], 16 * q)
                    act.activation(featT[:, s, :], feat_b[:, :], ACT.Copy).then_inc(featT_kept, 1)
                    act.wait_ge(dot_made, u + 1)
                    hold(act, rows_weighted, u)
                    act.activation(gate[:, :], dot[:, :], ACT.Sigmoid, bias=be2[:, 0:1]).then_inc(gate_made, 1)
                one(0, 0)
                one(0, 1)
                with act.Fori(1, NSUPER // 2) as q:
                    one(q, 0)
                    one(q, 1)

            @block.vector
            def _(v):
                v.memset(half_pi[:, :], TWO_PI / 4).then_inc(chain, 1)
                v.wait_ge(loaded, 64)
                C1, C2 = 6.28125, TWO_PI - 6.28125
                L = 9

                def one(q, s):
                    u = q * 2 + s
                    c = Chain(v, chain, u * L + 1)
                    hold(v, sums_made, GPS * (u - 1))
                    make_onehot(v, g, u, onehot[s], onehot_made)
                    v.wait_ge(gathered[s], seen[s] + 16 * ST * (q + 1))
                    hold(v, cos_made, u)
                    c.link(v.tensor_tensor(rel[:, :], rows[:, s, :, 2 * D], g.rel_t[:, tiles_of(u)], ALU.subtract))
                    wide = [P, ST, 64]
                    c.link(v.tensor_tensor(angle[:, :, :], rel[:, :].unsqueeze(2).to_broadcast(wide),
                                           wt[:, :].unsqueeze(1).to_broadcast(wide), ALU.mult))
                    c.link(v.tensor_tensor(angle[:, :, :], angle[:, :, :], bt[:, :].unsqueeze(1).to_broadcast(wide),
                                           ALU.add))
                    c.link(v.tensor_scalar(turns[:, :, :], angle[:, :, :], 1.0 / TWO_PI, 12582912.0, ALU.mult,
                                           ALU.add))
                    c.link(v.tensor_scalar(turns[:, :, :], turns[:, :, :], 12582912.0, None, ALU.subtract))
                    c.link(v.scalar_tensor_tensor(angle[:, :, :], turns[:, :, :], -C1, angle[:, :, :], ALU.mult,
                                                  ALU.add))
                    c.link(v.scalar_tensor_tensor(angle[:, :, :], turns[:, :, :], -C2, angle[:, :, :], ALU.mult,
                                                  ALU.add))
                    v.scalar_tensor_tensor(angle[:, :, :], angle[:, :, :], -1.0, angle[:, :, :], ALU.mult, ALU.max
                                           ).then_inc(angle_made, 1)
                    v.wait_ge(attrs_in[s], 16 * (q + 1))
                    hold(v, feat_flipped, u)
                    v.tensor_copy(feat[:, :, 64:128], attrs[:, s, :].rearrange("p (t r) -> p t r", r=REC)[:, :, 0:64]
                                  ).then_inc(msg_copied, 1)
                    v.wait_ge(dst_spread, u + 1)
                    ra = rows[:, s, :, D:2 * D]
                    c.link(v.tensor_tensor(ra, ra, dst_b[:, :].rearrange("p (t c) -> p t c", c=D), ALU.add))
                    c.link(v.scalar_tensor_tensor(ra, ra, 0.0, we2[:, :].unsqueeze(1).to_broadcast([P, ST, D]),
                                                  ALU.max, ALU.mult))
                    hold(v, gate_made, u)
                    v.tensor_reduce(dot[:, :], ra, AX, ALU.add).then_inc(dot_made, 1)
                    v.wait_ge(gate_made, u + 1)
                    rh = rows[:, s, :, 0:D]
                    v.tensor_tensor(rh, rh, gate[:, :].unsqueeze(2).to_broadcast([P, ST, D]), ALU.mult
                                    ).then_inc(rows_weighted, 1)
                    bins = load_bins(v, g, u)
                    for k in range(GPS):
                        v.wait_ge(sums_made, GPS * u + k + 1)
                        acc = g.acc[:, bass.ds(bins[k], 1), 0:D].rearrange("p b c -> p (b c)")
                        v.tensor_tensor(acc, acc, sum_b, ALU.add).then_inc(sums_taken, 1)
                        v.wait_ge(sums_taken, GPS * u + k + 1)
                    c.end(L)
                one(0, 0)
                one(0, 1)
                with v.Fori(1, NSUPER // 2) as q:
                    one(q, 0)
                    one(q, 1)


class Shared:
    pass


def program(nc, a, out):
    ctx = ExitStack()
    with ctx:
        def sb(name, shape, dt=F32):
            return ctx.enter_context(nc.sbuf_tensor(name, shape, dt))

        def dram(name, shape, dt=F32):
            return nc.dram_tensor(name, shape, dt, kind="Internal").ap()

        counter = [0]

        def sem(name):
            counter[0] += 1
            return ctx.enter_context(nc.semaphore(f"{name}_{counter[0]}"))

        bank = [ctx.enter_context(nc.psum_tensor(f"bank{i}", [P, 1024], F32)) for i in range(4)]

        rec = dram("rec", [SLOTS, REC])
        bins_d = dram("bins_d", [NGROUPS])
        table0 = dram("table0", [NBINS * P * RELS, D + ZW])
        table1 = dram("table1", [NBINS * P, 2 * D + 1])
        table2 = dram("table2", [NBINS * P, ZW])
        table3 = dram("table3", [NBINS * P, D + ZW])
        edge_feat = dram("edge_feat", [P, NTILES * P])

        ident = sb("ident", [P, P])
        identb = sb("identb", [P, P], BF16)
        ones = sb("ones", [P, P])
        before = sb("before", [P, P])
        place1 = sb("place1", [P, P])
        place0 = sb("place0", [P, P])
        row = sb("row", [P, 1])
        sel = sb("sel", [P, HEADS, P], BF16)
        headmask = sb("headmask", [P, HEADS])
        x = sb("x", [P, NBINS, D])
        h = sb("h", [P, NBINS, D])
        acc = sb("acc", [P, NBINS, D + ZW])
        top = sb("top", [P, NBINS, HEADS])
        dst = sb("dst", [P, NBINS, D])
        src_idx = sb("src_idx", [P, NTILES], U32)
        rel_idx = sb("rel_idx", [P, NTILES], U32)
        places = sb("places", [P, NTILES + ST])
        rel_t = sb("rel_t", [P, NTILES])
        edge_score = sb("edge_score", [P, NTILES, HEADS])
        bin_row = sb("bin_row", [1, NGROUPS], I32)
        tw_mean = sb("tw_mean", [P, 1])

        with ExitStack() as ph:
            made, chain, counted = sem("iota_made"), sem("const_chain"), sem("x_loaded")
            c_i = ph.enter_context(nc.sbuf_tensor("c_i", [P, P], I32))
            r_i = ph.enter_context(nc.sbuf_tensor("r_i", [P, 1], I32))
            padded = sem("x_padded")
            k_i = ph.enter_context(nc.sbuf_tensor("k_i", [P, HEADS], I32))
            k_f = ph.enter_context(nc.sbuf_tensor("k_f", [P, HEADS], F32))
            with nc.Block() as block:
                @block.gpsimd
                def _(pool):
                    pool.iota(c_i[:, :], [[1, P]], base=0, channel_multiplier=0).then_inc(made, 1)
                    pool.iota(r_i[:, :], [[0, 1]], base=0, channel_multiplier=1).then_inc(made, 1)
                    pool.iota(k_i[:, :], [[-1, HEADS]], base=128, channel_multiplier=1).then_inc(made, 1)

                @block.sync
                def _(sp):
                    full = (NBINS - 1) * P
                    sp.dma_start(x[:, 0:NBINS - 1, :], a["x"][0:full, :].rearrange("(b p) c -> p b c", p=P)
                                 ).then_inc(counted, 16)
                    sp.wait_ge(padded, 1)
                    sp.dma_start(x[0:LAST, NBINS - 1, :], a["x"][full:NODES, :]).then_inc(counted, 16)
                    sp.wait_ge(counted, 32)

                @block.vector
                def _(v):
                    v.memset(x[:, NBINS - 1, :], 0.0).then_inc(padded, 1)
                    v.wait_ge(made, 3)
                    c = Chain(v, chain)
                    v.memset(ones[:, :], 1.0)
                    v.memset(places[:, NTILES:NTILES + ST], 0.0)
                    v.tensor_copy(row[:, :], r_i[:, :])
                    c.link(v.tensor_copy(place0[:, :], c_i[:, :]))
                    v.tensor_scalar(place1[:, :], place0[:, :], 1.0, None, ALU.add)
                    c.link(v.tensor_copy(k_f[:, :], k_i[:, :]))
                    v.tensor_scalar(ident[:, :], place0[:, :], row[:, 0:1], None, ALU.is_equal)
                    v.tensor_scalar(identb[:, :], place0[:, :], row[:, 0:1], None, ALU.is_equal)
                    v.tensor_scalar(before[:, :], place0[:, :], row[:, 0:1], None, ALU.is_gt)
                    c.link(v.memset(headmask[:, :], 0.0))
                    for j in range(HEADS):
                        v.memset(headmask[DH * j:DH * (j + 1), j:j + 1], 1.0)
                    parts = [ph.enter_context(nc.sbuf_tensor(f"part{n}", [P, HEADS], F32)) for n in range(3)]
                    for n in range(3):
                        ins = v.tensor_scalar(parts[n][:, :], k_f[:, :], 128.0 + HEADS * n, None, ALU.is_equal)
                    c.link(ins)
                    c.link(v.tensor_tensor(parts[0][:, :], parts[0][:, :], parts[1][:, :], ALU.add))
                    c.link(v.tensor_tensor(parts[0][:, :], parts[0][:, :], parts[2][:, :], ALU.add))
                    for j in range(HEADS):
                        ins = v.tensor_scalar(sel[:, j, :], ones[:, :], parts[0][:, j:j + 1], None, ALU.mult)
                    c.link(ins)

        with ExitStack() as ph:
            def tb(name, shape, dt=F32):
                return ph.enter_context(nc.sbuf_tensor(name, shape, dt))

            dst_i, bin_i = tb("dst_i", [EP, EC], I32), tb("bin_i", [EP, EC], I32)
            src_i, type_i = tb("src_i", [EP, EC], I32), tb("type_i", [EP, EC], I32)
            weight = tb("weight", [EP, EC])
            ebin, meta = tb("ebin", [EP, EC]), tb("meta", [EP, EC, 4])
            slot_u = tb("slot_u", [EP, EC], U32)
            hit = acc[:, :, :].rearrange("p b c -> p (b c)")[0:EP, 0:EC]
            run = acc[:, :, :].rearrange("p b c -> p (b c)")[0:EP, EC:2 * EC]
            slot = acc[:, :, :].rearrange("p b c -> p (b c)")[0:EP, 2 * EC:3 * EC]
            gain = acc[:, :, :].rearrange("p b c -> p (b c)")[0:EP, 3 * EC:4 * EC]
            zeros = h[:, :, :].rearrange("p b c -> p (b c)")
            counts, offs = tb("counts", [EP, NBINS]), tb("offs", [P, NBINS])
            total, ngr = tb("total", [P, NBINS]), tb("ngr", [P, NBINS])
            ngr_i, last = tb("ngr_i", [P, NBINS], I32), tb("last", [P, NBINS])
            wsum = tb("wsum", [P, 1])
            gnum = tb("gnum", [110, GPS])
            gcmp = tb("gcmp", [110, GPS, NBINS])
            gbin, gbin_i = tb("gbin", [110, GPS]), tb("gbin_i", [110, GPS], I32)
            gnum_i = tb("gnum_i", [110, GPS], I32)
            lists_in, zeroed, zeros_made = sem("lists_in"), sem("records_zeroed"), sem("zeros_made")
            chain, counted, summed = sem("sort_chain"), sem("counts_made"), sem("counts_summed")
            bins_out, bins_in, bins_ready, gnum_made = (sem("bins_out"), sem("bins_in"), sem("bins_ready"),
                                                       sem("group_numbers"))
            ZR = SLOTS * REC // P
            ZC = NBINS * D
            with nc.Block() as block:
                @block.sync
                def _(sp):
                    for k, (t, name) in enumerate([(dst_i, "dst"), (src_i, "src"), (type_i, "edge_type_16"),
                                                   (weight, "edge_weight")]):
                        sp.dma_start(t[:, :], a[name].rearrange("(p t) -> p t", p=EP)).then_inc(lists_in, 16)
                    sp.wait_ge(zeros_made, 1)
                    n = 0
                    flat = rec.rearrange("(p s) r -> p (s r)", p=P)
                    for at in range(0, ZR, ZC):
                        m = min(ZC, ZR - at)
                        sp.dma_start(flat[:, at:at + m], zeros[:, 0:m]).then_inc(zeroed, 16)
                        n += 1
                    sp.wait_ge(bins_ready, 1)
                    sp.dma_start(bins_d.bitcast(I32).rearrange("(p g) -> p g", p=110), gbin_i[:, :]
                                 ).then_inc(bins_out, 16)
                    sp.wait_ge(bins_out, 16)
                    sp.dma_start(bin_row[:, :], bins_d.bitcast(I32).unsqueeze(0)).then_inc(bins_in, 16)
                    sp.wait_ge(bins_in, 16)
                    sp.wait_ge(zeroed, 16 * n)

                @block.gpsimd
                def _(pool):
                    pool.iota(gnum_i[:, :], [[1, GPS]], base=0, channel_multiplier=GPS).then_inc(gnum_made, 1)

                @block.vector
                def _(v):
                    v.memset(zeros[:, :], 0.0).then_inc(zeros_made, 1)
                    v.wait_ge(lists_in, 64)
                    c = Chain(v, chain)
                    c.link(v.tensor_scalar(bin_i[:, :], dst_i[:, :], 7, None, ALU.arith_shift_right))
                    v.tensor_copy(ebin[:, :], bin_i[:, :])
                    v.tensor_copy(meta[:, :, 0], src_i[:, :])
                    v.tensor_copy(meta[:, :, 2], type_i[:, :])
                    v.tensor_copy(meta[:, :, 3], weight[:, :])
                    v.memset(slot, -1.0)
                    v.memset(wsum[:, :], 0.0)
                    c.link(v.tensor_scalar(hit, dst_i[:, :], 1.0, None, ALU.add))
                    c.link(v.scalar_tensor_tensor(meta[:, :, 1], ebin[:, :], -float(P), hit, ALU.mult, ALU.add))
                    c.link(v.tensor_reduce(wsum[0:EP, :], weight[:, :], AX, ALU.add))
                    first = c.n
                    with v.Fori(0, NBINS) as b:
                        d = Chain(v, chain, b * 2 + first)
                        d.link(v.tensor_scalar(hit, ebin[:, :], place0[0:EP, bass.ds(b, 1)], None, ALU.is_equal))
                        d.link(v.tensor_reduce(total[0:EP, 0:1], hit, AX, ALU.add))
                        v.tensor_scalar(counts[:, bass.ds(b, 1)], total[0:EP, 0:1], 1.0, None, ALU.mult
                                        ).then_inc(counted, 1)
                    v.wait_ge(summed, 1)
                    c = Chain(v, chain, first + 2 * NBINS)
                    v.tensor_scalar(tw_mean[:, :], bank[0][:, 512:513], 1.0 / EDGES, None, ALU.mult)
                    v.tensor_copy(offs[:, :], bank[0][:, 64:64 + NBINS])
                    c.link(v.tensor_scalar(ngr_i[:, :], bank[0][:, 0:NBINS], float(GE - 1), None, ALU.add))
                    c.link(v.tensor_scalar(ngr_i[:, :], ngr_i[:, :], 8, None, ALU.arith_shift_right))
                    c.link(v.tensor_copy(ngr[:, :], ngr_i[:, :]))
                    c.link(v.tensor_tensor_scan(last[:, :], ones[:, 0:NBINS], ngr[:, :], 0.0, ALU.mult, ALU.add))
                    c.link(v.tensor_tensor(ngr[:, :], last[:, :], ngr[:, :], ALU.subtract))
                    c.link(v.scalar_tensor_tensor(offs[:, :], ngr[:, :], float(GE), offs[:, :], ALU.mult, ALU.add))
                    v.wait_ge(gnum_made, 1)
                    c.link(v.tensor_copy(gnum[:, :], gnum_i[:, :]))
                    c.link(v.tensor_tensor(gcmp[:, :, :], last[0:110, :].unsqueeze(1).to_broadcast([110, GPS, NBINS]),
                                           gnum[:, :].unsqueeze(2).to_broadcast([110, GPS, NBINS]), ALU.is_le))
                    c.link(v.tensor_reduce(gbin[:, :], gcmp[:, :, :], AX, ALU.add))
                    v.tensor_scalar(gbin_i[:, :], gbin[:, :], float(NBINS - 1), None, ALU.min
                                    ).then_inc(bins_ready, 1)
                    second = first + 2 * NBINS + c.n
                    with v.Fori(0, NBINS) as b:
                        d = Chain(v, chain, b * 4 + second)
                        d.link(v.tensor_scalar(hit, ebin[:, :], place0[0:EP, bass.ds(b, 1)], None, ALU.is_equal))
                        d.link(v.tensor_tensor_scan(run, ones[0:EP, 0:1].to_broadcast([EP, EC]), hit, 0.0,
                                                    ALU.mult, ALU.add))
                        d.link(v.scalar_tensor_tensor(gain, run, offs[0:EP, bass.ds(b, 1)], hit, ALU.add, ALU.mult))
                        d.link(v.tensor_tensor(slot, slot, gain, ALU.add))
                    c = Chain(v, chain, second + 4 * NBINS)
                    c.link(v.tensor_copy(slot_u[:, :], slot))

                @block.tensor
                def _(pe):
                    pe.wait_ge(counted, NBINS)
                    pe.matmul(bank[0][:, 0:NBINS], ones[0:EP, :], counts[:, :], start=True, stop=True)
                    pe.matmul(bank[0][:, 64:64 + NBINS], before[0:EP, :], counts[:, :], start=True, stop=True)
                    pe.matmul(bank[0][:, 512:513], ones[:, :], wsum[:, :], start=True, stop=True).then_inc(summed, 1)

            CH = 16
            NCH = EC // CH
            spare = dst[:, :, :].rearrange("p b c -> p (b c)")
            at16, atr = 2 * CH * 64, 2 * CH * 80
            a64 = spare[0:EP, 0:at16].rearrange("p (s c) -> p s c", s=2)
            a16 = spare[0:EP, at16:atr].rearrange("p (s c) -> p s c", s=2)
            recs = spare[0:EP, atr:atr + 2 * CH * REC].rearrange("p (s c) -> p s c", s=2)
            slots = tb("slots", [EP, 2 * CH], U32)
            attrs_packed, meta_packed = sem("attrs_packed"), sem("meta_packed")
            attrs_in = [sem(f"attrs_in{s}") for s in range(2)]
            scattered = [sem(f"scattered{s}") for s in range(2)]
            v64 = a["edge_attr_64"].rearrange("(p t) c -> p (t c)", p=EP)
            v16 = a["edge_attr_16"].rearrange("(p t) c -> p (t c)", p=EP)
            with nc.Block() as block:
                @block.sync
                def _(sp):
                    def load(q, s):
                        k = q * 2 + s
                        hold(sp, attrs_packed, (k - 1) * 2)
                        sp.dma_start(a64[:, s, :], v64[:, bass.ds(k * CH * 64, CH * 64)]).then_inc(attrs_in[s], 16)
                        sp.dma_start(a16[:, s, :], v16[:, bass.ds(k * CH * 16, CH * 16)]).then_inc(attrs_in[s], 16)
                    load(0, 0)
                    load(0, 1)
                    with sp.Fori(1, NCH // 2) as q:
                        load(q, 0)
                        load(q, 1)

                @block.scalar
                def _(act):
                    def pack(q, s):
                        r = recs[:, s, :].rearrange("p (t r) -> p t r", r=REC)
                        act.wait_ge(attrs_in[s], q * 32 + 32)
                        hold(act, scattered[s], q * 16 * CH)
                        act.activation(r[:, :, 0:64], a64[:, s, :].rearrange("p (t c) -> p t c", c=64), ACT.Copy
                                       ).then_inc(attrs_packed, 1)
                        act.activation(r[:, :, 64:80], a16[:, s, :].rearrange("p (t c) -> p t c", c=16), ACT.Copy
                                       ).then_inc(attrs_packed, 1)
                    pack(0, 0)
                    pack(0, 1)
                    with act.Fori(1, NCH // 2) as q:
                        pack(q, 0)
                        pack(q, 1)

                @block.vector
                def _(v):
                    def pack(q, s):
                        k = q * 2 + s
                        r = recs[:, s, :].rearrange("p (t r) -> p t r", r=REC)
                        hold(v, scattered[s], q * 16 * CH)
                        v.tensor_scalar(r[:, :, 80:84], meta[:, bass.ds(k * CH, CH), :], 1.0, None, ALU.mult
                                        ).then_inc(meta_packed, 1)
                        v.tensor_tensor(slots[:, s * CH:(s + 1) * CH], slot_u[:, bass.ds(k * CH, CH)],
                                        slot_u[:, bass.ds(k * CH, CH)], ALU.max).then_inc(meta_packed, 1)
                    pack(0, 0)
                    pack(0, 1)
                    with v.Fori(1, NCH // 2) as q:
                        pack(q, 0)
                        pack(q, 1)

                @block.gpsimd
                def _(pool):
                    def scatter(q, s):
                        k = q * 2 + s
                        pool.wait_ge(attrs_packed, k * 2 + 2)
                        pool.wait_ge(meta_packed, k * 2 + 2)
                        park(pool)
                        for j in range(CH):
                            pool.indirect_dma_start(
                                out=rec, out_offset=bass.IndirectOffsetOnAxis(
                                    ap=slots[:, s * CH + j:s * CH + j + 1], axis=0),
                                in_=recs[:, s, j * REC:(j + 1) * REC], in_offset=None).then_inc(scattered[s], 16)
                    with pool.Fori(0, NCH // 2) as q:
                        scatter(q, 0)
                        scatter(q, 1)
                    for s in range(2):
                        pool.wait_ge(scattered[s], 16 * EC // 2)

        with ExitStack() as ph:
            def tb(name, shape, dt=F32):
                return ph.enter_context(nc.sbuf_tensor(name, shape, dt))
            CG = 10
            CT = CG * GT
            NCK = NGROUPS // CG
            buf = tb("buf", [P, 2, CT * REC])
            w_edge, att_e = tb("w_edge", [P, 16]), tb("att_e", [P, 1])
            wmask, wfold = tb("wmask", [P, HEADS, 16]), tb("wfold", [P, HEADS, 16])
            prod = tb("prod", [P, CT, HEADS, 16])
            records_in = [sem(f"records_in{s}") for s in range(2)]
            weights_in, taken, chain, folded, fold_made = (
                sem("weights_in"), sem("records_taken"), sem("fold_chain"), sem("folded"),
                sem("fold_made"))
            rv = rec.rearrange("(g p s) r -> p g (s r)", p=P, s=GT)
            with nc.Block() as block:
                @block.sync
                def _(sp):
                    sp.dma_start(w_edge[:, :], a["L2_gnn_W_edge"]).then_inc(weights_in, 16)
                    sp.dma_start(att_e[:, :], a["L2_gnn_att_edge"].rearrange("a h c -> (h c) a")).then_inc(weights_in, 16)

                    def load(q, s):
                        k = q * 2 + s
                        hold(sp, taken, k - 1)
                        sp.dma_start(buf[:, s, :].rearrange("p (g r) -> p g r", g=CG),
                                     rv[:, bass.ds(k * CG, CG), :]).then_inc(records_in[s], 16)
                    load(0, 0)
                    load(0, 1)
                    with sp.Fori(1, NCK // 2) as q:
                        load(q, 0)
                        load(q, 1)

                @block.tensor
                def _(pe):
                    pe.wait_ge(fold_made, 1)
                    pe.matmul(bank[0][:, 0:HEADS * 16], ones[:, :], wmask[:, :, :].rearrange("p h k -> p (h k)"),
                              start=True, stop=True).then_inc(folded, 1)

                @block.vector
                def _(v):
                    v.wait_ge(weights_in, 32)
                    c = Chain(v, chain)
                    c.link(v.tensor_tensor(wmask[:, :, :], w_edge[:, :].unsqueeze(1).to_broadcast([P, HEADS, 16]),
                                           headmask[:, :].unsqueeze(2).to_broadcast([P, HEADS, 16]), ALU.mult))
                    v.tensor_scalar(wmask[:, :, :], wmask[:, :, :], att_e[:, 0:1], None, ALU.mult
                                    ).then_inc(fold_made, 1)
                    v.wait_ge(folded, 1)
                    c.link(v.tensor_copy(wfold[:, :, :], bank[0][:, 0:HEADS * 16].rearrange("p (h k) -> p h k", k=16)))

                    def take(q, s):
                        k = q * 2 + s
                        r = buf[:, s, :].rearrange("p (t r) -> p t r", r=REC)
                        at = bass.ds(k * CT, CT)
                        v.wait_ge(records_in[s], q * 16 + 16)
                        hold(v, taken, k)
                        d = Chain(v, chain, k + 2)
                        v.tensor_scalar(src_idx[:, at], r[:, :, 80], 1.0, None, ALU.mult)
                        v.scalar_tensor_tensor(rel_idx[:, at], r[:, :, 80], float(RELS), r[:, :, 82], ALU.mult, ALU.add)
                        v.tensor_scalar(places[:, at], r[:, :, PLACE], 1.0, None, ALU.mult)
                        v.tensor_scalar(rel_t[:, at], r[:, :, 83], 1.0, None, ALU.mult)
                        d.link(v.tensor_tensor(prod[:, :, :, :], r[:, :, 64:80].unsqueeze(2).to_broadcast([P, CT, HEADS, 16]),
                                               wfold[:, :, :].unsqueeze(1).to_broadcast([P, CT, HEADS, 16]), ALU.mult))
                        park(v)
                        v.tensor_reduce(edge_score[:, at, :], prod[:, :, :, :], AX, ALU.add).then_inc(taken, 1)
                    take(0, 0)
                    take(0, 1)
                    with v.Fori(1, NCK // 2) as q:
                        take(q, 0)
                        take(q, 1)

        g = Shared()
        g.nc, g.a, g.out, g.sem, g.bank, g.rec, g.edge_feat = nc, a, out, sem, bank, rec, edge_feat
        g.table0, g.table1, g.table2, g.table3 = table0, table1, table2, table3
        g.ident, g.identb, g.place1, g.sel = ident, identb, place1, sel
        g.x, g.h, g.acc, g.top, g.dst = x, h, acc, top, dst
        g.places, g.rel_t, g.edge_score, g.bin_row, g.tw_mean = places, rel_t, edge_score, bin_row, tw_mean
        g.src_idx, g.seen = src_idx, [0] * RING
        g.gathered = [sem(f"gathered{s}") for s in range(RING)]
        for layer in range(3):
            attention_sources(g, f"source0{layer}", h if layer else x, a["L0_gnn_W_gat"][layer], False,
                              a["L0_gnn_attn_l"][layer].rearrange("h c -> (h c)"),
                              a["L0_gnn_attn_r"][layer].rearrange("h c -> (h c)"), layer)
            attention_edges(g, f"edges0{layer}", table0, rel_idx)
            relational_close(g, layer)
        gated_sources(g)
        gated_edges(g)
        gated_close(g)
        attention_sources(g, "source2", x, a["L2_gnn_W_lin"], True,
                          a["L2_gnn_att_dst"].rearrange("a h c -> (a h c)"),
                          a["L2_gnn_att_src"].rearrange("a h c -> (a h c)"))
        attention_edges(g, "edges2", table2, src_idx, scored_edges=True)
        edge_attention_close(g)
        conv_sources(g, 1, x)
        attention_edges(g, "edges31", table3, src_idx, conv=1)
        conv_close(g, last=False)
        conv_sources(g, 2, h)
        attention_edges(g, "edges32", table3, src_idx, conv=2)
        conv_close(g, last=True)


INPUTS = ["x", "src", "dst", "edge_attr_16", "edge_attr_64", "edge_type_16", "edge_weight", "node_vec"]
INPUTS += ["L0_gnn_" + n for n in ("W_rel", "b_rel", "W_loop", "W_gat", "attn_l", "attn_r", "b_gat", "W_fuse",
                                   "b_fuse", "W_gate", "b_gate")]
INPUTS += ["L1_gnn_" + n for n in ("W1", "b1", "g1", "bt1", "We1", "be1", "We2", "be2", "Wg", "bg", "g2", "bt2")]
INPUTS += ["L2_gnn_" + n for n in ("W_lin", "W_edge", "att_src", "att_dst", "att_edge", "bias", "ln_gamma",
                                   "ln_beta")]
INPUTS += ["L3_gnn_Wt", "L3_gnn_bt"]
INPUTS += [f"L3_gnn_{n}{k}" for k in (1, 2) for n in ("Wq", "bq", "Wk", "bk", "Wv", "bv", "We", "Wskip", "bskip")]


def kernel(**inputs):
    import numpy as np
    import concourse.bacc as bacc
    from concourse.bass_utils import run_bass_kernel_spmd

    nc = bacc.Bacc("TRN2", target_bir_lowering=False, num_devices=1)
    arrays, aps = {}, {}
    for name in INPUTS:
        arr = np.ascontiguousarray(inputs[name])
        arrays["in_" + name] = arr
        aps[name] = nc.dram_tensor("in_" + name, arr.shape, mybir.dt.from_np(arr.dtype), kind="ExternalInput").ap()
    out = nc.dram_tensor("out", (NODES, D), F32, kind="ExternalOutput").ap()
    program(nc, aps, out)
    got = run_bass_kernel_spmd(nc, [arrays], core_ids=[0])
    return got.results[0]["out"]
```

```python
from contextlib import ExitStack

import concourse.bass as bass
from concourse import mybir

F32 = mybir.dt.float32
BF16 = mybir.dt.bfloat16
I32 = mybir.dt.int32
U32 = mybir.dt.uint32
ALU = mybir.AluOpType
ACT = mybir.ActivationFunctionType
AX = mybir.AxisListType.X

P = 128
NODES, EDGES, D = 6250, 100000, 128
RELS, HEADS, DH = 16, 4, 32
NBINS = -(-NODES // P)
LAST = NODES - (NBINS - 1) * P
NB = 7
NSTEPS = NBINS // NB
EP = 125
EC = EDGES // EP
GT = 2
GE = GT * P
GPS = 4
ST = GPS * GT
NGROUPS = (EDGES + NBINS * (GE - 1)) // GE
NSUPER = -(-NGROUPS // GPS)
NGROUPS = NSUPER * GPS
NTILES = NGROUPS * GT
SLOTS = NTILES * P
RING = 4
REC = 64 + 16 + 4
SOURCE, PLACE, TYPE, WEIGHT = 80, 81, 82, 83
HZ = DH + 1
ZW = HEADS * HZ
BIG = 1e30
LN_EPS = 1e-5
TWO_PI = 6.283185307179586


class Chain:

    def __init__(self, engine, sem, start=0):
        self.engine, self.sem, self.start, self.n = engine, sem, start, 0

    def link(self, ins):
        ins.then_inc(self.sem, 1)
        self.n += 1
        self.engine.wait_ge(self.sem, self.start + self.n)

    def later(self, ins):
        ins.then_inc(self.sem, 1)
        self.n += 1

    def catch_up(self):
        if self.n:
            self.engine.wait_ge(self.sem, self.start + self.n)

    def end(self, per):
        assert self.n == per, self.n


def hold(engine, sem, value):
    if not isinstance(value, int) or value > 0:
        engine.wait_ge(sem, value)


def park(engine):
    engine.nop(nofuse=True)



def steps(engine, count, step):
    step(0)
    with engine.Fori(1, count) as t:
        step(t)


def bins_of(t):
    return bass.ds(t * NB, NB)


def flat(tile):
    return tile[:, :, :].rearrange("p b c -> p (b c)")


def heads_of(tile):
    return tile.rearrange("p b (h c) -> p b h c", h=HEADS)


def over_bins(vec):
    return vec[:, :].unsqueeze(1).to_broadcast([P, NB, D])


def load_row(sp, tile, vec, loaded):
    sp.dma_start(tile[:, :], vec.partition_broadcast(P)).then_inc(loaded, 16)


class Pass:

    def __init__(self, g, name):
        self.g, self.stack, self.name = g, ExitStack(), name
        self.used = []

    def __enter__(self):
        return self

    def __exit__(self, failed, *_):
        if failed:
            return
        with self.g.nc.Block() as block:
            @block.gpsimd
            def _(pool):
                for used in self.used:
                    pool.sem_clear(used)
        self.stack.close()

    def buffer(self, name, shape=(P, NB, D), dt=F32):
        return self.stack.enter_context(self.g.nc.sbuf_tensor(f"{self.name}_{name}", list(shape), dt))

    def gathers_before(self, slots=RING):
        before = list(self.g.seen)
        for u in range(NSUPER):
            self.g.seen[u % slots] += 16 * ST
        return before

    def semaphore(self, name):
        self.used.append(self.stack.enter_context(self.g.nc.semaphore(f"{self.name}_{name}")))
        return self.used[-1]


def flip(pe, g, src, tile_ready, ready, flipped):
    pe.wait_ge(tile_ready, ready)
    for j in range(NB):
        ins = pe.transpose(g.bank[0][:, j * D:(j + 1) * D], src[:, j, :], g.ident[:, :])
    ins.then_inc(flipped, 1)


def keep_flipped(act, g, dst, flipped, value, kept):
    act.wait_ge(flipped, value)
    act.activation(flat(dst), g.bank[0][:, 0:NB * D], ACT.Copy).then_inc(kept, 1)


def product(pe, g, bank, pairs, made):
    for j in range(NB):
        for n, (tT, w) in enumerate(pairs):
            ins = pe.matmul(g.bank[bank][:, j * D:(j + 1) * D], tT[:, j, :], w,
                            start=n == 0, stop=n == len(pairs) - 1)
    ins.then_inc(made, 1)


def bank_tiles(g, n):
    return g.bank[n][:, 0:NB * D].rearrange("p (b c) -> p b c", c=D)


def normalise(v, c, tile, square, stat, variance_ready, deviation_ready, value):
    def wide(col):
        return stat[:, col, :].unsqueeze(2).to_broadcast([P, NB, D])
    c.link(v.tensor_reduce(stat[:, 0, :], tile[:, :, :], AX, ALU.add))
    c.link(v.tensor_scalar(stat[:, 0, :], stat[:, 0, :], 1.0 / D, None, ALU.mult))
    c.link(v.tensor_tensor(tile[:, :, :], tile[:, :, :], wide(0), ALU.subtract))
    c.link(v.tensor_tensor(square[:, :, :], tile[:, :, :], tile[:, :, :], ALU.mult))
    c.link(v.tensor_reduce(stat[:, 1, :], square[:, :, :], AX, ALU.add))
    v.tensor_scalar(stat[:, 1, :], stat[:, 1, :], 1.0 / D, LN_EPS, ALU.mult, ALU.add).then_inc(variance_ready, 1)
    v.wait_ge(deviation_ready, value)
    c.link(v.reciprocal(stat[:, 3, :], stat[:, 2, :]))
    c.link(v.tensor_tensor(tile[:, :, :], tile[:, :, :], wide(3), ALU.mult))


NORM_LINKS = 7


def deviation(act, stat, variance_ready, value, deviation_ready):
    act.wait_ge(variance_ready, value)
    act.activation(stat[:, 2, :], stat[:, 1, :], ACT.Sqrt).then_inc(deviation_ready, 1)


def attended(v, c, g, t, tile, denom):
    z = g.acc[:, bins_of(t), D:D + ZW].rearrange("p b (h z) -> p b h z", h=HEADS)
    c.link(v.tensor_scalar(denom[:, :, :], z[:, :, :, DH], 1e-16, None, ALU.add))
    c.link(v.reciprocal(denom[:, :, :], denom[:, :, :]))
    c.link(v.tensor_tensor(heads_of(tile[:, :, :]), z[:, :, :, 0:DH],
                           denom[:, :, :].unsqueeze(3).to_broadcast([P, NB, HEADS, DH]), ALU.mult))


ATTENDED_LINKS = 3


def node_scores(v, c, zrow, prod, weights, out):
    z = zrow[:, :, :].rearrange("p b (h z) -> p b h z", h=HEADS)[:, :, :, 0:DH]
    w = weights[:, :].rearrange("p (h c) -> p h c", h=HEADS).unsqueeze(1).to_broadcast([P, NB, HEADS, DH])
    c.link(v.tensor_tensor(heads_of(prod[:, :, :]), z, w, ALU.mult))
    return v.tensor_reduce(out, heads_of(prod[:, :, :]), AX, ALU.add)


def dst_parts(g):
    return g.dst[:, :, :].rearrange("p b c -> p (b c)").bitcast(BF16).rearrange("p (b c) -> p b c", c=2 * D)


def clear_sums(v, c, g):
    v.memset(g.acc[:, :, :].rearrange("p b c -> p (b c)"), 0.0)
    c.link(v.memset(g.top[:, :, :].rearrange("p b h -> p (b h)"), -BIG))


def attention_sources(g, name, inp, w_z, flip_w, w_src, w_dst, layer=None):
    a, nc = g.a, g.nc
    rel = layer is not None
    with Pass(g, name) as p:
        wz_in, wz = p.buffer("wz_in", (P, D)), p.buffer("wz", (P, D))
        asrc, adst = p.buffer("asrc", (P, D)), p.buffer("adst", (P, D))
        cur, curT, prod = p.buffer("cur"), p.buffer("curT"), p.buffer("prod")
        zrow, er = p.buffer("zrow", (P, NB, ZW)), p.buffer("er", (P, NB, HEADS))
        if rel:
            w_rel, w_loop = p.buffer("w_rel", (P, RELS, D)), p.buffer("w_loop", (P, D))
            b_rel, relbuf = p.buffer("b_rel", (P, D)), p.buffer("relbuf", (P, 2, RELS * D))
        loaded, wflip, wkept = p.semaphore("weights_in"), p.semaphore("weight_flipped"), p.semaphore("weight_kept")
        tile_ready, flipped, kept = p.semaphore("tile_ready"), p.semaphore("flipped"), p.semaphore("kept")
        z_made, z_kept, rows_ready = p.semaphore("z_made"), p.semaphore("z_kept"), p.semaphore("rows_ready")
        dst_kept, rows_out, chain = p.semaphore("dst_kept"), p.semaphore("rows_out"), p.semaphore("chain")
        loop_made, loop_kept = p.semaphore("loop_made"), p.semaphore("loop_kept")
        rel_made, even_kept, odd_kept = p.semaphore("rel_made"), p.semaphore("even_kept"), p.semaphore("odd_kept")
        rel_out = [p.semaphore(f"rel_out{s}") for s in range(2)]
        uses = [NB - NB // 2, NB // 2]
        n_loads = 16 * (6 if rel else 3)
        zv = zrow[:, :, :].rearrange("p b (h z) -> p b h z", h=HEADS)

        def slot_free(engine, t, j):
            hold(engine, rel_out[j % 2], (t * uses[j % 2] + j // 2) * 16)

        with nc.Block() as block:
            @block.sync
            def _(sp):
                sp.dma_start(wz_in[:, :], w_z).then_inc(loaded, 16)
                load_row(sp, asrc, w_src, loaded)
                load_row(sp, adst, w_dst, loaded)
                if rel:
                    sp.dma_start(w_rel[:, :, :], a["L0_gnn_W_rel"][layer].rearrange("r d o -> d r o")
                                 ).then_inc(loaded, 16)
                    sp.dma_start(w_loop[:, :], a["L0_gnn_W_loop"][layer]).then_inc(loaded, 16)
                    load_row(sp, b_rel, a["L0_gnn_b_rel"][layer], loaded)
                if rel:
                    tab = g.table0.rearrange("(b p r) c -> p b r c", p=P, r=RELS)
                else:
                    tab = g.table2.rearrange("(b p) c -> p b c", p=P)

                def step(t):
                    sp.wait_ge(rows_ready, t + 1)
                    park(sp)
                    if not rel:
                        sp.dma_start(tab[:, bins_of(t), :], zrow[:, :, :]).then_inc(rows_out, 16)
                        return
                    for j in range(NB):
                        sp.dma_start(tab[:, bass.ds(t * NB + j, 1), :, D:D + ZW].rearrange("p b r c -> p (b r) c"),
                                     zrow[:, j, :].unsqueeze(1).to_broadcast([P, RELS, ZW])).then_inc(rows_out, 16)
                    for j in range(NB):
                        sp.wait_ge(even_kept, t * NB + j + 1)
                        park(sp)
                        sp.wait_ge(odd_kept, t * NB + j + 1)
                        park(sp)
                        sp.dma_start(tab[:, bass.ds(t * NB + j, 1), :, 0:D].rearrange("p b r c -> p (b r) c"),
                                     relbuf[:, j % 2, :].rearrange("p (r c) -> p r c", r=RELS)
                                     ).then_inc(rel_out[j % 2], 16)
                steps(sp, NSTEPS, step)
                sp.wait_ge(rows_out, 16 * (NBINS if rel else NSTEPS))
                if rel:
                    for s in range(2):
                        sp.wait_ge(rel_out[s], 16 * NSTEPS * uses[s])

            @block.tensor
            def _(pe):
                pe.wait_ge(loaded, n_loads)
                weight = wz_in
                if flip_w:
                    pe.transpose(g.bank[1][:, 0:D], wz_in[:, :], g.ident[:, :]).then_inc(wflip, 1)
                    pe.wait_ge(wkept, 1)
                    weight = wz

                def step(t):
                    if rel:
                        hold(pe, loop_kept, t)
                    else:
                        hold(pe, kept, t)
                    flip(pe, g, cur, tile_ready, t + 1, flipped)
                    pe.wait_ge(kept, t + 1)
                    hold(pe, z_kept, t)
                    product(pe, g, 1, [(curT, weight[:, :])], z_made)
                    if not rel:
                        return
                    product(pe, g, 0, [(curT, w_loop[:, :])], loop_made)
                    for j in range(NB):
                        for half in range(2):
                            hold(pe, odd_kept if half else even_kept, t * NB + j)
                            for q in range(2):
                                r = half * 8 + q * 4
                                ins = pe.matmul(g.bank[2 + half][:, q * 512:(q + 1) * 512], curT[:, j, :],
                                                w_rel[:, r:r + 4, :].rearrange("p r c -> p (r c)"),
                                                start=True, stop=True)
                            ins.then_inc(rel_made, 1)
                steps(pe, NSTEPS, step)

            @block.scalar
            def _(act):
                if flip_w:
                    act.wait_ge(wflip, 1)
                    act.activation(wz[:, :], g.bank[1][:, 0:D], ACT.Copy).then_inc(wkept, 1)

                def step(t):
                    hold(act, rel_made if rel else z_made, t * (2 * NB if rel else 1))
                    keep_flipped(act, g, curT, flipped, t + 1, kept)
                    act.wait_ge(z_made, t + 1)
                    hold(act, dst_kept, t)
                    hold(act, rows_out, 16 * t * (NB if rel else 1))
                    act.activation(zv[:, :, :, 0:DH].rearrange("p b h z -> p (b h) z"),
                                   g.bank[1][:, 0:NB * D].rearrange("p (k z) -> p k z", z=DH), ACT.Copy
                                   ).then_inc(z_kept, 1)
                    if rel:
                        for j in range(NB):
                            act.wait_ge(rel_made, t * 2 * NB + 2 * j + 1)
                            slot_free(act, t, j)
                            act.activation(relbuf[:, j % 2, 0:1024], g.bank[2][:, :], ACT.Copy
                                           ).then_inc(even_kept, 1)
                steps(act, NSTEPS, step)

            @block.vector
            def _(v):
                c = Chain(v, chain)
                clear_sums(v, c, g)
                v.wait_ge(loaded, n_loads)
                PER = 6

                def step(t):
                    d = Chain(v, chain, t * PER + 1)
                    hold(v, flipped, t)
                    v.tensor_scalar(cur[:, :, :], inp[:, bins_of(t), :], 1.0, None, ALU.mult).then_inc(tile_ready, 1)
                    v.wait_ge(z_kept, t + 1)
                    hold(v, dst_kept, t)
                    ins = node_scores(v, d, zrow, prod, asrc, zv[:, :, :, DH])
                    ins.then_inc(rows_ready, 1)
                    v.wait_ge(rows_ready, t + 1)
                    d.link(node_scores(v, d, zrow, prod, adst, er[:, :, :]))
                    part = [dst_parts(g)[:, bins_of(t), 0:3 * HEADS].rearrange("p b (h k) -> p b h k", k=3)[:, :, :, k]
                            for k in range(3)]
                    d.link(v.tensor_scalar(part[0], er[:, :, :], 1.0, None, ALU.mult))
                    d.link(v.tensor_tensor(er[:, :, :], er[:, :, :], part[0], ALU.subtract))
                    d.link(v.tensor_scalar(part[1], er[:, :, :], 1.0, None, ALU.mult))
                    v.tensor_tensor(part[2], er[:, :, :], part[1], ALU.subtract).then_inc(dst_kept, 1)
                    d.end(PER)
                    if rel:
                        v.wait_ge(loop_made, t + 1)
                        v.tensor_tensor(g.acc[:, bins_of(t), 0:D], bank_tiles(g, 0), over_bins(b_rel), ALU.add
                                        ).then_inc(loop_kept, 1)
                        for j in range(NB):
                            v.wait_ge(rel_made, t * 2 * NB + 2 * j + 2)
                            slot_free(v, t, j)
                            v.tensor_copy(relbuf[:, j % 2, 1024:2048], g.bank[3][:, :]).then_inc(odd_kept, 1)
                steps(v, NSTEPS, step)


def relational_close(g, layer):
    a, nc = g.a, g.nc
    gated, last = layer == 0, layer == 2
    with Pass(g, f"close0{layer}") as p:
        w_fuse, b_gat, b_fuse = p.buffer("w_fuse", (P, 2, D)), p.buffer("b_gat", (P, D)), p.buffer("b_fuse", (P, D))
        w_gate, b_gate, w_tw = p.buffer("w_gate", (P, D)), p.buffer("b_gate", (P, D)), p.buffer("w_tw", (P, D))
        rel, gat, hc = p.buffer("rel"), p.buffer("gat"), p.buffer("hc")
        relT, gatT, denom = p.buffer("relT"), p.buffer("gatT"), p.buffer("denom", (P, NB, HEADS))
        stat, square = p.buffer("stat", (P, 4, NB)), p.buffer("square")
        loaded, tile_ready, flipped, kept = (p.semaphore("weights_in"), p.semaphore("tile_ready"), p.semaphore("flipped"),
                                             p.semaphore("kept"))
        made, gate_in, gate_made, chain = (p.semaphore("product_made"), p.semaphore("gate_in"), p.semaphore("gate_made"),
                                           p.semaphore("chain"))
        hc_kept = p.semaphore("hc_kept")
        variance_ready, deviation_ready = p.semaphore("variance_ready"), p.semaphore("deviation_ready")
        F = 3 if gated else 2
        M = 2 if gated else 1
        with nc.Block() as block:
            @block.sync
            def _(sp):
                sp.dma_start(w_fuse[:, :, :], a["L0_gnn_W_fuse"].rearrange("(k p) c -> p k c", k=2)
                             ).then_inc(loaded, 16)
                load_row(sp, b_gat, a["L0_gnn_b_gat"][layer], loaded)
                load_row(sp, b_fuse, a["L0_gnn_b_fuse"], loaded)
                sp.dma_start(w_gate[:, :], a["L0_gnn_W_gate"][0:D, :]).then_inc(loaded, 16)
                load_row(sp, w_tw, a["L0_gnn_W_gate"][D, :], loaded)
                load_row(sp, b_gate, a["L0_gnn_b_gate"], loaded)
                sp.wait_ge(loaded, 96)

            @block.tensor
            def _(pe):
                pe.wait_ge(loaded, 96)

                def step(t):
                    hold(pe, kept, F * t)
                    flip(pe, g, rel, tile_ready, 2 * t + 1, flipped)
                    pe.wait_ge(kept, F * t + 1)
                    flip(pe, g, gat, tile_ready, 2 * t + 2, flipped)
                    pe.wait_ge(kept, F * t + 2)
                    hold(pe, hc_kept, t)
                    product(pe, g, 1, [(relT, w_fuse[:, 0, :]), (gatT, w_fuse[:, 1, :])], made)
                    if gated:
                        flip(pe, g, hc, hc_kept, t + 1, flipped)
                        pe.wait_ge(kept, F * t + 3)
                        hold(pe, gate_in, t)
                        product(pe, g, 2, [(relT, w_gate[:, :])], made)
                steps(pe, NSTEPS, step)

            @block.scalar
            def _(act):
                def step(t):
                    hold(act, made, M * t)
                    keep_flipped(act, g, relT, flipped, F * t + 1, kept)
                    keep_flipped(act, g, gatT, flipped, F * t + 2, kept)
                    if gated:
                        act.wait_ge(made, M * t + 1)
                        keep_flipped(act, g, relT, flipped, F * t + 3, kept)
                        act.wait_ge(gate_in, t + 1)
                        act.activation(flat(gat), flat(rel), ACT.Sigmoid).then_inc(gate_made, 1)
                    if last:
                        deviation(act, stat, variance_ready, t + 1, deviation_ready)
                steps(act, NSTEPS, step)

            @block.vector
            def _(v):
                v.wait_ge(loaded, 96)
                c = Chain(v, chain)
                c.link(v.scalar_tensor_tensor(b_gate[:, :], w_tw[:, :], g.tw_mean[:, 0:1], b_gate[:, :],
                                              ALU.mult, ALU.add))
                PER = ATTENDED_LINKS + (2 + NORM_LINKS if last else 1) + (1 if gated else 0)

                def step(t):
                    d = Chain(v, chain, t * PER + 1)
                    hold(v, flipped, F * t)
                    v.tensor_scalar(rel[:, :, :], g.acc[:, bins_of(t), 0:D], 1.0, None, ALU.mult
                                    ).then_inc(tile_ready, 1)
                    attended(v, d, g, t, gat, denom)
                    v.tensor_tensor(gat[:, :, :], gat[:, :, :], over_bins(b_gat), ALU.add).then_inc(tile_ready, 1)
                    v.wait_ge(made, M * t + 1)
                    v.tensor_tensor(hc[:, :, :], bank_tiles(g, 1), over_bins(b_fuse), ALU.add
                                    ).then_inc(hc_kept, 1)
                    v.wait_ge(hc_kept, t + 1)
                    if gated:
                        v.wait_ge(made, M * t + 2)
                        v.tensor_tensor(rel[:, :, :], bank_tiles(g, 2), over_bins(b_gate), ALU.add
                                        ).then_inc(gate_in, 1)
                        v.wait_ge(gate_made, t + 1)
                        d.link(v.tensor_tensor(hc[:, :, :], hc[:, :, :], gat[:, :, :], ALU.mult))
                    if last:
                        d.link(v.scalar_tensor_tensor(hc[:, :, :], hc[:, :, :], 0.0, g.x[:, bins_of(t), :],
                                                      ALU.max, ALU.add))
                        normalise(v, d, hc, square, stat, variance_ready, deviation_ready, t + 1)
                        d.link(v.tensor_scalar(g.x[:, bins_of(t), :], hc[:, :, :], 1.0, None, ALU.mult))
                    else:
                        d.link(v.tensor_scalar(g.h[:, bins_of(t), :], hc[:, :, :], 0.0, None, ALU.max))
                    d.end(PER)
                steps(v, NSTEPS, step)


def gated_sources(g):
    a, nc = g.a, g.nc
    with Pass(g, "source1") as p:
        w1, we1 = p.buffer("w1", (P, D)), p.buffer("we1", (P, 2, D))
        b1, g1, bt1, be1 = (p.buffer(n, (P, D)) for n in ("b1", "g1", "bt1", "be1"))
        nv = p.buffer("nv", (P, NBINS))
        cur, curT, square, stat = p.buffer("cur"), p.buffer("curT"), p.buffer("square"), p.buffer("stat", (P, 4, NB))
        hc, row = p.buffer("hc"), p.buffer("row", (P, NB, 2 * D + 1))
        loaded, nv_zero, tile_ready, flipped, kept = (p.semaphore("weights_in"), p.semaphore("node_vec_cleared"),
                                                      p.semaphore("tile_ready"), p.semaphore("flipped"), p.semaphore("kept"))
        made, bank_read, rows_ready, rows_out, chain = (p.semaphore("product_made"), p.semaphore("product_read"),
                                                        p.semaphore("rows_ready"), p.semaphore("rows_out"),
                                                        p.semaphore("chain"))
        a_kept, h_ready = p.semaphore("a_kept"), p.semaphore("h_ready")
        variance_ready, deviation_ready = p.semaphore("variance_ready"), p.semaphore("deviation_ready")
        with nc.Block() as block:
            @block.sync
            def _(sp):
                sp.dma_start(w1[:, :], a["L1_gnn_W1"]).then_inc(loaded, 16)
                sp.dma_start(we1[:, :, :], a["L1_gnn_We1"].rearrange("(k p) c -> p k c", k=2)).then_inc(loaded, 16)
                for tile, n in ((b1, "b1"), (g1, "g1"), (bt1, "bt1"), (be1, "be1")):
                    load_row(sp, tile, a["L1_gnn_" + n], loaded)
                full = (NBINS - 1) * P
                sp.wait_ge(nv_zero, 1)
                sp.dma_start(nv[:, 0:NBINS - 1], a["node_vec"][0:full].rearrange("(b p) -> p b", p=P),
                             allow_slow_non_contiguous=True).then_inc(loaded, 16)
                sp.dma_start(nv[0:LAST, NBINS - 1:NBINS], a["node_vec"][full:NODES].unsqueeze(1)
                             ).then_inc(loaded, 16)
                tab = g.table1.rearrange("(b p) c -> p b c", p=P)

                def step(t):
                    sp.wait_ge(rows_ready, t + 1)
                    park(sp)
                    sp.wait_ge(a_kept, t + 1)
                    park(sp)
                    sp.dma_start(tab[:, bins_of(t), :], row[:, :, :]).then_inc(rows_out, 16)
                steps(sp, NSTEPS, step)
                sp.wait_ge(rows_out, 16 * NSTEPS)

            @block.tensor
            def _(pe):
                pe.wait_ge(loaded, 128)

                def step(t):
                    hold(pe, kept, 2 * t)
                    flip(pe, g, cur, tile_ready, t + 1, flipped)
                    pe.wait_ge(kept, 2 * t + 1)
                    hold(pe, bank_read, 2 * t)
                    product(pe, g, 1, [(curT, w1[:, :])], made)
                    flip(pe, g, hc, h_ready, t + 1, flipped)
                    pe.wait_ge(kept, 2 * t + 2)
                    hold(pe, a_kept, t)
                    product(pe, g, 2, [(curT, we1[:, 0, :])], made)
                    product(pe, g, 3, [(curT, we1[:, 1, :])], made)
                steps(pe, NSTEPS, step)

            @block.scalar
            def _(act):
                def step(t):
                    hold(act, made, 3 * t)
                    keep_flipped(act, g, curT, flipped, 2 * t + 1, kept)
                    deviation(act, stat, variance_ready, t + 1, deviation_ready)
                    act.wait_ge(made, 3 * t + 1)
                    keep_flipped(act, g, curT, flipped, 2 * t + 2, kept)
                    act.wait_ge(made, 3 * t + 2)
                    hold(act, rows_out, 16 * t)
                    act.activation(row[:, :, D:2 * D], bank_tiles(g, 2), ACT.Copy).then_inc(a_kept, 1)
                steps(act, NSTEPS, step)

            @block.vector
            def _(v):
                v.memset(nv[:, :], 0.0).then_inc(nv_zero, 1)
                c = Chain(v, chain)
                clear_sums(v, c, g)
                v.wait_ge(loaded, 128)
                PER = NORM_LINKS + 4

                def step(t):
                    d = Chain(v, chain, t * PER + 1)
                    hold(v, flipped, 2 * t)
                    v.tensor_scalar(cur[:, :, :], g.x[:, bins_of(t), :], 1.0, None, ALU.mult).then_inc(tile_ready, 1)
                    v.wait_ge(made, 3 * t + 1)
                    v.tensor_tensor(hc[:, :, :], bank_tiles(g, 1), over_bins(b1), ALU.add).then_inc(bank_read, 1)
                    v.wait_ge(bank_read, 2 * t + 1)
                    normalise(v, d, hc, square, stat, variance_ready, deviation_ready, t + 1)
                    d.link(v.tensor_tensor(hc[:, :, :], hc[:, :, :], over_bins(g1), ALU.mult))
                    d.link(v.tensor_tensor(hc[:, :, :], hc[:, :, :], over_bins(bt1), ALU.add))
                    v.tensor_scalar(hc[:, :, :], hc[:, :, :], 0.0, None, ALU.max).then_inc(h_ready, 1)
                    v.wait_ge(h_ready, t + 1)
                    d.link(v.tensor_scalar(g.h[:, bins_of(t), :], hc[:, :, :], 1.0, None, ALU.mult))
                    hold(v, rows_out, 16 * t)
                    v.tensor_copy(row[:, :, 0:D], hc[:, :, :])
                    v.tensor_tensor(row[:, :, 2 * D], nv[:, bins_of(t)], nv[:, bins_of(t)], ALU.max
                                    ).then_inc(rows_ready, 1)
                    v.wait_ge(made, 3 * t + 3)
                    d.link(v.tensor_tensor(square[:, :, :], bank_tiles(g, 3), over_bins(be1), ALU.add))
                    v.tensor_scalar(g.dst[:, bins_of(t), :], square[:, :, :], 1.0, None, ALU.mult
                                    ).then_inc(bank_read, 1)
                    v.wait_ge(bank_read, 2 * t + 2)
                    d.end(PER)
                steps(v, NSTEPS, step)


def gated_close(g):
    a, nc = g.a, g.nc
    with Pass(g, "close1") as p:
        wg = p.buffer("wg", (P, 2, D))
        bg, g2, bt2 = (p.buffer(n, (P, D)) for n in ("bg", "g2", "bt2"))
        hc, ag, hT, aT = p.buffer("hc"), p.buffer("ag"), p.buffer("hT"), p.buffer("aT")
        gin, gate, square, stat = p.buffer("gin"), p.buffer("gate"), p.buffer("square"), p.buffer("stat", (P, 4, NB))
        loaded, tile_ready, flipped, kept = (p.semaphore("weights_in"), p.semaphore("tile_ready"), p.semaphore("flipped"),
                                             p.semaphore("kept"))
        made, gate_in, gate_made, chain = (p.semaphore("product_made"), p.semaphore("gate_in"), p.semaphore("gate_made"),
                                           p.semaphore("chain"))
        variance_ready, deviation_ready = p.semaphore("variance_ready"), p.semaphore("deviation_ready")
        with nc.Block() as block:
            @block.sync
            def _(sp):
                sp.dma_start(wg[:, :, :], a["L1_gnn_Wg"].rearrange("(k p) c -> p k c", k=2)).then_inc(loaded, 16)
                for tile, n in ((bg, "bg"), (g2, "g2"), (bt2, "bt2")):
                    load_row(sp, tile, a["L1_gnn_" + n], loaded)
                sp.wait_ge(loaded, 64)

            @block.tensor
            def _(pe):
                pe.wait_ge(loaded, 64)

                def step(t):
                    hold(pe, kept, 2 * t)
                    flip(pe, g, hc, tile_ready, 2 * t + 1, flipped)
                    pe.wait_ge(kept, 2 * t + 1)
                    flip(pe, g, ag, tile_ready, 2 * t + 2, flipped)
                    pe.wait_ge(kept, 2 * t + 2)
                    hold(pe, gate_in, t)
                    product(pe, g, 1, [(hT, wg[:, 0, :]), (aT, wg[:, 1, :])], made)
                steps(pe, NSTEPS, step)

            @block.scalar
            def _(act):
                def step(t):
                    hold(act, made, t)
                    keep_flipped(act, g, hT, flipped, 2 * t + 1, kept)
                    keep_flipped(act, g, aT, flipped, 2 * t + 2, kept)
                    act.wait_ge(gate_in, t + 1)
                    act.activation(flat(gate), flat(gin), ACT.Sigmoid).then_inc(gate_made, 1)
                    deviation(act, stat, variance_ready, 2 * t + 1, deviation_ready)
                    deviation(act, stat, variance_ready, 2 * t + 2, deviation_ready)
                steps(act, NSTEPS, step)

            @block.vector
            def _(v):
                v.wait_ge(loaded, 64)
                PER = 2 * NORM_LINKS + 7

                def step(t):
                    d = Chain(v, chain, t * PER)
                    hold(v, flipped, 2 * t)
                    v.tensor_scalar(hc[:, :, :], g.h[:, bins_of(t), :], 1.0, None, ALU.mult).then_inc(tile_ready, 1)
                    v.tensor_scalar(ag[:, :, :], plain_sums(g)[:, bins_of(t), :], 1.0, None, ALU.mult
                                    ).then_inc(tile_ready, 1)
                    v.wait_ge(made, t + 1)
                    v.tensor_tensor(gin[:, :, :], bank_tiles(g, 1), over_bins(bg), ALU.add).then_inc(gate_in, 1)
                    v.wait_ge(gate_made, t + 1)
                    d.link(v.tensor_tensor(ag[:, :, :], ag[:, :, :], hc[:, :, :], ALU.subtract))
                    d.link(v.tensor_tensor(ag[:, :, :], ag[:, :, :], gate[:, :, :], ALU.mult))
                    d.link(v.tensor_tensor(ag[:, :, :], ag[:, :, :], hc[:, :, :], ALU.add))
                    normalise(v, d, ag, square, stat, variance_ready, deviation_ready, 2 * t + 1)
                    d.link(v.tensor_tensor(ag[:, :, :], ag[:, :, :], over_bins(g2), ALU.mult))
                    d.link(v.tensor_tensor(ag[:, :, :], ag[:, :, :], over_bins(bt2), ALU.add))
                    d.link(v.tensor_tensor(ag[:, :, :], ag[:, :, :], g.x[:, bins_of(t), :], ALU.add))
                    normalise(v, d, ag, square, stat, variance_ready, deviation_ready, 2 * t + 2)
                    d.link(v.tensor_scalar(g.x[:, bins_of(t), :], ag[:, :, :], 1.0, None, ALU.mult))
                    d.end(PER)
                steps(v, NSTEPS, step)


def edge_attention_close(g):
    a, nc = g.a, g.nc
    with Pass(g, "close2") as p:
        bias, gamma, beta = (p.buffer(n, (P, D)) for n in ("bias", "gamma", "beta"))
        y, low, square, stat = p.buffer("y"), p.buffer("low"), p.buffer("square"), p.buffer("stat", (P, 4, NB))
        denom = p.buffer("denom", (P, NB, HEADS))
        loaded, low_ready, low_made, chain = (p.semaphore("weights_in"), p.semaphore("low_ready"), p.semaphore("low_made"),
                                              p.semaphore("chain"))
        variance_ready, deviation_ready = p.semaphore("variance_ready"), p.semaphore("deviation_ready")
        with nc.Block() as block:
            @block.sync
            def _(sp):
                for tile, n in ((bias, "bias"), (gamma, "ln_gamma"), (beta, "ln_beta")):
                    load_row(sp, tile, a["L2_gnn_" + n], loaded)
                sp.wait_ge(loaded, 48)

            @block.scalar
            def _(act):
                def step(t):
                    deviation(act, stat, variance_ready, 2 * t + 1, deviation_ready)
                    act.wait_ge(low_ready, t + 1)
                    act.activation(flat(low), flat(low), ACT.Exp).then_inc(low_made, 1)
                    deviation(act, stat, variance_ready, 2 * t + 2, deviation_ready)
                steps(act, NSTEPS, step)

            @block.vector
            def _(v):
                v.wait_ge(loaded, 48)
                PER = ATTENDED_LINKS + 2 * NORM_LINKS + 8

                def step(t):
                    d = Chain(v, chain, t * PER)
                    attended(v, d, g, t, y, denom)
                    d.link(v.tensor_tensor(y[:, :, :], y[:, :, :], over_bins(bias), ALU.add))
                    d.link(v.tensor_tensor(y[:, :, :], y[:, :, :], g.x[:, bins_of(t), :], ALU.add))
                    normalise(v, d, y, square, stat, variance_ready, deviation_ready, 2 * t + 1)
                    d.link(v.tensor_tensor(y[:, :, :], y[:, :, :], over_bins(gamma), ALU.mult))
                    d.link(v.tensor_tensor(y[:, :, :], y[:, :, :], over_bins(beta), ALU.add))
                    v.tensor_scalar(low[:, :, :], y[:, :, :], 0.0, None, ALU.min).then_inc(low_ready, 1)
                    d.link(v.tensor_scalar(y[:, :, :], y[:, :, :], 0.0, -1.0, ALU.max, ALU.add))
                    v.wait_ge(low_made, t + 1)
                    d.link(v.tensor_tensor(y[:, :, :], y[:, :, :], low[:, :, :], ALU.add))
                    d.link(v.tensor_tensor(y[:, :, :], y[:, :, :], g.x[:, bins_of(t), :], ALU.add))
                    normalise(v, d, y, square, stat, variance_ready, deviation_ready, 2 * t + 2)
                    d.link(v.tensor_scalar(g.x[:, bins_of(t), :], y[:, :, :], 1.0, None, ALU.mult))
                    d.end(PER)
                steps(v, NSTEPS, step)


def conv_sources(g, k, inp):
    a, nc = g.a, g.nc
    with Pass(g, f"source3{k}") as p:
        names = ("q", "k", "v", "skip")
        w = {n: p.buffer("w" + n, (P, D)) for n in names}
        b = {n: p.buffer("b" + n, (P, D)) for n in names}
        cur, curT, qs, row = p.buffer("cur"), p.buffer("curT"), p.buffer("qs"), p.buffer("row", (P, NB, D + ZW))
        loaded, tile_ready, flipped, kept = (p.semaphore("weights_in"), p.semaphore("tile_ready"), p.semaphore("flipped"),
                                             p.semaphore("kept"))
        made, taken, rows_ready, rows_out, chain = (p.semaphore("product_made"), p.semaphore("products_taken"),
                                                    p.semaphore("rows_ready"), p.semaphore("rows_out"), p.semaphore("chain"))
        with nc.Block() as block:
            @block.sync
            def _(sp):
                for n in names:
                    sp.dma_start(w[n][:, :], a[f"L3_gnn_W{n}{k}"]).then_inc(loaded, 16)
                    load_row(sp, b[n], a[f"L3_gnn_b{n}{k}"], loaded)
                tab = g.table3.rearrange("(b p) c -> p b c", p=P)

                def step(t):
                    sp.wait_ge(rows_ready, t + 1)
                    park(sp)
                    sp.dma_start(tab[:, bins_of(t), :], row[:, :, :]).then_inc(rows_out, 16)
                steps(sp, NSTEPS, step)
                sp.wait_ge(rows_out, 16 * NSTEPS)

            @block.tensor
            def _(pe):
                pe.wait_ge(loaded, 128)

                def step(t):
                    hold(pe, taken, t)
                    flip(pe, g, cur, tile_ready, t + 1, flipped)
                    pe.wait_ge(kept, t + 1)
                    for bank, n in ((1, "k"), (2, "v"), (3, "q"), (0, "skip")):
                        product(pe, g, bank, [(curT, w[n][:, :])], made)
                steps(pe, NSTEPS, step)

            @block.scalar
            def _(act):
                def step(t):
                    hold(act, made, 4 * t)
                    keep_flipped(act, g, curT, flipped, t + 1, kept)
                steps(act, NSTEPS, step)

            @block.vector
            def _(v):
                c = Chain(v, chain)
                clear_sums(v, c, g)
                c.link(v.memset(row[:, :, :].rearrange("p b c -> p (b c)"), 0.0))
                v.wait_ge(loaded, 128)
                PER = 1
                rz = row[:, :, D:D + ZW].rearrange("p b (h z) -> p b h z", h=HEADS)[:, :, :, 0:DH]
                bv = b["v"][:, :].rearrange("p (h c) -> p h c", h=HEADS).unsqueeze(1).to_broadcast([P, NB, HEADS, DH])

                def step(t):
                    d = Chain(v, chain, t * PER + 2)
                    hold(v, flipped, t)
                    v.tensor_scalar(cur[:, :, :], inp[:, bins_of(t), :], 1.0, None, ALU.mult).then_inc(tile_ready, 1)
                    v.wait_ge(made, 4 * t + 2)
                    hold(v, rows_out, 16 * t)
                    v.tensor_tensor(row[:, :, 0:D], bank_tiles(g, 1), over_bins(b["k"]), ALU.add)
                    v.tensor_tensor(rz, heads_of(bank_tiles(g, 2)), bv, ALU.add).then_inc(rows_ready, 1)
                    v.wait_ge(made, 4 * t + 3)
                    hold(v, taken, t)
                    d.link(v.tensor_tensor(qs[:, :, :], bank_tiles(g, 3), over_bins(b["q"]), ALU.add))
                    v.tensor_scalar(g.dst[:, bins_of(t), :], qs[:, :, :], float(DH) ** -0.5, None, ALU.mult)
                    v.wait_ge(made, 4 * t + 4)
                    v.tensor_tensor(g.acc[:, bins_of(t), 0:D], bank_tiles(g, 0), over_bins(b["skip"]), ALU.add
                                    ).then_inc(taken, 1)
                    d.end(PER)
                steps(v, NSTEPS, step)


def conv_close(g, last):
    nc = g.nc
    with Pass(g, f"close3{int(last)}") as p:
        y, square, stat = p.buffer("y"), p.buffer("square"), p.buffer("stat", (P, 4, NB))
        denom = p.buffer("denom", (P, NB, HEADS))
        chain, variance_ready, deviation_ready = (p.semaphore("chain"), p.semaphore("variance_ready"),
                                                  p.semaphore("deviation_ready"))
        written = p.semaphore("result_written")
        PER = ATTENDED_LINKS + (3 + NORM_LINKS if last else 1)
        with nc.Block() as block:
            if last:
                @block.scalar
                def _(act):
                    steps(act, NSTEPS, lambda t: deviation(act, stat, variance_ready, t + 1, deviation_ready))

                @block.sync
                def _(sp):
                    sp.wait_ge(chain, NSTEPS * PER)
                    full = (NBINS - 1) * P
                    sp.dma_start(g.out[0:full, :].rearrange("(b p) c -> p b c", p=P), g.x[:, 0:NBINS - 1, :]
                                 ).then_inc(written, 16)
                    sp.dma_start(g.out[full:NODES, :], g.x[0:LAST, NBINS - 1, :]).then_inc(written, 16)
                    sp.wait_ge(written, 32)

            @block.vector
            def _(v):
                def step(t):
                    d = Chain(v, chain, t * PER)
                    attended(v, d, g, t, y, denom)
                    skip = g.acc[:, bins_of(t), 0:D]
                    if last:
                        d.link(v.tensor_tensor(y[:, :, :], y[:, :, :], skip, ALU.add))
                        d.link(v.tensor_tensor(y[:, :, :], y[:, :, :], g.x[:, bins_of(t), :], ALU.add))
                        normalise(v, d, y, square, stat, variance_ready, deviation_ready, t + 1)
                        d.link(v.tensor_scalar(g.x[:, bins_of(t), :], y[:, :, :], 1.0, None, ALU.mult))
                    else:
                        d.link(v.tensor_tensor(g.h[:, bins_of(t), :], y[:, :, :], skip, ALU.add))
                    d.end(PER)
                steps(v, NSTEPS, step)



def superblocks(engine, step):
    def full(q, s):
        n, m = s + 2, s + 1
        step((q + n // RING, n % RING), (q + m // RING, m % RING), (q, s))
    step((0, 0), None, None)
    step((0, 1), (0, 0), None)
    for s in range(RING):
        full(0, s)
    with engine.Fori(1, (NSUPER - 2) // RING) as q:
        for s in range(RING):
            full(q, s)
    end = (NSUPER - 2) // RING
    step(None, (end, 1), (end, 0))
    step(None, None, (end, 1))


def superblock_pairs(engine, step):
    step((0, 0), None)
    for s in range(RING):
        step(after((0, s)), (0, s))
    full = (NSUPER - 1) // RING
    with engine.Fori(1, full) as q:
        for s in range(RING):
            step(after((q, s)), (q, s))
    for s in range(NSUPER - 1 - RING * full):
        step(after((full, s)), (full, s))
    step(None, (full, NSUPER - 1 - RING * full))


def number(qs):
    return qs[0] * RING + qs[1]


def after(qs):
    return (qs[0] + (qs[1] + 1) // RING, (qs[1] + 1) % RING)


def tiles_of(u):
    return bass.ds(u * ST, ST)


def load_bin(engine, g, u, k):
    return engine.value_load(g.bin_row[0:1, bass.ds(u * GPS + k, 1)], min_val=0, max_val=NBINS - 1)


def load_bins(engine, g, u):
    return [load_bin(engine, g, u, k) for k in range(GPS)]


def make_onehot(v, g, u, onehot, onehot_made):
    v.tensor_tensor(onehot[:, :, :], g.place1[:, :].unsqueeze(1).to_broadcast([P, ST, P]),
                    g.places[:, tiles_of(u)].unsqueeze(2).to_broadcast([P, ST, P]), ALU.is_equal
                    ).then_inc(onehot_made, 1)


def gather_rows(pool, g, table, index, ring, rows, ring_kept, sums_made, gathered):
    def one(q, s):
        u = q * len(rows) + s
        hold(pool, sums_made, GPS * (u - len(rows) + 1))
        hold(pool, ring_kept, u)
        park(pool)
        pool.tensor_copy(ring[:, s * ST:(s + 1) * ST], index[:, tiles_of(u)]).then_inc(ring_kept, 1)
        pool.wait_ge(ring_kept, u + 1)
        park(pool)
        for j in range(ST):
            pool.indirect_dma_start(out=rows[s][:, j, :], out_offset=None, in_=table,
                                    in_offset=bass.IndirectOffsetOnAxis(ap=ring[:, s * ST + j:s * ST + j + 1], axis=0)
                                    ).then_inc(gathered[s], 16)
    for s in range(len(rows)):
        one(0, s)
    with pool.Fori(1, NSUPER // len(rows)) as q:
        for s in range(len(rows)):
            one(q, s)
    for s in range(NSUPER % len(rows)):
        one(NSUPER // len(rows), s)


def attention_edges(g, name, table, index, scored_edges=False, conv=None):
    a, nc = g.a, g.nc
    Z = 0 if scored_edges else D
    W = Z + ZW
    A0 = 0 if conv is None and not scored_edges else Z
    ACC0 = D - Z + A0
    with Pass(g, name) as p:
        spare = g.h[:, :, :].rearrange("p b c -> p (b c)")
        rows = [spare[:, s * ST * W:(s + 1) * ST * W].rearrange("p (t c) -> p t c", c=W) for s in range(RING - 1)]
        rows.append(p.buffer("rows3", (P, ST, W))[:, :, :])
        ring = p.buffer("ring", (P, RING * ST), U32)
        onehot = [p.buffer(f"onehot{s}", (P, ST, P)) for s in range(RING)]
        flippedT = [p.buffer(f"onehotT{s}", (P, ST, P), BF16) for s in range(2)]
        if conv is None:
            narrow = p.buffer("narrow_onehot", (P, ST, P), BF16)
            narrow_made = p.semaphore("narrow_made")
        else:
            wideT = [p.buffer(f"wideT{s}", (P, ST, P)) for s in range(2)]
        maskT = [p.buffer(f"maskT{s}", (P, ST, P), BF16) for s in range(2)]
        parts = p.buffer("parts", (P, ST, P), BF16)
        partsT = [p.buffer(f"partsT{s}", (P, ST, P), BF16) for s in range(2)]
        score = [p.buffer(f"score{s}", (P, ST, HEADS)) for s in range(2)]
        rest = p.buffer("rest", (P, ST, HEADS))
        arg, weight = p.buffer("arg", (P, ST, HEADS)), p.buffer("weight", (P, ST, HEADS))
        gmax, newmax, fall, max_rest = (p.buffer(n, (P, GPS, HEADS)) for n in ("gmax", "newmax", "fall", "max_rest"))
        max_parts = p.buffer("max_parts", (P, GPS, HEADS, 3), BF16)
        spread = p.buffer("spread", (P, ST, HEADS))
        rate = [p.buffer(f"rate{s}", (P, GPS, HEADS)) for s in range(2)]
        gathered, seen = g.gathered, p.gathers_before()
        (ring_kept, onehot_made, onehot_flipped, flipped_kept, dst_spread, parts_made, parts_flipped, parts_kept,
         scores_spread, group_scanned, max_made, max_spread, arg_made, weight_made, rate_made, rows_weighted,
         sums_made, sums_taken, chain, cleared) = (p.semaphore(n) for n in (
             "ring_kept", "onehot_made", "onehot_flipped", "flipped_kept", "dst_spread", "parts_made",
             "parts_flipped", "parts_kept", "scores_spread", "group_scanned", "max_made", "max_spread", "arg_made",
             "weight_made", "rate_made", "rows_weighted", "sums_made", "sums_taken", "chain", "cleared"))
        if conv is not None:
            w_e = p.buffer("w_e", (P, D))
            feat = g.edge_score[:, :, :].rearrange("p t h -> p (t h)")[:, 0:2 * ST * P].rearrange(
                "p (s c) -> p s c", s=2)
            feat_in = [p.semaphore(f"feat_in{s}") for s in range(2)]
            w_in, half_ready, half_taken = p.semaphore("w_in"), p.semaphore("half_ready"), p.semaphore("half_taken")
        flip_b = g.bank[0]
        narrow_b, partsT_b = flip_b[:, 0:512].bitcast(BF16), flip_b[:, 512:1024].bitcast(BF16)
        spread_b = [g.bank[1], g.bank[2]]
        sum_b = [g.bank[3][:, 512:512 + W - A0], g.bank[3][:, 3 * ST * HEADS:3 * ST * HEADS + W - A0]]
        dst_b, max_b = flip_b[:, 512:512 + 3 * ST * HEADS], g.bank[3][:, 0:3 * ST * HEADS]
        KEPT = 2 if conv is None else 3

        def add_parts(v, bank):
            return v.tensor_reduce(spread[:, :, :].rearrange("p t h -> p (t h)"),
                                   bank.rearrange("p (b k) -> p b k", k=3), AX, ALU.add)

        def zrows(s):
            return rows[s][:, :, Z:Z + ZW].rearrange("p b (h z) -> p b h z", h=HEADS)

        with nc.Block() as block:
            @block.gpsimd
            def _(pool):
                gather_rows(pool, g, table, index, ring, rows, ring_kept, sums_made, gathered)

            if conv is not None:
                @block.sync
                def _(sp):
                    sp.dma_start(w_e[:, :], a[f"L3_gnn_We{conv}"]).then_inc(w_in, 16)

                    def load(q, s):
                        u = q * 2 + s
                        hold(sp, half_ready, 2 * (u - 1))
                        park(sp)
                        sp.dma_start(feat[:, s, :], g.edge_feat[:, bass.ds(u * (ST * P), ST * P)]
                                     ).then_inc(feat_in[s], 16)
                    load(0, 0)
                    load(0, 1)
                    with sp.Fori(1, NSUPER // 2) as q:
                        load(q, 0)
                        load(q, 1)

            @block.tensor
            def _(pe):
                if conv is not None:
                    pe.wait_ge(w_in, 16)

                def flip_onehot(n):
                    u, s = number(n), n[1]
                    if conv is None:
                        pe.wait_ge(narrow_made, u + 1)
                        hold(pe, flipped_kept, KEPT * u)
                        for j in range(ST):
                            ins = pe.transpose(narrow_b[:, j * P:(j + 1) * P], narrow[:, j, :], g.identb[:, :])
                    else:
                        pe.wait_ge(onehot_made, u + 1)
                        hold(pe, parts_kept, u)
                        for j in range(ST):
                            ins = pe.transpose(flip_b[:, j * P:(j + 1) * P], onehot[s][:, j, :], g.ident[:, :])
                    ins.then_inc(onehot_flipped, 1)

                def spread_dst(n, bins):
                    u, s = number(n), n[1] % 2
                    pe.wait_ge(flipped_kept, KEPT * (u + 1))
                    hold(pe, parts_kept, u)
                    for j in range(ST):
                        ins = pe.matmul(dst_b[:, j * 3 * HEADS:(j + 1) * 3 * HEADS], flippedT[s][:, j, :],
                                        dst_parts(g)[:, bass.ds(bins[j // GT], 1), 0:3 * HEADS]
                                        .rearrange("p b c -> p (b c)"), start=True, stop=True)
                    ins.then_inc(dst_spread, 1)

                def spread_half(n, half, bins):
                    u, s = number(n), n[1] % 2
                    if half == 0:
                        pe.wait_ge(flipped_kept, KEPT * u + 1)
                        pe.wait_ge(feat_in[s], 16 * (n[0] * (RING // 2) + (n[1] // 2 + 1)))
                    hold(pe, half_taken, 2 * u + half)
                    for j in range(ST // 2):
                        tile = half * (ST // 2) + j
                        pe.matmul(flip_b[:, j * P:(j + 1) * P], wideT[s][:, tile, :],
                                  g.dst[:, bass.ds(bins[tile // GT], 1), :].rearrange("p b c -> p (b c)"),
                                  start=True, stop=True)
                        ins = pe.matmul(flip_b[:, 512 + j * P:512 + (j + 1) * P],
                                        feat[:, s, tile * P:(tile + 1) * P], w_e[:, :], start=True, stop=True)
                    ins.then_inc(half_ready, 1)

                def flip_parts(n):
                    u, s = number(n), n[1] % 2
                    pe.wait_ge(parts_made, u + 1)
                    for j in range(ST):
                        ins = pe.transpose(partsT_b[:, j * P:(j + 1) * P], parts[:, j, :], g.identb[:, :])
                    ins.then_inc(parts_flipped, 1)

                def spread_scores(m, k):
                    u, s = number(m), m[1] % 2
                    if k == 0:
                        pe.wait_ge(parts_kept, u + 1)
                    hold(pe, group_scanned, GPS * u + k - 1)
                    b = spread_b[k % 2]
                    mask = maskT[s][:, k * GT:(k + 1) * GT, :].rearrange("p t c -> p (t c)")
                    partT = partsT[s][:, k * GT:(k + 1) * GT, :].rearrange("p t c -> p (t c)")
                    for half in range(2):
                        pe.matmul(b[:, half * 512:(half + 1) * 512], g.identb[:, :],
                                  mask.unsqueeze(1).to_broadcast([P, 2, GE]), start=True, stop=False,
                                  skip_group_check=True)
                        for hh in range(2):
                            at = half * 512 + hh * GE
                            ins = pe.matmul(b[:, at:at + GE], g.sel[:, half * 2 + hh, :], partT, start=False,
                                            stop=True, skip_group_check=True)
                    ins.then_inc(scores_spread, 1)

                def spread_max(m):
                    u, s = number(m), m[1] % 2
                    pe.wait_ge(max_made, u + 1)
                    hold(pe, arg_made, u)
                    for j in range(ST):
                        ins = pe.matmul(max_b[:, j * 3 * HEADS:(j + 1) * 3 * HEADS], flippedT[s][:, j, :],
                                        max_parts[:, j // GT, :, :].rearrange("p h k -> p (h k)"),
                                        start=True, stop=True)
                    ins.then_inc(max_spread, 1)

                def sum_group(o, k):
                    u, s = number(o), o[1]
                    if k == 0:
                        pe.wait_ge(rows_weighted, u + 1)
                    hold(pe, sums_taken, GPS * u + k - 1)
                    for j in range(k * GT, (k + 1) * GT):
                        ins = pe.matmul(sum_b[k % 2], onehot[s][:, j, :], rows[s][:, j, A0:W],
                                        start=j == k * GT, stop=j == (k + 1) * GT - 1)
                    ins.then_inc(sums_made, 1)

                def step(n, m, o):
                    bins = []
                    if m:
                        spread_scores(m, 0)
                    if n:
                        bins.append(load_bin(pe, g, number(n), 0))
                    if m:
                        spread_scores(m, 1)
                    if n:
                        bins.append(load_bin(pe, g, number(n), 1))
                        flip_onehot(n)
                        bins.append(load_bin(pe, g, number(n), 2))
                    if o:
                        sum_group(o, 0)
                    if n:
                        bins.append(load_bin(pe, g, number(n), 3))
                    if m:
                        spread_scores(m, 2)
                    if n and conv is not None:
                        spread_half(n, 0, bins)
                    if o:
                        sum_group(o, 1)
                    if m:
                        spread_scores(m, 3)
                    if n and conv is None:
                        spread_dst(n, bins)
                    if n and conv is not None:
                        spread_half(n, 1, bins)
                    if o:
                        sum_group(o, 2)
                        sum_group(o, 3)
                    if n:
                        flip_parts(n)
                    if m:
                        spread_max(m)
                superblocks(pe, step)

            @block.scalar
            def _(act):
                def narrow_ahead(n):
                    act.wait_ge(onehot_made, number(n) + 1)
                    hold(act, onehot_flipped, number(n))
                    act.activation(narrow[:, :, :].rearrange("p t c -> p (t c)"),
                                   onehot[n[1]][:, :, :].rearrange("p t c -> p (t c)"), ACT.Copy
                                   ).then_inc(narrow_made, 1)

                def step(n, m, o):
                    if n:
                        u, s = number(n), n[1] % 2
                        act.wait_ge(onehot_flipped, u + 1)
                        hold(act, max_spread, u - 1)
                        onehotT = narrow_b[:, :]
                        if conv is not None:
                            onehotT = wideT[s][:, :, :].rearrange("p t c -> p (t c)")
                            act.activation(onehotT, flip_b[:, :], ACT.Copy).then_inc(flipped_kept, 1)
                            act.wait_ge(flipped_kept, KEPT * u + 1)
                        act.activation(flippedT[s][:, :, :].rearrange("p t c -> p (t c)"), onehotT, ACT.Copy
                                       ).then_inc(flipped_kept, 1)
                        hold(act, scores_spread, GPS * (u - 1))
                        act.activation(maskT[s][:, :, :].rearrange("p t c -> p (t c)"), onehotT, ACT.Copy,
                                       bias=-BIG, scale=BIG).then_inc(flipped_kept, 1)
                    if n:
                        u, s = number(n), n[1] % 2
                        act.wait_ge(parts_flipped, u + 1)
                        act.activation(partsT[s][:, :, :].rearrange("p t c -> p (t c)"), partsT_b[:, :], ACT.Copy
                                       ).then_inc(parts_kept, 1)
                    if m:
                        u, s = number(m), m[1] % 2
                        act.wait_ge(max_made, u + 1)
                        hold(act, sums_taken, GPS * (u - 1))
                        act.activation(rate[s][:, :, :].rearrange("p k h -> p (k h)"),
                                       fall[:, :, :].rearrange("p k h -> p (k h)"), ACT.Exp).then_inc(rate_made, 1)
                        act.wait_ge(arg_made, u + 1)
                        act.activation(weight[:, :, :].rearrange("p k h -> p (k h)"),
                                       arg[:, :, :].rearrange("p k h -> p (k h)"), ACT.Exp).then_inc(weight_made, 1)
                    if n and conv is None:
                        narrow_ahead(after(n))
                if conv is None:
                    narrow_ahead((0, 0))
                superblocks(act, step)

            @block.vector
            def _(v):
                v.memset(parts[:, :, :].rearrange("p t c -> p (t c)"), 0.0).then_inc(cleared, 1)
                v.wait_ge(cleared, 1)
                LA = (4 if scored_edges else 3) + 3
                LB = 2 * GPS + 6
                LC = GPS

                def onehot_ahead(n):
                    hold(v, sums_made, GPS * (number(n) - RING + 1))
                    make_onehot(v, g, number(n), onehot[n[1]], onehot_made)

                def convolve_half(n, half, c):
                    u, s = number(n), n[1]
                    if half == 0:
                        v.wait_ge(gathered[s], seen[s] + 16 * ST * (n[0] + 1))
                    tiles = slice(half * (ST // 2), (half + 1) * (ST // 2))
                    v.wait_ge(half_ready, 2 * u + half + 1)
                    e = flip_b[:, 512:1024].rearrange("p (t c) -> p t c", c=D)
                    qd = flip_b[:, 0:512].rearrange("p (t c) -> p t c", c=D)
                    kr = rows[s][:, tiles, 0:D]
                    zr = zrows(s)[:, tiles, :, 0:DH]
                    v.tensor_tensor(zr, zr, e.rearrange("p t (h c) -> p t h c", h=HEADS), ALU.add)
                    c.link(v.tensor_tensor(kr, kr, e, ALU.add))
                    v.tensor_tensor(kr, kr, qd, ALU.mult).then_inc(half_taken, 1)

                def scores_and_maxima(n, m, c, bins):
                    if n:
                        u, s = number(n), n[1]
                        sc = score[s % 2][:, :, :]
                        if conv is None:
                            v.wait_ge(gathered[s], seen[s] + 16 * ST * (n[0] + 1))
                            v.wait_ge(dst_spread, u + 1)
                            c.later(add_parts(v, dst_b))
                        else:
                            v.wait_ge(half_taken, 2 * u + 2)
                    if m:
                        write_max(1, c, bins)
                    c.catch_up()
                    if n and conv is None:
                        c.later(v.tensor_tensor(sc, zrows(s)[:, :, :, DH], spread[:, :, :], ALU.add))
                    if m:
                        read_max(m, 2, c, bins)
                    c.catch_up()
                    if n and scored_edges:
                        c.link(v.tensor_tensor(sc, sc, g.edge_score[:, tiles_of(u), :], ALU.add))
                    if n and conv is None:
                        c.later(v.scalar_tensor_tensor(sc, sc, 0.2, sc, ALU.mult, ALU.max))
                    elif n:
                        c.later(v.tensor_reduce(sc, rows[s][:, :, 0:D].rearrange("p t (h c) -> p t h c", h=HEADS),
                                                AX, ALU.add))
                    if m:
                        write_max(2, c, bins)
                    c.catch_up()
                    if n:
                        hold(v, parts_flipped, u)
                        c.later(v.tensor_copy(parts[:, :, 0:4], sc))
                    if m:
                        read_max(m, 3, c, bins)
                    c.catch_up()
                    if n:
                        c.later(v.tensor_tensor(rest[:, :, :], sc, parts[:, :, 0:4], ALU.subtract))
                    if m:
                        write_max(3, c, bins)
                    c.catch_up()
                    if n:
                        c.later(v.tensor_copy(parts[:, :, 4:8], rest[:, :, :]))
                    if m:
                        split_max(m, 0, c)
                    c.catch_up()
                    if n:
                        v.tensor_tensor(parts[:, :, 8:12], rest[:, :, :], parts[:, :, 4:8], ALU.subtract
                                        ).then_inc(parts_made, 1)
                    if m:
                        split_max(m, 1, c)
                    c.catch_up()
                    if n:
                        v.wait_ge(parts_made, u + 1)

                def scan_group(m, k):
                    u = number(m)
                    v.wait_ge(scores_spread, GPS * u + k + 1)
                    v.tensor_reduce(gmax[:, k, :], spread_b[k % 2][:, :].rearrange("p (h e) -> p h e", h=HEADS),
                                    AX, ALU.max).then_inc(group_scanned, 1)

                def read_max(m, k, c, bins):
                    u = number(m)
                    v.wait_ge(group_scanned, GPS * u + k + 1)
                    if k == 0:
                        hold(v, rate_made, u)
                    now = g.top[:, bass.ds(bins[k], 1), :].rearrange("p b h -> p (b h)")
                    v.tensor_tensor(newmax[:, k, :], now, gmax[:, k, :], ALU.max)
                    c.later(v.tensor_tensor(fall[:, k, :], now, now, ALU.max))

                def write_max(k, c, bins):
                    now = g.top[:, bass.ds(bins[k], 1), :].rearrange("p b h -> p (b h)")
                    c.later(v.tensor_tensor(now, newmax[:, k, :], newmax[:, k, :], ALU.max))

                def split_max(m, part, c):
                    if part == 0:
                        hold(v, max_spread, number(m))
                        c.later(v.tensor_copy(max_parts[:, :, :, 0], newmax[:, :, :]))
                    elif part == 1:
                        c.later(v.tensor_tensor(max_rest[:, :, :], newmax[:, :, :], max_parts[:, :, :, 0],
                                                ALU.subtract))
                    else:
                        c.link(v.tensor_copy(max_parts[:, :, :, 1], max_rest[:, :, :]))
                        c.link(v.tensor_tensor(max_parts[:, :, :, 2], max_rest[:, :, :], max_parts[:, :, :, 1],
                                               ALU.subtract))
                        v.tensor_tensor(fall[:, :, :], fall[:, :, :], newmax[:, :, :], ALU.subtract
                                        ).then_inc(max_made, 1)

                def subtract_max(m, c):
                    u, s = number(m), m[1]
                    v.wait_ge(max_spread, u + 1)
                    hold(v, weight_made, u)
                    c.link(add_parts(v, max_b))
                    v.tensor_tensor(arg[:, :, :], score[s % 2][:, :, :], spread[:, :, :], ALU.subtract
                                    ).then_inc(arg_made, 1)

                def weigh_rows(m, c):
                    u, s = number(m), m[1]
                    v.wait_ge(weight_made, u + 1)
                    c.link(v.tensor_scalar(zrows(s)[:, :, :, DH], weight[:, :, :], 1.0, None, ALU.min))
                    zr = zrows(s)[:, :, :, 0:DH]
                    v.tensor_tensor(zr, zr, zrows(s)[:, :, :, DH:HZ].to_broadcast([P, ST, HEADS, DH]), ALU.mult
                                    ).then_inc(rows_weighted, 1)

                def scale_sums(o, k, c, bins):
                    u, s = number(o), o[1] % 2
                    az = g.acc[:, bass.ds(bins[k], 1), D:D + ZW].rearrange("p b (h z) -> p (b h) z", h=HEADS)
                    if k == 0:
                        v.wait_ge(rate_made, u + 1)
                    hold(v, sums_taken, GPS * u + k)
                    c.later(v.tensor_tensor(az, az, rate[s][:, k, :].unsqueeze(2).to_broadcast([P, HEADS, HZ]),
                                            ALU.mult))

                def add_sums(o, k, c, bins):
                    u = number(o)
                    v.wait_ge(sums_made, GPS * u + k + 1)
                    c.catch_up()
                    part = g.acc[:, bass.ds(bins[k], 1), ACC0:D + ZW].rearrange("p b c -> p (b c)")
                    v.tensor_tensor(part, part, sum_b[k % 2], ALU.add).then_inc(sums_taken, 1)

                def step(n, m, o):
                    if o is None:
                        start = LA if m else 0
                    else:
                        start = 2 * LA + LB + number(o) * (LA + LB + LC)
                        if m is None:
                            start -= LA
                    c = Chain(v, chain, start)
                    if o:
                        bins_o = [v.snap(r, min_val=0, max_val=NBINS - 1) for r in kept_bins]
                    bins_m = []

                    def scan_and_load(k):
                        scan_group(m, k)
                        bins_m.append(load_bin(v, g, number(m), k))
                        v.reg_mov(kept_bins[k], bins_m[k])
                    if m:
                        scan_and_load(0)
                    if o:
                        scale_sums(o, 0, c, bins_o)
                    if m:
                        scan_and_load(1)
                    if o:
                        add_sums(o, 0, c, bins_o)
                    if n and conv is not None:
                        convolve_half(n, 0, c)
                    if m:
                        read_max(m, 0, c, bins_m)
                    if o:
                        scale_sums(o, 1, c, bins_o)
                    if m:
                        scan_and_load(2)
                    if o:
                        add_sums(o, 1, c, bins_o)
                    c.catch_up()
                    if m:
                        write_max(0, c, bins_m)
                    if o:
                        scale_sums(o, 2, c, bins_o)
                    if m:
                        scan_and_load(3)
                    if o:
                        add_sums(o, 2, c, bins_o)
                    c.catch_up()
                    if m:
                        read_max(m, 1, c, bins_m)
                    if n and conv is not None:
                        convolve_half(n, 1, c)
                    if o:
                        scale_sums(o, 3, c, bins_o)
                    c.catch_up()
                    scores_and_maxima(n, m, c, bins_m)
                    if o:
                        add_sums(o, 3, c, bins_o)
                    if m:
                        split_max(m, 2, c)
                    if n:
                        onehot_ahead(after(n))
                    if m:
                        subtract_max(m, c)
                        weigh_rows(m, c)
                    assert c.n == (LA if n else 0) + (LB if m else 0) + (LC if o else 0)
                kept_bins = [v.alloc_register(f"{name}_bin{k}") for k in range(GPS)]
                onehot_ahead((0, 0))
                superblocks(v, step)


def plain_sums(g):
    return g.acc[:, :, :].rearrange("p b c -> p (b c)")[:, 0:NBINS * D].rearrange("p (b c) -> p b c", c=D)


def gated_edges(g):
    a, nc = g.a, g.nc
    W = 2 * D + 1
    with Pass(g, "edges1") as p:
        ring = p.buffer("ring", (P, RING * ST), U32)
        sums = plain_sums(g)
        spare = g.acc[:, :, :].rearrange("p b c -> p (b c)")[:, NBINS * D:]
        rows = [spare[:, s * ST * W:(s + 1) * ST * W].rearrange("p (t c) -> p t c", c=W) for s in range(RING - 1)]
        rows.append(p.buffer("rows3", (P, ST, W))[:, :, :])
        onehot = [p.buffer(f"onehot{s}", (P, ST, P)) for s in range(RING)]
        flippedT = p.buffer("onehotT", (P, ST, P))
        we2, be2 = p.buffer("we2", (P, D)), p.buffer("be2", (P, 1))
        dot, gate = p.buffer("dot", (P, ST)), p.buffer("gate", (P, ST))
        wt, bt = p.buffer("wt", (P, 64)), p.buffer("bt", (P, 64))
        feat = [p.buffer(f"feat{s}", (P, ST, P)) for s in range(2)]
        featT = p.buffer("featT", (P, 2, ST * P))
        rel, turns, half_pi = p.buffer("rel", (P, ST)), p.buffer("turns", (P, ST, 64)), p.buffer("half_pi", (P, 1))
        angle = p.buffer("angle", (P, ST, 64))
        gathered, seen = g.gathered, p.gathers_before()
        message_in = [p.semaphore(f"message_in{s}") for s in range(2)]
        feat_out = [p.semaphore(f"feat_out{s}") for s in range(2)]
        (ring_kept, onehot_made, onehot_flipped, flipped_kept, dst_spread, dot_made, gate_made, rows_weighted,
         sums_made, sums_taken, chain, loaded, angle_made, cos_made, feat_flipped, featT_kept) = (
             p.semaphore(n) for n in (
                 "ring_kept", "onehot_made", "onehot_flipped", "flipped_kept", "dst_spread", "dot_made", "gate_made",
                 "rows_weighted", "sums_made", "sums_taken", "chain", "weights_in", "angle_made", "cos_made",
                 "feat_flipped", "featT_kept"))
        flip_b, dst_b, feat_b, sum_b = g.bank[0], g.bank[1], g.bank[2], [g.bank[3][:, 0:D], g.bank[3][:, 512:512 + D]]
        rec = g.rec.rearrange("(g p s) r -> p g s r", p=P, s=GT)
        with nc.Block() as block:
            @block.gpsimd
            def _(pool):
                gather_rows(pool, g, g.table1, g.src_idx, ring, rows, ring_kept,
                            sums_made, gathered)

            @block.sync
            def _(sp):
                load_row(sp, we2, a["L1_gnn_We2"].rearrange("k o -> (o k)"), loaded)
                load_row(sp, be2, a["L1_gnn_be2"], loaded)
                load_row(sp, wt, a["L3_gnn_Wt"].rearrange("o k -> (o k)"), loaded)
                load_row(sp, bt, a["L3_gnn_bt"], loaded)

                def load(q, s):
                    u = q * 2 + s
                    hold(sp, feat_flipped, u - 1)
                    park(sp)
                    for j in range(GT):
                        sp.dma_start(feat[s][:, j::GT, 64:128], rec[:, bass.ds(u * GPS, GPS), j, 0:64]
                                     ).then_inc(message_in[s], 16)

                def store(q, s):
                    u = q * 2 + s
                    sp.wait_ge(featT_kept, u + 1)
                    park(sp)
                    sp.dma_start(g.edge_feat[:, bass.ds(u * (ST * P), ST * P)], featT[:, s, :]
                                 ).then_inc(feat_out[s], 16)
                load(0, 0)
                load(0, 1)
                store(0, 0)
                with sp.Fori(0, NSUPER // 2 - 1) as q:
                    load(q + 1, 0)
                    store(q, 1)
                    load(q + 1, 1)
                    store(q + 1, 0)
                store(NSUPER // 2 - 1, 1)
                for s in range(2):
                    sp.wait_ge(feat_out[s], 16 * NSUPER // 2)

            @block.tensor
            def _(pe):
                def step(n, o):
                    if n:
                        u, s = number(n), n[1] % 2
                        bins = [load_bin(pe, g, u, 0)]
                        pe.wait_ge(onehot_made, u + 1)
                        hold(pe, flipped_kept, u)
                        for j in range(ST):
                            ins = pe.transpose(flip_b[:, j * P:(j + 1) * P], onehot[n[1]][:, j, :], g.ident[:, :])
                        ins.then_inc(onehot_flipped, 1)
                        bins.append(load_bin(pe, g, u, 1))
                    if o:
                        sum_group(o, 0)
                    if n:
                        bins.append(load_bin(pe, g, u, 2))
                    if o:
                        sum_group(o, 1)
                    if n:
                        bins.append(load_bin(pe, g, u, 3))
                    if n:
                        pe.wait_ge(flipped_kept, u + 1)
                        hold(pe, dot_made, u)
                        for j in range(ST):
                            ins = pe.matmul(dst_b[:, j * P:(j + 1) * P], flippedT[:, j, :],
                                            g.dst[:, bass.ds(bins[j // GT], 1), :].rearrange("p b c -> p (b c)"),
                                            start=True, stop=True)
                        ins.then_inc(dst_spread, 1)
                    if o:
                        sum_group(o, 2)
                    if n:
                        pe.wait_ge(cos_made, u + 1)
                        pe.wait_ge(message_in[s], 16 * GT * (n[0] * (RING // 2) + n[1] // 2 + 1))
                        hold(pe, featT_kept, u)
                        for j in range(ST):
                            ins = pe.transpose(feat_b[:, j * P:(j + 1) * P], feat[s][:, j, :], g.ident[:, :])
                        ins.then_inc(feat_flipped, 1)
                    if o:
                        sum_group(o, 3)

                def sum_group(o, k):
                    u, s = number(o), o[1]
                    if k == 0:
                        pe.wait_ge(rows_weighted, u + 1)
                    hold(pe, sums_taken, GPS * u + k - 1)
                    for j in range(k * GT, (k + 1) * GT):
                        ins = pe.matmul(sum_b[k % 2], onehot[s][:, j, :], rows[s][:, j, 0:D],
                                        start=j == k * GT, stop=j == (k + 1) * GT - 1)
                    ins.then_inc(sums_made, 1)
                superblock_pairs(pe, step)

            @block.scalar
            def _(act):
                act.wait_ge(loaded, 64)
                act.wait_ge(chain, 1)

                def step(n, o):
                    if not n:
                        return
                    u, s = number(n), n[1] % 2
                    act.wait_ge(onehot_flipped, u + 1)
                    hold(act, dst_spread, u)
                    act.activation(flippedT[:, :, :].rearrange("p t c -> p (t c)"), flip_b[:, :], ACT.Copy
                                   ).then_inc(flipped_kept, 1)
                    act.wait_ge(angle_made, u + 1)
                    hold(act, feat_flipped, u - 1)
                    act.activation(feat[s][:, :, 0:64], angle[:, :, :], ACT.Sin, bias=half_pi[:, 0:1], scale=-1.0
                                   ).then_inc(cos_made, 1)
                    act.wait_ge(feat_flipped, u + 1)
                    hold(act, feat_out[s], 16 * (n[0] * (RING // 2) + n[1] // 2))
                    act.activation(featT[:, s, :], feat_b[:, :], ACT.Copy).then_inc(featT_kept, 1)
                    act.wait_ge(dot_made, u + 1)
                    hold(act, rows_weighted, u)
                    act.activation(gate[:, :], dot[:, :], ACT.Sigmoid, bias=be2[:, 0:1]).then_inc(gate_made, 1)
                superblock_pairs(act, step)

            @block.vector
            def _(v):
                v.memset(half_pi[:, :], TWO_PI / 4).then_inc(chain, 1)
                v.wait_ge(loaded, 64)
                C1, C2 = 6.28125, TWO_PI - 6.28125
                L = 9
                wide = [P, ST, 64]

                def ahead(n):
                    hold(v, sums_made, GPS * (number(n) - RING + 1))
                    make_onehot(v, g, number(n), onehot[n[1]], onehot_made)

                def take(o, k, bins):
                    u = number(o)
                    v.wait_ge(sums_made, GPS * u + k + 1)
                    acc = sums[:, bass.ds(bins[k], 1), :].rearrange("p b c -> p (b c)")
                    v.tensor_tensor(acc, acc, sum_b[k % 2], ALU.add).then_inc(sums_taken, 1)
                    v.wait_ge(sums_taken, GPS * u + k + 1)

                def step(n, o):
                    if o:
                        u, s = number(o), o[1]
                        v.wait_ge(gate_made, u + 1)
                        rh = rows[s][:, :, 0:D]
                        v.tensor_tensor(rh, rh, gate[:, :].unsqueeze(2).to_broadcast([P, ST, D]), ALU.mult
                                        ).then_inc(rows_weighted, 1)
                        bins = load_bins(v, g, u)
                    if n:
                        u, s = number(n), n[1]
                        c = Chain(v, chain, u * L + 1)
                        v.wait_ge(gathered[s], seen[s] + 16 * ST * (n[0] + 1))
                        hold(v, cos_made, u)
                        c.link(v.tensor_tensor(rel[:, :], rows[s][:, :, 2 * D], g.rel_t[:, tiles_of(u)],
                                               ALU.subtract))
                        c.link(v.tensor_tensor(angle[:, :, :], rel[:, :].unsqueeze(2).to_broadcast(wide),
                                               wt[:, :].unsqueeze(1).to_broadcast(wide), ALU.mult))
                        c.link(v.tensor_tensor(angle[:, :, :], angle[:, :, :],
                                               bt[:, :].unsqueeze(1).to_broadcast(wide), ALU.add))
                    if o:
                        take(o, 0, bins)
                    if n:
                        c.link(v.tensor_scalar(turns[:, :, :], angle[:, :, :], 1.0 / TWO_PI, 12582912.0, ALU.mult,
                                               ALU.add))
                        c.link(v.tensor_scalar(turns[:, :, :], turns[:, :, :], 12582912.0, None, ALU.subtract))
                        c.link(v.scalar_tensor_tensor(angle[:, :, :], turns[:, :, :], -C1, angle[:, :, :], ALU.mult,
                                                      ALU.add))
                    if o:
                        take(o, 1, bins)
                    if n:
                        c.link(v.scalar_tensor_tensor(angle[:, :, :], turns[:, :, :], -C2, angle[:, :, :], ALU.mult,
                                                      ALU.add))
                        v.scalar_tensor_tensor(angle[:, :, :], angle[:, :, :], -1.0, angle[:, :, :], ALU.mult,
                                               ALU.max).then_inc(angle_made, 1)
                        v.wait_ge(dst_spread, u + 1)
                        ra = rows[s][:, :, D:2 * D]
                        c.link(v.tensor_tensor(ra, ra, dst_b[:, :].rearrange("p (t c) -> p t c", c=D), ALU.add))
                    if o:
                        take(o, 2, bins)
                    if n:
                        c.link(v.scalar_tensor_tensor(ra, ra, 0.0, we2[:, :].unsqueeze(1).to_broadcast([P, ST, D]),
                                                      ALU.max, ALU.mult))
                        hold(v, gate_made, u)
                        v.tensor_reduce(dot[:, :], ra, AX, ALU.add).then_inc(dot_made, 1)
                    if o:
                        take(o, 3, bins)
                    if n:
                        ahead(after(n))
                        c.end(L)
                ahead((0, 0))
                superblock_pairs(v, step)


class Shared:
    pass


def program(nc, a, out):
    ctx = ExitStack()
    with ctx:
        def sb(name, shape, dt=F32):
            return ctx.enter_context(nc.sbuf_tensor(name, shape, dt))

        def dram(name, shape, dt=F32):
            return nc.dram_tensor(name, shape, dt, kind="Internal").ap()

        counter = [0]

        def sem(name):
            counter[0] += 1
            return ctx.enter_context(nc.semaphore(f"{name}_{counter[0]}"))

        bank = [ctx.enter_context(nc.psum_tensor(f"bank{i}", [P, 1024], F32)) for i in range(4)]

        rec = dram("rec", [SLOTS, REC])
        bins_d = dram("bins_d", [NGROUPS])
        table0 = dram("table0", [NBINS * P * RELS, D + ZW])
        table1 = dram("table1", [NBINS * P, 2 * D + 1])
        table2 = dram("table2", [NBINS * P, ZW])
        table3 = dram("table3", [NBINS * P, D + ZW])
        edge_feat = dram("edge_feat", [P, NTILES * P])

        ident = sb("ident", [P, P])
        identb = sb("identb", [P, P], BF16)
        ones = sb("ones", [P, P])
        before = sb("before", [P, P])
        place1 = sb("place1", [P, P])
        place0 = sb("place0", [P, P])
        row = sb("row", [P, 1])
        sel = sb("sel", [P, HEADS, P], BF16)
        headmask = sb("headmask", [P, HEADS])
        x = sb("x", [P, NBINS, D])
        h = sb("h", [P, NBINS, D])
        acc = sb("acc", [P, NBINS, D + ZW])
        top = sb("top", [P, NBINS, HEADS])
        dst = sb("dst", [P, NBINS, D])
        src_idx = sb("src_idx", [P, NTILES], U32)
        rel_idx = sb("rel_idx", [P, NTILES], U32)
        places = sb("places", [P, NTILES + ST])
        rel_t = sb("rel_t", [P, NTILES])
        edge_score = sb("edge_score", [P, NTILES, HEADS])
        bin_row = sb("bin_row", [1, NGROUPS], I32)
        tw_mean = sb("tw_mean", [P, 1])

        with ExitStack() as ph:
            made, chain, counted = sem("iota_made"), sem("const_chain"), sem("x_loaded")
            c_i = ph.enter_context(nc.sbuf_tensor("c_i", [P, P], I32))
            r_i = ph.enter_context(nc.sbuf_tensor("r_i", [P, 1], I32))
            padded = sem("x_padded")
            k_i = ph.enter_context(nc.sbuf_tensor("k_i", [P, HEADS], I32))
            k_f = ph.enter_context(nc.sbuf_tensor("k_f", [P, HEADS], F32))
            with nc.Block() as block:
                @block.gpsimd
                def _(pool):
                    pool.iota(c_i[:, :], [[1, P]], base=0, channel_multiplier=0).then_inc(made, 1)
                    pool.iota(r_i[:, :], [[0, 1]], base=0, channel_multiplier=1).then_inc(made, 1)
                    pool.iota(k_i[:, :], [[-1, HEADS]], base=128, channel_multiplier=1).then_inc(made, 1)

                @block.sync
                def _(sp):
                    full = (NBINS - 1) * P
                    sp.dma_start(x[:, 0:NBINS - 1, :], a["x"][0:full, :].rearrange("(b p) c -> p b c", p=P)
                                 ).then_inc(counted, 16)
                    sp.wait_ge(padded, 1)
                    sp.dma_start(x[0:LAST, NBINS - 1, :], a["x"][full:NODES, :]).then_inc(counted, 16)
                    sp.wait_ge(counted, 32)

                @block.vector
                def _(v):
                    v.memset(x[:, NBINS - 1, :], 0.0).then_inc(padded, 1)
                    v.wait_ge(made, 3)
                    c = Chain(v, chain)
                    v.memset(ones[:, :], 1.0)
                    v.memset(places[:, NTILES:NTILES + ST], 0.0)
                    v.tensor_copy(row[:, :], r_i[:, :])
                    c.link(v.tensor_copy(place0[:, :], c_i[:, :]))
                    v.tensor_scalar(place1[:, :], place0[:, :], 1.0, None, ALU.add)
                    c.link(v.tensor_copy(k_f[:, :], k_i[:, :]))
                    v.tensor_scalar(ident[:, :], place0[:, :], row[:, 0:1], None, ALU.is_equal)
                    v.tensor_scalar(identb[:, :], place0[:, :], row[:, 0:1], None, ALU.is_equal)
                    v.tensor_scalar(before[:, :], place0[:, :], row[:, 0:1], None, ALU.is_gt)
                    c.link(v.memset(headmask[:, :], 0.0))
                    for j in range(HEADS):
                        v.memset(headmask[DH * j:DH * (j + 1), j:j + 1], 1.0)
                    parts = [ph.enter_context(nc.sbuf_tensor(f"part{n}", [P, HEADS], F32)) for n in range(3)]
                    for n in range(3):
                        ins = v.tensor_scalar(parts[n][:, :], k_f[:, :], 128.0 + HEADS * n, None, ALU.is_equal)
                    c.link(ins)
                    c.link(v.tensor_tensor(parts[0][:, :], parts[0][:, :], parts[1][:, :], ALU.add))
                    c.link(v.tensor_tensor(parts[0][:, :], parts[0][:, :], parts[2][:, :], ALU.add))
                    for j in range(HEADS):
                        ins = v.tensor_scalar(sel[:, j, :], ones[:, :], parts[0][:, j:j + 1], None, ALU.mult)
                    c.link(ins)

        with ExitStack() as ph:
            def tb(name, shape, dt=F32):
                return ph.enter_context(nc.sbuf_tensor(name, shape, dt))

            dst_i, bin_i = tb("dst_i", [EP, EC], I32), tb("bin_i", [EP, EC], I32)
            src_i, type_i = tb("src_i", [EP, EC], I32), tb("type_i", [EP, EC], I32)
            weight = tb("weight", [EP, EC])
            ebin, meta = tb("ebin", [EP, EC]), tb("meta", [EP, EC, 4])
            slot_u = tb("slot_u", [EP, EC], U32)
            hit = acc[:, :, :].rearrange("p b c -> p (b c)")[0:EP, 0:EC]
            run = acc[:, :, :].rearrange("p b c -> p (b c)")[0:EP, EC:2 * EC]
            slot = acc[:, :, :].rearrange("p b c -> p (b c)")[0:EP, 2 * EC:3 * EC]
            gain = acc[:, :, :].rearrange("p b c -> p (b c)")[0:EP, 3 * EC:4 * EC]
            zeros = h[:, :, :].rearrange("p b c -> p (b c)")
            counts, offs = tb("counts", [EP, NBINS]), tb("offs", [P, NBINS])
            total, ngr = tb("total", [P, NBINS]), tb("ngr", [P, NBINS])
            ngr_i, last = tb("ngr_i", [P, NBINS], I32), tb("last", [P, NBINS])
            wsum = tb("wsum", [P, 1])
            gnum = tb("gnum", [110, GPS])
            gcmp = tb("gcmp", [110, GPS, NBINS])
            gbin, gbin_i = tb("gbin", [110, GPS]), tb("gbin_i", [110, GPS], I32)
            gnum_i = tb("gnum_i", [110, GPS], I32)
            lists_in, zeroed, zeros_made = sem("lists_in"), sem("records_zeroed"), sem("zeros_made")
            chain, counted, summed = sem("sort_chain"), sem("counts_made"), sem("counts_summed")
            bins_out, bins_in, bins_ready, gnum_made = (sem("bins_out"), sem("bins_in"), sem("bins_ready"),
                                                       sem("group_numbers"))
            ZR = SLOTS * REC // P
            ZC = NBINS * D
            with nc.Block() as block:
                @block.sync
                def _(sp):
                    for k, (t, name) in enumerate([(dst_i, "dst"), (src_i, "src"), (type_i, "edge_type_16"),
                                                   (weight, "edge_weight")]):
                        sp.dma_start(t[:, :], a[name].rearrange("(p t) -> p t", p=EP)).then_inc(lists_in, 16)
                    sp.wait_ge(zeros_made, 1)
                    n = 0
                    flat = rec.rearrange("(p s) r -> p (s r)", p=P)
                    for at in range(0, ZR, ZC):
                        m = min(ZC, ZR - at)
                        sp.dma_start(flat[:, at:at + m], zeros[:, 0:m]).then_inc(zeroed, 16)
                        n += 1
                    sp.wait_ge(bins_ready, 1)
                    sp.dma_start(bins_d.bitcast(I32).rearrange("(p g) -> p g", p=110), gbin_i[:, :]
                                 ).then_inc(bins_out, 16)
                    sp.wait_ge(bins_out, 16)
                    sp.dma_start(bin_row[:, :], bins_d.bitcast(I32).unsqueeze(0)).then_inc(bins_in, 16)
                    sp.wait_ge(bins_in, 16)
                    sp.wait_ge(zeroed, 16 * n)

                @block.gpsimd
                def _(pool):
                    pool.iota(gnum_i[:, :], [[1, GPS]], base=0, channel_multiplier=GPS).then_inc(gnum_made, 1)

                @block.vector
                def _(v):
                    v.memset(zeros[:, :], 0.0).then_inc(zeros_made, 1)
                    v.wait_ge(lists_in, 64)
                    c = Chain(v, chain)
                    c.link(v.tensor_scalar(bin_i[:, :], dst_i[:, :], 7, None, ALU.arith_shift_right))
                    v.tensor_copy(ebin[:, :], bin_i[:, :])
                    v.tensor_copy(meta[:, :, 0], src_i[:, :])
                    v.tensor_copy(meta[:, :, 2], type_i[:, :])
                    v.tensor_copy(meta[:, :, 3], weight[:, :])
                    v.memset(slot, -1.0)
                    v.memset(wsum[:, :], 0.0)
                    c.link(v.tensor_scalar(hit, dst_i[:, :], 1.0, None, ALU.add))
                    c.link(v.scalar_tensor_tensor(meta[:, :, 1], ebin[:, :], -float(P), hit, ALU.mult, ALU.add))
                    c.link(v.tensor_reduce(wsum[0:EP, :], weight[:, :], AX, ALU.add))
                    first = c.n
                    with v.Fori(0, NBINS) as b:
                        d = Chain(v, chain, b * 2 + first)
                        d.link(v.tensor_scalar(hit, ebin[:, :], place0[0:EP, bass.ds(b, 1)], None, ALU.is_equal))
                        d.link(v.tensor_reduce(total[0:EP, 0:1], hit, AX, ALU.add))
                        v.tensor_scalar(counts[:, bass.ds(b, 1)], total[0:EP, 0:1], 1.0, None, ALU.mult
                                        ).then_inc(counted, 1)
                    v.wait_ge(summed, 1)
                    c = Chain(v, chain, first + 2 * NBINS)
                    v.tensor_scalar(tw_mean[:, :], bank[0][:, 512:513], 1.0 / EDGES, None, ALU.mult)
                    v.tensor_copy(offs[:, :], bank[0][:, 64:64 + NBINS])
                    c.link(v.tensor_scalar(ngr_i[:, :], bank[0][:, 0:NBINS], float(GE - 1), None, ALU.add))
                    c.link(v.tensor_scalar(ngr_i[:, :], ngr_i[:, :], 8, None, ALU.arith_shift_right))
                    c.link(v.tensor_copy(ngr[:, :], ngr_i[:, :]))
                    c.link(v.tensor_tensor_scan(last[:, :], ones[:, 0:NBINS], ngr[:, :], 0.0, ALU.mult, ALU.add))
                    c.link(v.tensor_tensor(ngr[:, :], last[:, :], ngr[:, :], ALU.subtract))
                    c.link(v.scalar_tensor_tensor(offs[:, :], ngr[:, :], float(GE), offs[:, :], ALU.mult, ALU.add))
                    v.wait_ge(gnum_made, 1)
                    c.link(v.tensor_copy(gnum[:, :], gnum_i[:, :]))
                    c.link(v.tensor_tensor(gcmp[:, :, :], last[0:110, :].unsqueeze(1).to_broadcast([110, GPS, NBINS]),
                                           gnum[:, :].unsqueeze(2).to_broadcast([110, GPS, NBINS]), ALU.is_le))
                    c.link(v.tensor_reduce(gbin[:, :], gcmp[:, :, :], AX, ALU.add))
                    v.tensor_scalar(gbin_i[:, :], gbin[:, :], float(NBINS - 1), None, ALU.min
                                    ).then_inc(bins_ready, 1)
                    second = first + 2 * NBINS + c.n
                    with v.Fori(0, NBINS) as b:
                        d = Chain(v, chain, b * 4 + second)
                        d.link(v.tensor_scalar(hit, ebin[:, :], place0[0:EP, bass.ds(b, 1)], None, ALU.is_equal))
                        d.link(v.tensor_tensor_scan(run, ones[0:EP, 0:1].to_broadcast([EP, EC]), hit, 0.0,
                                                    ALU.mult, ALU.add))
                        d.link(v.scalar_tensor_tensor(gain, run, offs[0:EP, bass.ds(b, 1)], hit, ALU.add, ALU.mult))
                        d.link(v.tensor_tensor(slot, slot, gain, ALU.add))
                    c = Chain(v, chain, second + 4 * NBINS)
                    c.link(v.tensor_copy(slot_u[:, :], slot))

                @block.tensor
                def _(pe):
                    pe.wait_ge(counted, NBINS)
                    pe.matmul(bank[0][:, 0:NBINS], ones[0:EP, :], counts[:, :], start=True, stop=True)
                    pe.matmul(bank[0][:, 64:64 + NBINS], before[0:EP, :], counts[:, :], start=True, stop=True)
                    pe.matmul(bank[0][:, 512:513], ones[:, :], wsum[:, :], start=True, stop=True).then_inc(summed, 1)

            CH = 16
            NCH = EC // CH
            spare = dst[:, :, :].rearrange("p b c -> p (b c)")
            at16, atr = 2 * CH * 64, 2 * CH * 80
            a64 = spare[0:EP, 0:at16].rearrange("p (s c) -> p s c", s=2)
            a16 = spare[0:EP, at16:atr].rearrange("p (s c) -> p s c", s=2)
            recs = spare[0:EP, atr:atr + 2 * CH * REC].rearrange("p (s c) -> p s c", s=2)
            slots = tb("slots", [EP, 2 * CH], U32)
            attrs_packed, meta_packed = sem("attrs_packed"), sem("meta_packed")
            attrs_in = [sem(f"attrs_in{s}") for s in range(2)]
            scattered = [sem(f"scattered{s}") for s in range(2)]
            v64 = a["edge_attr_64"].rearrange("(p t) c -> p (t c)", p=EP)
            v16 = a["edge_attr_16"].rearrange("(p t) c -> p (t c)", p=EP)
            with nc.Block() as block:
                @block.sync
                def _(sp):
                    def load(q, s):
                        k = q * 2 + s
                        hold(sp, attrs_packed, (k - 1) * 2)
                        sp.dma_start(a64[:, s, :], v64[:, bass.ds(k * CH * 64, CH * 64)]).then_inc(attrs_in[s], 16)
                        sp.dma_start(a16[:, s, :], v16[:, bass.ds(k * CH * 16, CH * 16)]).then_inc(attrs_in[s], 16)
                    load(0, 0)
                    load(0, 1)
                    with sp.Fori(1, NCH // 2) as q:
                        load(q, 0)
                        load(q, 1)

                @block.scalar
                def _(act):
                    def pack(q, s):
                        r = recs[:, s, :].rearrange("p (t r) -> p t r", r=REC)
                        act.wait_ge(attrs_in[s], q * 32 + 32)
                        hold(act, scattered[s], q * 16 * CH)
                        act.activation(r[:, :, 0:64], a64[:, s, :].rearrange("p (t c) -> p t c", c=64), ACT.Copy
                                       ).then_inc(attrs_packed, 1)
                        act.activation(r[:, :, 64:80], a16[:, s, :].rearrange("p (t c) -> p t c", c=16), ACT.Copy
                                       ).then_inc(attrs_packed, 1)
                    pack(0, 0)
                    pack(0, 1)
                    with act.Fori(1, NCH // 2) as q:
                        pack(q, 0)
                        pack(q, 1)

                @block.vector
                def _(v):
                    def pack(q, s):
                        k = q * 2 + s
                        r = recs[:, s, :].rearrange("p (t r) -> p t r", r=REC)
                        hold(v, scattered[s], q * 16 * CH)
                        v.tensor_scalar(r[:, :, 80:84], meta[:, bass.ds(k * CH, CH), :], 1.0, None, ALU.mult
                                        ).then_inc(meta_packed, 1)
                        v.tensor_tensor(slots[:, s * CH:(s + 1) * CH], slot_u[:, bass.ds(k * CH, CH)],
                                        slot_u[:, bass.ds(k * CH, CH)], ALU.max).then_inc(meta_packed, 1)
                    pack(0, 0)
                    pack(0, 1)
                    with v.Fori(1, NCH // 2) as q:
                        pack(q, 0)
                        pack(q, 1)

                @block.gpsimd
                def _(pool):
                    def scatter(q, s):
                        k = q * 2 + s
                        pool.wait_ge(attrs_packed, k * 2 + 2)
                        pool.wait_ge(meta_packed, k * 2 + 2)
                        park(pool)
                        for j in range(CH):
                            pool.indirect_dma_start(
                                out=rec, out_offset=bass.IndirectOffsetOnAxis(
                                    ap=slots[:, s * CH + j:s * CH + j + 1], axis=0),
                                in_=recs[:, s, j * REC:(j + 1) * REC], in_offset=None).then_inc(scattered[s], 16)
                    with pool.Fori(0, NCH // 2) as q:
                        scatter(q, 0)
                        scatter(q, 1)
                    for s in range(2):
                        pool.wait_ge(scattered[s], 16 * EC // 2)

        with ExitStack() as ph:
            def tb(name, shape, dt=F32):
                return ph.enter_context(nc.sbuf_tensor(name, shape, dt))
            CG = 10
            CT = CG * GT
            NCK = NGROUPS // CG
            buf = tb("buf", [P, 2, CT * REC])
            w_edge, att_e = tb("w_edge", [P, 16]), tb("att_e", [P, 1])
            wmask, wfold = tb("wmask", [P, HEADS, 16]), tb("wfold", [P, HEADS, 16])
            prod = tb("prod", [P, CT, HEADS, 16])
            records_in = [sem(f"records_in{s}") for s in range(2)]
            weights_in, taken, chain, folded, fold_made = (
                sem("weights_in"), sem("records_taken"), sem("fold_chain"), sem("folded"),
                sem("fold_made"))
            rv = rec.rearrange("(g p s) r -> p g (s r)", p=P, s=GT)
            with nc.Block() as block:
                @block.sync
                def _(sp):
                    sp.dma_start(w_edge[:, :], a["L2_gnn_W_edge"]).then_inc(weights_in, 16)
                    sp.dma_start(att_e[:, :], a["L2_gnn_att_edge"].rearrange("a h c -> (h c) a")).then_inc(weights_in, 16)

                    def load(q, s):
                        k = q * 2 + s
                        hold(sp, taken, k - 1)
                        sp.dma_start(buf[:, s, :].rearrange("p (g r) -> p g r", g=CG),
                                     rv[:, bass.ds(k * CG, CG), :]).then_inc(records_in[s], 16)
                    load(0, 0)
                    load(0, 1)
                    with sp.Fori(1, NCK // 2) as q:
                        load(q, 0)
                        load(q, 1)

                @block.tensor
                def _(pe):
                    pe.wait_ge(fold_made, 1)
                    pe.matmul(bank[0][:, 0:HEADS * 16], ones[:, :], wmask[:, :, :].rearrange("p h k -> p (h k)"),
                              start=True, stop=True).then_inc(folded, 1)

                @block.vector
                def _(v):
                    v.wait_ge(weights_in, 32)
                    c = Chain(v, chain)
                    c.link(v.tensor_tensor(wmask[:, :, :], w_edge[:, :].unsqueeze(1).to_broadcast([P, HEADS, 16]),
                                           headmask[:, :].unsqueeze(2).to_broadcast([P, HEADS, 16]), ALU.mult))
                    v.tensor_scalar(wmask[:, :, :], wmask[:, :, :], att_e[:, 0:1], None, ALU.mult
                                    ).then_inc(fold_made, 1)
                    v.wait_ge(folded, 1)
                    c.link(v.tensor_copy(wfold[:, :, :], bank[0][:, 0:HEADS * 16].rearrange("p (h k) -> p h k", k=16)))

                    def take(q, s):
                        k = q * 2 + s
                        r = buf[:, s, :].rearrange("p (t r) -> p t r", r=REC)
                        at = bass.ds(k * CT, CT)
                        v.wait_ge(records_in[s], q * 16 + 16)
                        hold(v, taken, k)
                        d = Chain(v, chain, k + 2)
                        v.tensor_scalar(src_idx[:, at], r[:, :, SOURCE], 1.0, None, ALU.mult)
                        v.scalar_tensor_tensor(rel_idx[:, at], r[:, :, SOURCE], float(RELS), r[:, :, TYPE], ALU.mult, ALU.add)
                        v.tensor_scalar(places[:, at], r[:, :, PLACE], 1.0, None, ALU.mult)
                        v.tensor_scalar(rel_t[:, at], r[:, :, WEIGHT], 1.0, None, ALU.mult)
                        d.link(v.tensor_tensor(prod[:, :, :, :], r[:, :, 64:80].unsqueeze(2).to_broadcast([P, CT, HEADS, 16]),
                                               wfold[:, :, :].unsqueeze(1).to_broadcast([P, CT, HEADS, 16]), ALU.mult))
                        park(v)
                        v.tensor_reduce(edge_score[:, at, :], prod[:, :, :, :], AX, ALU.add).then_inc(taken, 1)
                    take(0, 0)
                    take(0, 1)
                    with v.Fori(1, NCK // 2) as q:
                        take(q, 0)
                        take(q, 1)

        g = Shared()
        g.nc, g.a, g.out, g.sem, g.bank, g.rec, g.edge_feat = nc, a, out, sem, bank, rec, edge_feat
        g.table0, g.table1, g.table2, g.table3 = table0, table1, table2, table3
        g.ident, g.identb, g.place1, g.sel = ident, identb, place1, sel
        g.x, g.h, g.acc, g.top, g.dst = x, h, acc, top, dst
        g.places, g.rel_t, g.edge_score, g.bin_row, g.tw_mean = places, rel_t, edge_score, bin_row, tw_mean
        g.src_idx, g.seen = src_idx, [0] * RING
        g.gathered = [sem(f"gathered{s}") for s in range(RING)]
        for layer in range(3):
            attention_sources(g, f"source0{layer}", h if layer else x, a["L0_gnn_W_gat"][layer], False,
                              a["L0_gnn_attn_l"][layer].rearrange("h c -> (h c)"),
                              a["L0_gnn_attn_r"][layer].rearrange("h c -> (h c)"), layer)
            attention_edges(g, f"edges0{layer}", table0, rel_idx)
            relational_close(g, layer)
        gated_sources(g)
        gated_edges(g)
        gated_close(g)
        attention_sources(g, "source2", x, a["L2_gnn_W_lin"], True,
                          a["L2_gnn_att_dst"].rearrange("a h c -> (a h c)"),
                          a["L2_gnn_att_src"].rearrange("a h c -> (a h c)"))
        attention_edges(g, "edges2", table2, src_idx, scored_edges=True)
        edge_attention_close(g)
        conv_sources(g, 1, x)
        attention_edges(g, "edges31", table3, src_idx, conv=1)
        conv_close(g, last=False)
        conv_sources(g, 2, h)
        attention_edges(g, "edges32", table3, src_idx, conv=2)
        conv_close(g, last=True)


INPUTS = ["x", "src", "dst", "edge_attr_16", "edge_attr_64", "edge_type_16", "edge_weight", "node_vec"]
INPUTS += ["L0_gnn_" + n for n in ("W_rel", "b_rel", "W_loop", "W_gat", "attn_l", "attn_r", "b_gat", "W_fuse",
                                   "b_fuse", "W_gate", "b_gate")]
INPUTS += ["L1_gnn_" + n for n in ("W1", "b1", "g1", "bt1", "We1", "be1", "We2", "be2", "Wg", "bg", "g2", "bt2")]
INPUTS += ["L2_gnn_" + n for n in ("W_lin", "W_edge", "att_src", "att_dst", "att_edge", "bias", "ln_gamma",
                                   "ln_beta")]
INPUTS += ["L3_gnn_Wt", "L3_gnn_bt"]
INPUTS += [f"L3_gnn_{n}{k}" for k in (1, 2) for n in ("Wq", "bq", "Wk", "bk", "Wv", "bv", "We", "Wskip", "bskip")]


def kernel(**inputs):
    import numpy as np
    import concourse.bacc as bacc
    from concourse.bass_utils import run_bass_kernel_spmd

    nc = bacc.Bacc("TRN2", target_bir_lowering=False, num_devices=1)
    arrays, aps = {}, {}
    for name in INPUTS:
        arr = np.ascontiguousarray(inputs[name])
        arrays["in_" + name] = arr
        aps[name] = nc.dram_tensor("in_" + name, arr.shape, mybir.dt.from_np(arr.dtype), kind="ExternalInput").ap()
    out = nc.dram_tensor("out", (NODES, D), F32, kind="ExternalOutput").ap()
    program(nc, aps, out)
    got = run_bass_kernel_spmd(nc, [arrays], core_ids=[0])
    return got.results[0]["out"]
```
